# Optimizing a Trainium2 kernel written in Bass

```python
import numpy as np
import jax
import jax.numpy as jnp

def _softmax(x, axis=-1):
    return jax.nn.softmax(x, axis=axis)

def _gelu(x):
    return jax.nn.gelu(x, approximate=True)

def _silu(x):
    return jax.nn.silu(x)

def _sigmoid(x):
    return jax.nn.sigmoid(x)

def _layernorm(x, axis=-1, eps=1e-05):
    m = jnp.mean(x, axis=axis, keepdims=True)
    v = jnp.var(x, axis=axis, keepdims=True)
    return (x - m) / jnp.sqrt(v + eps)

def _scatter_add(tgt, idx, src, axis=0):
    return tgt.at[idx].add(src)

def _segment_sum(src, seg, n):
    return jax.ops.segment_sum(src, seg, n)
kernel_name = 'mk_xattn_ffn_d2_seqx_r4_bf8dc0'

def setup_inputs(seed: int=0):
    np.random.seed(seed)
    _w = jnp.asarray

    def _rec_inputs():
        import jax
        import jax.numpy as jnp
        _rk = jax.random.key(seed)
        x = -0.0002928 + 1 * jax.random.normal(jax.random.fold_in(_rk, 1), (4, 1024, 256), jnp.float32)
        _lenS = 1024 - jax.random.randint(jax.random.fold_in(_rk, 7), (4,), 0, max(1, 1024 // 4) + 1, jnp.int32)
        _lenS2 = 64 - jax.random.randint(jax.random.fold_in(_rk, 8), (4,), 0, max(1, 64 // 4) + 1, jnp.int32)
        _ctx_1024P = jax.random.normal(jax.random.fold_in(_rk, 11), (4, 16, 256), jnp.float32)
        _ctx_1024c = jax.random.dirichlet(jax.random.fold_in(_rk, 511), 0.3 * jnp.ones((16,), jnp.float32), (4, 64))
        _ctx_1024t = jnp.einsum('bsk,bkd->bsd', _ctx_1024c, _ctx_1024P)
        _ctx_1024t = _ctx_1024t * jax.lax.rsqrt(jnp.mean(jnp.square(_ctx_1024t)) + 1e-12) * 0.953939
        ctx_1024 = -1.39393e-06 + 0.999914 * (_ctx_1024t + 0.3 * jax.random.normal(jax.random.fold_in(_rk, 611), (4, 64, 256), jnp.float32))
        return (x, ctx_1024)
    x, ctx_1024 = _rec_inputs()

    def _L0_xattn_setup():
        import jax, jax.numpy as jnp
        import numpy as np
        NOT_EPSILON = 1.0
        W_SCALE = 0.05
        H, T, A, C = (8, 256, 64, 64)

        def swishmax(x, axis):
            m = jnp.max(x, axis=axis, keepdims=True)
            xe = x * jnp.exp(x - m)
            return xe / (jnp.sum(jnp.abs(xe), axis=axis, keepdims=True) + NOT_EPSILON)
        key = jax.random.key(seed)
        ks = jax.random.split(key, 7)
        B, Q, K = (2, 512, 512)
        return {'query_tokens': jax.random.normal(ks[0], (B, Q, T), dtype=jnp.float32), 'key_tokens': jax.random.normal(ks[1], (B, K, T), dtype=jnp.float32), 'key_down': jax.random.normal(ks[2], (H, T, A), dtype=jnp.float32) * W_SCALE, 'query_down': jax.random.normal(ks[3], (H, T, A), dtype=jnp.float32) * W_SCALE, 'query_down_bias': jax.random.normal(ks[4], (H, 1, A), dtype=jnp.float32) * W_SCALE, 'value_down': jax.random.normal(ks[5], (H, T, C), dtype=jnp.float32) * W_SCALE, 'value_up': jax.random.normal(ks[6], (H, C, T), dtype=jnp.float32) * W_SCALE}
    _L0_xattn_all = _L0_xattn_setup()
    _L0_xattn_in = {k: v for k, v in _L0_xattn_all.items() if k in ('key_down', 'query_down', 'query_down_bias', 'value_down', 'value_up')}
    del _L0_xattn_all

    def _L0_ffn_setup():
        import jax, jax.numpy as jnp
        import numpy as np
        D_MODEL, D_FF, N_EXPERTS, TOP_K = (256, 1024, 8, 2)
        BATCH, SEQ = (2, 512)
        key = jax.random.key(seed)
        ks = jax.random.split(key, 10)
        s = 0.02
        return {'x': jax.random.normal(ks[0], (BATCH, SEQ, D_MODEL), jnp.float32), 'Wg': jax.random.normal(ks[1], (D_MODEL, N_EXPERTS), jnp.float32) * s, 'W1': jax.random.normal(ks[2], (N_EXPERTS, D_MODEL, D_FF), jnp.float32) * s, 'b1': jnp.zeros((N_EXPERTS, D_FF), jnp.float32), 'W2': jax.random.normal(ks[3], (N_EXPERTS, D_FF, D_MODEL), jnp.float32) * s, 'b2': jnp.zeros((N_EXPERTS, D_MODEL), jnp.float32), 'Ws1': jax.random.normal(ks[4], (D_MODEL, D_FF), jnp.float32) * s, 'bs1': jnp.zeros((D_FF,), jnp.float32), 'Ws2': jax.random.normal(ks[5], (D_FF, D_MODEL), jnp.float32) * s, 'bs2': jnp.zeros((D_MODEL,), jnp.float32)}
    _L0_ffn_all = _L0_ffn_setup()
    _L0_ffn_in = {k: v for k, v in _L0_ffn_all.items() if k in ('Wg', 'W1', 'b1', 'W2', 'b2', 'Ws1', 'bs1', 'Ws2', 'bs2')}
    del _L0_ffn_all

    def _L1_xattn_setup():
        import jax, jax.numpy as jnp
        import numpy as np
        H = 16
        key = jax.random.key(seed)
        ks = jax.random.split(key, 11)
        B, S, D = (4, 512, 256)
        s = 1.0 / np.sqrt(D)
        return {'query': jax.random.normal(ks[0], (B, S, D), jnp.float32), 'key': jax.random.normal(ks[1], (B, S, D), jnp.float32), 'value': jax.random.normal(ks[2], (B, S, D), jnp.float32), 'Wq': jax.random.normal(ks[3], (D, D), jnp.float32) * s, 'bq': jax.random.normal(ks[4], (D,), jnp.float32) * 0.01, 'Wk': jax.random.normal(ks[5], (D, D), jnp.float32) * s, 'bk': jax.random.normal(ks[6], (D,), jnp.float32) * 0.01, 'Wv': jax.random.normal(ks[7], (D, D), jnp.float32) * s, 'bv': jax.random.normal(ks[8], (D,), jnp.float32) * 0.01, 'Wo': jax.random.normal(ks[9], (D, D), jnp.float32) * s, 'bo': jax.random.normal(ks[10], (D,), jnp.float32) * 0.01}
    _L1_xattn_all = _L1_xattn_setup()
    _L1_xattn_in = {k: v for k, v in _L1_xattn_all.items() if k in ('Wq', 'bq', 'Wk', 'bk', 'Wv', 'bv', 'Wo', 'bo')}
    del _L1_xattn_all

    def _L1_ffn_setup():
        import jax, jax.numpy as jnp
        import numpy as np
        QMAX = 127.0

        def _ste_round(v):
            return v + jax.lax.stop_gradient(jnp.round(v) - v)

        def _act_fake_quant(x, clip_factor):
            scale = jax.nn.sigmoid(clip_factor) * jnp.max(jnp.abs(x)) / QMAX
            return jnp.clip(_ste_round(x / scale), -QMAX - 1.0, QMAX) * scale

        def _weight_fake_quant(w):
            scale = jnp.max(jnp.abs(w), axis=1, keepdims=True) / QMAX
            return jnp.clip(_ste_round(w / scale), -QMAX - 1.0, QMAX) * scale
        key = jax.random.key(seed)
        k1, k2, k3, k4 = jax.random.split(key, 4)
        B, S, H, I = (8, 2048, 256, 704)
        return {'x': jax.random.normal(k1, (B, S, H), dtype=jnp.float32), 'clip_x': jnp.full((1,), 4.0, dtype=jnp.float32), 'clip_down': jnp.full((1,), 4.0, dtype=jnp.float32), 'w_gate': jax.random.normal(k2, (I, H), dtype=jnp.float32) * 0.02, 'w_up': jax.random.normal(k3, (I, H), dtype=jnp.float32) * 0.02, 'w_down': jax.random.normal(k4, (H, I), dtype=jnp.float32) * 0.02}
    _L1_ffn_all = _L1_ffn_setup()
    _L1_ffn_in = {k: v for k, v in _L1_ffn_all.items() if k in ('clip_x', 'clip_down', 'w_gate', 'w_up', 'w_down')}
    del _L1_ffn_all
    return {'x': x, 'ctx_1024': ctx_1024, 'L0_xattn_key_down': _L0_xattn_in['key_down'], 'L0_xattn_query_down': _L0_xattn_in['query_down'], 'L0_xattn_query_down_bias': _L0_xattn_in['query_down_bias'], 'L0_xattn_value_down': _L0_xattn_in['value_down'], 'L0_xattn_value_up': _L0_xattn_in['value_up'], 'L0_ffn_Wg': _L0_ffn_in['Wg'], 'L0_ffn_W1': _L0_ffn_in['W1'], 'L0_ffn_b1': _L0_ffn_in['b1'], 'L0_ffn_W2': _L0_ffn_in['W2'], 'L0_ffn_b2': _L0_ffn_in['b2'], 'L0_ffn_Ws1': _L0_ffn_in['Ws1'], 'L0_ffn_bs1': _L0_ffn_in['bs1'], 'L0_ffn_Ws2': _L0_ffn_in['Ws2'], 'L0_ffn_bs2': _L0_ffn_in['bs2'], 'L1_xattn_Wq': _L1_xattn_in['Wq'], 'L1_xattn_bq': _L1_xattn_in['bq'], 'L1_xattn_Wk': _L1_xattn_in['Wk'], 'L1_xattn_bk': _L1_xattn_in['bk'], 'L1_xattn_Wv': _L1_xattn_in['Wv'], 'L1_xattn_bv': _L1_xattn_in['bv'], 'L1_xattn_Wo': _L1_xattn_in['Wo'], 'L1_xattn_bo': _L1_xattn_in['bo'], 'L1_ffn_clip_x': _L1_ffn_in['clip_x'], 'L1_ffn_clip_down': _L1_ffn_in['clip_down'], 'L1_ffn_w_gate': _L1_ffn_in['w_gate'], 'L1_ffn_w_up': _L1_ffn_in['w_up'], 'L1_ffn_w_down': _L1_ffn_in['w_down']}

def reference(x, ctx_1024, L0_xattn_key_down, L0_xattn_query_down, L0_xattn_query_down_bias, L0_xattn_value_down, L0_xattn_value_up, L0_ffn_Wg, L0_ffn_W1, L0_ffn_b1, L0_ffn_W2, L0_ffn_b2, L0_ffn_Ws1, L0_ffn_bs1, L0_ffn_Ws2, L0_ffn_bs2, L1_xattn_Wq, L1_xattn_bq, L1_xattn_Wk, L1_xattn_bk, L1_xattn_Wv, L1_xattn_bv, L1_xattn_Wo, L1_xattn_bo, L1_ffn_clip_x, L1_ffn_clip_down, L1_ffn_w_gate, L1_ffn_w_up, L1_ffn_w_down):
    import jax
    import jax.numpy as jnp

    def _L0_xattn_ref(query_tokens, key_tokens, key_down, query_down, query_down_bias, value_down, value_up):
        import jax, jax.numpy as jnp
        import numpy as np
        NOT_EPSILON = 1.0
        W_SCALE = 0.05
        H, T, A, C = (8, 256, 64, 64)

        def swishmax(x, axis):
            m = jnp.max(x, axis=axis, keepdims=True)
            xe = x * jnp.exp(x - m)
            return xe / (jnp.sum(jnp.abs(xe), axis=axis, keepdims=True) + NOT_EPSILON)
        k = jnp.einsum('bkt,hta->bhka', key_tokens, key_down)
        q = jnp.einsum('bqt,hta->bhqa', query_tokens, query_down) + query_down_bias[None]
        logits = jnp.einsum('bhka,bhqa->bhkq', k, q)
        attn = swishmax(logits, axis=-2)
        vs = jnp.einsum('bhkq,bkt->bhqt', attn, key_tokens)
        vs = jnp.einsum('bhqc,hct->bhqt', jnp.einsum('bhqt,htc->bhqc', vs, value_down), value_up)
        return vs.sum(axis=1)

    def _L0_ffn_ref(x, Wg, W1, b1, W2, b2, Ws1, bs1, Ws2, bs2):
        import jax, jax.numpy as jnp
        import numpy as np
        D_MODEL, D_FF, N_EXPERTS, TOP_K = (256, 1024, 8, 2)
        BATCH, SEQ = (2, 512)
        B, S, D = x.shape
        xf = x.reshape(B * S, D)
        T = B * S
        logits = xf @ Wg
        top_vals, top_idx = jax.lax.top_k(logits, TOP_K)
        top_w = jax.nn.softmax(top_vals, axis=-1)
        combine = jnp.zeros((T, N_EXPERTS), x.dtype).at[jnp.arange(T)[:, None], top_idx].add(top_w)
        h = jax.nn.relu(jnp.einsum('td,edf->tef', xf, W1) + b1)
        sparse = jnp.einsum('te,tef,efd->td', combine, h, W2)
        sparse = sparse + combine @ b2
        shared = jax.nn.relu(xf @ Ws1 + bs1) @ Ws2 + bs2
        out = sparse + shared
        return out.reshape(B, S, D)

    def _L1_xattn_ref(query, key, value, Wq, bq, Wk, bk, Wv, bv, Wo, bo):
        import jax, jax.numpy as jnp
        import numpy as np
        H = 16
        B, S, D = query.shape
        d_k = D // H

        def proj(x, W, b):
            y = jnp.einsum('bsd,ed->bse', x, W) + b
            return y.reshape(B, -1, H, d_k).transpose(0, 2, 1, 3)
        q = proj(query, Wq, bq)
        k = proj(key, Wk, bk)
        v = proj(value, Wv, bv)
        scores = jnp.einsum('bhqd,bhkd->bhqk', q, k) / jnp.sqrt(jnp.float32(d_k))
        p = jax.nn.softmax(scores, axis=-1)
        x = jnp.einsum('bhqk,bhkd->bhqd', p, v)
        x = x.transpose(0, 2, 1, 3).reshape(B, S, D)
        return jnp.einsum('bsd,ed->bse', x, Wo) + bo

    def _L1_ffn_ref(x, clip_x, clip_down, w_gate, w_up, w_down):
        import jax, jax.numpy as jnp
        import numpy as np
        QMAX = 127.0

        def _ste_round(v):
            return v + jax.lax.stop_gradient(jnp.round(v) - v)

        def _act_fake_quant(x, clip_factor):
            scale = jax.nn.sigmoid(clip_factor) * jnp.max(jnp.abs(x)) / QMAX
            return jnp.clip(_ste_round(x / scale), -QMAX - 1.0, QMAX) * scale

        def _weight_fake_quant(w):
            scale = jnp.max(jnp.abs(w), axis=1, keepdims=True) / QMAX
            return jnp.clip(_ste_round(w / scale), -QMAX - 1.0, QMAX) * scale
        xq = _act_fake_quant(x, clip_x[0])
        gate = jnp.einsum('bsh,ih->bsi', xq, _weight_fake_quant(w_gate))
        up = jnp.einsum('bsh,ih->bsi', xq, _weight_fake_quant(w_up))
        h = _act_fake_quant(jax.nn.silu(gate) * up, clip_down[0])
        return jnp.einsum('bsi,hi->bsh', h, _weight_fake_quant(w_down))
    x = x + _L0_xattn_ref(_layernorm(x, axis=-1), ctx_1024, L0_xattn_key_down, L0_xattn_query_down, L0_xattn_query_down_bias, L0_xattn_value_down, L0_xattn_value_up)
    x = x + _L0_ffn_ref(_layernorm(x, axis=-1), L0_ffn_Wg, L0_ffn_W1, L0_ffn_b1, L0_ffn_W2, L0_ffn_b2, L0_ffn_Ws1, L0_ffn_bs1, L0_ffn_Ws2, L0_ffn_bs2)
    x = x + _L1_xattn_ref(_layernorm(x, axis=-1), ctx_1024, ctx_1024, L1_xattn_Wq, L1_xattn_bq, L1_xattn_Wk, L1_xattn_bk, L1_xattn_Wv, L1_xattn_bv, L1_xattn_Wo, L1_xattn_bo)
    x = x + _L1_ffn_ref(_layernorm(x, axis=-1), L1_ffn_clip_x, L1_ffn_clip_down, L1_ffn_w_gate, L1_ffn_w_up, L1_ffn_w_down)
    return x

_drawn_inputs = setup_inputs


def setup_inputs(seed=0):
    import zlib

    import numpy as np

    out = dict(_drawn_inputs(seed))
    spreads = {'L0_ffn_b1': (0.0, 0.347),
     'L0_ffn_b2': (0.0, 0.1),
     'L0_ffn_bs1': (0.0, 0.272),
     'L0_ffn_bs2': (0.0, 0.1)}
    factors = {'L1_xattn_bq': 8.0,
     'L1_xattn_bk': 8.0,
     'L1_xattn_bv': 8.0,
     'L1_xattn_bo': 7.796,
     'L1_ffn_w_gate': 2.903,
     'L1_ffn_w_up': 2.802,
     'L1_ffn_w_down': 2.776}
    for name, (base, spread) in spreads.items():
        noise = np.random.default_rng([zlib.crc32(name.encode()), seed]).standard_normal(out[name].shape)
        drawn = base * np.exp(spread * noise) if base else spread * noise
        out[name] = jnp.asarray(drawn.astype(out[name].dtype))
    for name, factor in factors.items():
        out[name] = (out[name] * factor).astype(out[name].dtype)
    return out
```

```python
import concourse.bass as bass
from concourse import mybir
from contextlib import ExitStack
import numpy as np

F32 = mybir.dt.float32
F16 = mybir.dt.float16
BF16 = mybir.dt.bfloat16
I32 = mybir.dt.int32
ALU = mybir.AluOpType
ACT = mybir.ActivationFunctionType
AX_X = mybir.AxisListType.X
AX_XY = mybir.AxisListType.XY

RMAX = bass.bass_isa.ReduceOp.max

P = 128
B, S, D = 4, 1024, 256
KEYS = 64
T = B * S
NT = T // P
TPB = S // P
DC = D // P
EXPERTS, FF = 8, 1024
NE = EXPERTS + 1
FC = FF // P
SLOT = 256
SHARED = T // SLOT
ROUTED = (2 * T + EXPERTS * (SLOT - 1)) // SLOT
NTILE = SHARED + ROUTED
ROWS = NTILE * SLOT
PIECES = 4 * NE
EARLY = 32
INTER = 704
IC = (INTER + P - 1) // P
TAIL = INTER - (IC - 1) * P
MAGIC = 1.5 * 2.0 ** 23
EPS = 1e-5

XS = 64.0
PS = 1024.0
UNSCALE = 1.0 / (XS * XS)
UNSCALE_P = 1.0 / (XS * PS)


class Layer:
    def __init__(self, heads, dim, scale):
        self.heads, self.dim = heads, dim
        self.feat = heads * dim
        self.nc_ = self.feat // P
        self.hpc = P // dim
        self.width = self.hpc * KEYS
        self.cols = heads * KEYS
        self.banks = self.cols // 512
        self.nu = self.cols // P
        self.gscale = XS * scale


LAYERS = [Layer(8, 64, 1.0), Layer(16, 16, 0.25)]

C_ID, C_TRI = 0, P
C_SEL = C_TRI + P
C_IOTA = C_SEL + 2
C_RESET = C_IOTA + EXPERTS
C_THR = C_RESET + EXPERTS * NT
C_ONE = C_THR + ROUTED
C_POW = C_ONE + P
C_END = C_POW + 1


def run_steps(eng, lo, hi, step):
    pairs = (hi - lo) // 2
    if pairs:
        with eng.Fori(0, pairs) as j:
            step(j * 2 + lo, lo % 2)
            step(j * 2 + (lo + 1), (lo + 1) % 2)
    if (hi - lo) % 2:
        step(hi - 1, (hi - 1) % 2)


def skewed(eng, n, first, stages):
    def step(t, parity):
        for lag, body in stages:
            if not isinstance(t, int) or 0 <= t - lag < n:
                body(t - lag, (parity - lag) % 2)
    for t in range(first):
        step(t, t % 2)
    run_steps(eng, first, n, step)
    for t in range(n, n + max(lag for lag, _ in stages)):
        step(t, t % 2)


def past(i, depth):
    return not isinstance(i, int) or i >= depth


def wait_apart(eng, passed, sem, value):
    eng.wait_ge(sem, value)
    eng.sem_inc(passed, 1)


def turns(i, par):
    return (i - par) * 8 + 16


def prepare_attention(nc, L, d, consts, G, U, Brow, wg16, room):
    l = LAYERS[L]
    C, W, NU = l.nc_, l.width, l.nu
    gsplit = l.banks
    units = [("g", m, c) for m in range(DC) for c in range(gsplit)]
    units += [("b", c, 0) for c in range(gsplit)]
    units += [("u", k, 0) for k in range(NU // 2)]
    RING = 5
    NUn = len(units)
    G = G.rearrange("p (b m h c) -> p b m h c", b=B, m=DC, h=2)
    U = U.rearrange("p (b u h c) -> p b u h c", b=B, u=NU, h=2)
    Brow = Brow.rearrange("p (b c) -> p b c", b=B)
    with ExitStack() as ctx:
        def sb(name, shape, dt=F32):
            return ctx.enter_context(nc.sbuf_tensor(f"p{L}_{name}", shape, dt))

        def sem(name):
            return ctx.enter_context(nc.semaphore(f"p{L}_{name}"))
        if room is None:
            room = sb("w", [P, 4 * DC * l.feat])[:, :]
        wk, wv, wq, wo = (room[:, n * DC * l.feat:(n + 1) * DC * l.feat] for n in range(4))
        wk, wv = (w.rearrange("p (m f) -> p m f", m=DC) for w in (wk, wv))
        wq, wo = (w.rearrange("p (c d) -> p c d", c=C) for w in (wq, wo))
        ctxT = sb("ctxT", [P, DC, B * KEYS])
        bias = sb("bias", [P, 3, C])
        bqb = sb("bqb", [P, C, P])
        kvT = sb("kvT", [P, 2, C, B * KEYS])
        bd = sb("bd", [P, 2, 2, C, W])
        bhi = sb("bhi", [P, 512], F16)
        blo = sb("blo", [P, 512], F16)
        bmix = sb("bmix", [P, 512], F16)
        wg = sb("wg", [P, DC, EXPERTS])
        mask_sb = sb("mask", [P, W])
        ps_kv = [ctx.enter_context(nc.psum_tensor(f"p{L}_pskv{i}", [P, 512], F32)) for i in range(2)]
        ps = [ctx.enter_context(nc.psum_tensor(f"p{L}_ps{i}", [P, 512], F32)) for i in range(RING)]
        loaded, kv_ready, kv_done = sem("loaded"), sem("kv_ready"), sem("kv_done")
        bq_done, k_ready, v_ready, unit_ready = sem("bq_done"), sem("k_ready"), sem("v_ready"), sem("unit_ready")
        hi_done, lo_done, mix = sem("hi_done"), sem("lo_done"), sem("mix")
        wg_hi = sem("wg_hi")
        block = ctx.enter_context(nc.Block())
        n_loads = 7 + (2 if L == 0 else 0)
        mask = mask_sb[:, :].rearrange("p (h k) -> p h k", k=KEYS)

        @block.sync
        def _(sp):
            if L == 0:
                sp.dma_start(consts[:, :], d["consts"]).then_inc(loaded, 16)
                sp.dma_start(wg[:, :, :], d["wg"]).then_inc(loaded, 16)
            sp.dma_start(mask_sb[:, :], d["mask"][L]).then_inc(loaded, 16)
            sp.dma_start(wk, d["wk"][L]).then_inc(loaded, 16)
            sp.dma_start(ctxT[:, :, :], d["ctxT"]).then_inc(loaded, 16)
            sp.dma_start(wv, d["wv"][L]).then_inc(loaded, 16)
            sp.dma_start(bias[:, :, :], d["bias"][L]).then_inc(loaded, 16)
            sp.dma_start(wq, d["wq"][L]).then_inc(loaded, 16)
            sp.dma_start(wo, d["wo"][L]).then_inc(loaded, 16)

        @block.tensor
        def _(pe):
            pe.wait_ge(loaded, 16 * n_loads)
            for c in range(C):
                if c >= 2:
                    pe.wait_ge(kv_done, 2 * (c - 1))
                for j, w in enumerate((wk, wv)):
                    for m in range(DC):
                        last = nc.tensor.matmul(ps_kv[c % 2][:, j * 256:(j + 1) * 256], w[:, m, c * P:(c + 1) * P],
                                                ctxT[:, m, :], start=m == 0, stop=m == DC - 1)
                last.then_inc(kv_ready, 1)
            pe.wait_ge(bq_done, 1)
            for b in range(B):
                pe.wait_ge(k_ready, b + 1)
                for n, (kind, x, y) in enumerate(units):
                    at = b * NUn + n
                    bank = ps[at % RING]
                    if at >= RING:
                        pe.wait_ge(lo_done, at - RING + 1)
                    if kind == "u" and x == 0:
                        pe.wait_ge(v_ready, b + 1)
                    if kind == "g" and l.banks == 1:
                        for c in range(C):
                            last = nc.tensor.matmul(bank[:, c * W:(c + 1) * W], wq[:, c, x * P:(x + 1) * P],
                                                    bd[:, b % 2, 0, c, :], start=True, stop=True)
                    elif kind == "g":
                        last = nc.tensor.matmul(bank[:, :], wq[:, y, x * P:(x + 1) * P], bd[:, b % 2, 0, y, :],
                                                start=True, stop=True)
                    elif kind == "b":
                        for c in (range(C) if l.banks == 1 else (x,)):
                            o = c * W if l.banks == 1 else 0
                            last = nc.tensor.matmul(bank[:, o:o + W], bqb[:, c, :], bd[:, b % 2, 0, c, :],
                                                    start=True, stop=True)
                    else:
                        for k in range(2):
                            u = 2 * x + k
                            c, o = (u * P) // W, (u * P) % W
                            last = nc.tensor.matmul(bank[:, k * D:(k + 1) * D], bd[:, b % 2, 1, c, o:o + P], wo[:, c, :],
                                                    start=True, stop=True)
                    last.then_inc(unit_ready, 1)

        @block.scalar
        def _(act):
            act.wait_ge(loaded, 16 * n_loads)
            if L == 0:
                nc.scalar.activation(wg16[:, :, 0, :], wg[:, :, :], ACT.Copy, scale=XS).then_inc(wg_hi, 1)
            for b in range(B):
                for n, (kind, x, y) in enumerate(units):
                    at = b * NUn + n
                    act.wait_ge(unit_ready, at + 1)
                    bank = ps[at % RING]
                    if kind == "g":
                        nc.scalar.activation(G[:, b, x, 0, y * 512:(y + 1) * 512], bank[:, :], ACT.Copy,
                                             scale=l.gscale).then_inc(hi_done, 1)
                    elif kind == "b":
                        if b * gsplit + x > 0:
                            act.wait_ge(mix, 2 * (b * gsplit + x))
                        nc.scalar.activation(bhi[:, :], bank[:, :], ACT.Copy, scale=l.gscale).then_inc(hi_done, 1)
                    else:
                        nc.scalar.activation(U[:, b, 2 * x:2 * x + 2, 0, :], bank[:, :].rearrange("p (k d) -> p k d", d=D),
                                             ACT.Copy, scale=XS).then_inc(hi_done, 1)

        @block.gpsimd
        def _(pool):
            pool.wait_ge(kv_done, 2 * C)
            for b in range(B):
                if b >= 2:
                    pool.wait_ge(unit_ready, (b - 1) * NUn)
                for c in range(C):
                    src = kvT[:, 1, c, b * KEYS:(b + 1) * KEYS].unsqueeze(1).to_broadcast([P, l.hpc, KEYS])
                    last = nc.gpsimd.tensor_tensor(bd[:, b % 2, 1, c, :].rearrange("p (h k) -> p h k", k=KEYS),
                                                   src, mask, ALU.mult)
                last.then_inc(v_ready, 1)

        @block.vector
        def _(dve):
            dve.wait_ge(loaded, 16 * n_loads)
            for c in range(C):
                dve.wait_ge(kv_ready, c + 1)
                for j in range(2):
                    nc.vector.tensor_scalar(kvT[:, j, c, :], ps_kv[c % 2][:, j * 256:(j + 1) * 256],
                                            bias[:, 1 + j, c:c + 1], None, ALU.add).then_inc(kv_done, 1)
            nc.vector.tensor_copy(bqb[:, :, :], bias[:, 0, :].unsqueeze(2).to_broadcast([P, C, P])).then_inc(bq_done, 1)
            if L == 0:
                dve.wait_ge(wg_hi, 1)
                nc.vector.scalar_tensor_tensor(out=wg16[:, :, 1, :], in0=wg[:, :, :], scalar=XS, in1=wg16[:, :, 0, :],
                                               op0=ALU.mult, op1=ALU.subtract).then_inc(wg_hi, 1)
            dve.wait_ge(kv_done, 2 * C)
            def diagonal_k(b):
                if b >= 2:
                    dve.wait_ge(unit_ready, (b - 1) * NUn)
                for c in range(C):
                    src = kvT[:, 0, c, b * KEYS:(b + 1) * KEYS].unsqueeze(1).to_broadcast([P, l.hpc, KEYS])
                    last = nc.vector.tensor_tensor(bd[:, b % 2, 0, c, :].rearrange("p (h k) -> p h k", k=KEYS),
                                                   src, mask, ALU.mult)
                last.then_inc(k_ready, 1)
            diagonal_k(0)
            for b in range(B):
                if b + 1 < B:
                    diagonal_k(b + 1)
                for n, (kind, x, y) in enumerate(units):
                    at = b * NUn + n
                    dve.wait_ge(hi_done, at + 1)
                    bank = ps[at % RING]
                    if kind == "g":
                        nc.vector.scalar_tensor_tensor(out=G[:, b, x, 1, y * 512:(y + 1) * 512], in0=bank[:, :],
                                                       scalar=l.gscale, in1=G[:, b, x, 0, y * 512:(y + 1) * 512],
                                                       op0=ALU.mult, op1=ALU.subtract).then_inc(lo_done, 1)
                    elif kind == "b":
                        nc.vector.scalar_tensor_tensor(out=blo[:, :], in0=bank[:, :], scalar=l.gscale, in1=bhi[:, :],
                                                       op0=ALU.mult, op1=ALU.subtract).then_inc(lo_done, 1)
                        dve.wait_ge(lo_done, at + 1)
                        k = 2 * (b * gsplit + x)
                        nc.vector.tensor_scalar(bmix[:, :], bhi[:, :], consts[:, C_SEL:C_SEL + 1], None,
                                                ALU.mult).then_inc(mix, 1)
                        dve.wait_ge(mix, k + 1)
                        nc.vector.scalar_tensor_tensor(out=Brow[:, b, x * 512:(x + 1) * 512], in0=blo[:, :],
                                                       scalar=consts[:, C_SEL + 1:C_SEL + 2], in1=bmix[:, :],
                                                       op0=ALU.mult, op1=ALU.add).then_inc(mix, 1)
                    else:
                        nc.vector.scalar_tensor_tensor(out=U[:, b, 2 * x:2 * x + 2, 1, :],
                                                       in0=bank[:, :].rearrange("p (k d) -> p k d", d=D), scalar=XS,
                                                       in1=U[:, b, 2 * x:2 * x + 2, 0, :],
                                                       op0=ALU.mult, op1=ALU.subtract).then_inc(lo_done, 1)


def attention(nc, L, d, consts, ones16, ident16, G, U, Brow, env):
    l = LAYERS[L]
    H, COLS, NU, BANKS = l.heads, l.cols, l.nu, l.banks
    first = L == 0
    with ExitStack() as ctx:
        def sb(name, shape, dt=F32):
            return ctx.enter_context(nc.sbuf_tensor(f"a{L}_{name}", shape, dt))

        def pb(name, shape, dt=F32):
            return ctx.enter_context(nc.psum_tensor(f"a{L}_{name}", shape, dt))

        def sem(name):
            return ctx.enter_context(nc.semaphore(f"a{L}_{name}"))

        stat = sb("stat", [P, 2, 6])
        mv = sb("mv", [P, 2, 2])
        rstd = sb("rstd", [P, 2, 1])
        stat2 = sb("stat2", [P, 2, 6])
        mv2 = sb("mv2", [P, 2, 2])
        rstd2 = sb("rstd2", [P, 2, 1])
        xn = sb("xn", [P, 2, D])
        xT = sb("xT", [P, 2, 2, D], F16)
        top = sb("top", [P, 2, H])
        prob = sb("prob", [P, 2, COLS])
        total = sb("total", [P, 2, H])
        rtotal = sb("rtotal", [P, 2, H])
        pT = sb("pT", [P, 2, 2, COLS], F16)
        psT = pb("psT", [P, 512])
        ob = 2 if first else 1
        psO = [pb(f"psO{k}", [P, 512]) for k in range(ob)]
        psS = [pb(f"psS{k}", [P, COLS]) for k in range(2)]
        psP = pb("psP", [P, COLS])
        if first:
            x_in = sb("x_in", [P, 2, D])
            x_res = sb("x_res", [P, 2, D])
            x_out = sb("x_out", [P, 2, D])
            xe = sb("xe", [P, 2, COLS])
            added = sb("added", [P, 2, H])
            xn2 = sb("xn2", [P, 2, D])
            xs = sb("xs", [P, 2, 2, D], F16)
            x2T = sb("x2T", [P, 2, 2 * D], F16)
            stage = sb("stage", [P, 2, 1024])
            psX = pb("psX", [P, 4 * D], F16)
            psL = pb("psL", [P, 512])
            logits, W_all, zero16, wg16 = env["logits"], env["W_all"], env["zero16"], env["wg16"]
        else:
            y_sh = sb("y_sh", [P, 2, D])
            y_exp = sb("y_exp", [P, 2, 2, D])
            idx = sb("idx", [P, 2, 2], I32)
            acc = sb("acc", [P, 2, D])
            xall, xn4, mx = env["xall"], env["xn4"], env["mx"]
            pos, wts, bo_row = env["pos"], env["wts"], env["bo_row"]

        ld_x = [sem(f"ld_x{k}") for k in range(2)]
        LNK = 4 if first else 6
        SUMK = 4 if first else 2
        OUTK = 5 if first else 6
        ln_done = sem("ln_done")
        rstd_in, rstd_out = sem("rstd_in"), sem("rstd_out")
        xT_ready, x_hi, x_lo = sem("xT_ready"), sem("x_hi"), sem("x_lo")
        scores_ready, shifted = sem("scores_ready"), sem("shifted")
        exp_done, sum_done, prob_done = sem("exp_done"), sem("sum_done"), sem("prob_done")
        pT_ready, p_hi, p_lo = sem("pT_ready"), sem("p_hi"), sem("p_lo")
        pv_ready, out_done = sem("pv_ready"), sem("out_done")
        if first:
            ld_res = [sem(f"ld_res{k}") for k in range(2)]
            ld_w = [sem(f"ld_w{k}") for k in range(2)]
            st_x = [sem(f"st_x{k}") for k in range(2)]
            st_s = [sem(f"st_s{k}") for k in range(2)]
            st_zero = sem("st_zero")
            n_hi, n_lo = sem("n_hi"), sem("n_lo")
            nT_ready, nT_done, logit_ready, logit_done = sem("nT_ready"), sem("nT_done"), sem("logit_ready"), sem("logit_done")
            w_hi, w_lo = sem("w_hi"), sem("w_lo")
        else:
            ld_y = [sem(f"ld_y{k}") for k in range(2)]
            ld_e = [sem(f"ld_e{k}") for k in range(2)]
            ld_bo = sem("ld_bo")
            idx_done, shared_added, bo_added = sem("idx_done"), sem("shared_added"), sem("bo_added")

        block = ctx.enter_context(nc.Block())
        FIRST = 12
        A = 0 if first else 2

        def batch(i):
            return i // TPB

        def seg(tensor, flat, i, count, size):
            v = tensor[:, :, :].rearrange("p t c -> p (t c)")
            return v[:, bass.ds(i * count + flat, size)]

        @block.sync
        def _(sp):
            if first:
                sp.dma_start(d["xs"][T:ROWS, :].rearrange("(j p) c -> p j c", p=P),
                             zero16[:, :].unsqueeze(1).to_broadcast([P, (ROWS - T) // P, 2 * D])).then_inc(st_zero, 16)
            else:
                sp.dma_start(bo_row[:, :], d["bo"]).then_inc(ld_bo, 16)

            def load(i, par):
                rows = d["x0" if first else "x1"][bass.ds(i * P, P), :]
                if past(i, 2):
                    sp.wait_ge(ln_done, (i - 2) * LNK + (LNK if first else 2))
                if first:
                    sp.dma_start(x_in[:, par, :], rows).then_inc(ld_x[par], 16)
                else:
                    sp.dma_start(seg(xall, 0, i, D, D), rows).then_inc(ld_x[par], 16)
                    sp.dma_start(y_sh[:, par, :], d["y"][bass.ds(i * P, P), :]).then_inc(ld_y[par], 16)

            def load_res(i, par):
                if past(i, 2):
                    sp.wait_ge(out_done, (i - 2) * OUTK + 1)
                sp.dma_start(x_res[:, par, :], d["x0"][bass.ds(i * P, P), :]).then_inc(ld_res[par], 16)

            def load_piece(i, par):
                if past(i, 2):
                    sp.wait_ge(w_lo, i - 1)
                sp.dma_start(stage[:, par, :], d["w"][bass.ds(i * P, P), :]).then_inc(ld_w[par], 16)

            def store(i, par):
                sp.wait_ge(out_done, i * OUTK + 1)
                sp.dma_start(d["x1"][bass.ds(i * P, P), :], x_out[:, par, :]).then_inc(st_x[par], 16)
                sp.wait_ge(n_lo, i + 1)
                sp.dma_start(d["xs"][bass.ds(i * P, P), :], xs[:, par, :, :].rearrange("p h c -> p (h c)")).then_inc(st_s[par], 16)

            if first:
                skewed(sp, NT, FIRST, [(0, load), (5, load_res), (7, store), (0, load_piece)])
                for k in range(2):
                    sp.wait_ge(st_x[k], NT * 8)
                    sp.wait_ge(st_s[k], NT * 8)
                sp.wait_ge(st_zero, 16)
            else:
                skewed(sp, NT, FIRST, [(0, load)])

        @block.tensor
        def _(pe):
            def transpose_x(i, par):
                pe.wait_ge(ln_done, (i + 1) * LNK)
                if past(i, 1):
                    pe.wait_ge(x_lo, i)
                for m in range(DC):
                    last = nc.tensor.transpose(psT[:, m * P:(m + 1) * P], xn[:, par, m * P:(m + 1) * P],
                                               consts[:, C_ID:C_ID + P])
                last.then_inc(xT_ready, 1)

            def scores(i, par):
                b = batch(i)
                pe.wait_ge(x_lo, i + 1)
                if past(i, 2):
                    pe.wait_ge(sum_done if first else shifted, (i - 2) * (SUMK if first else 2) + (1 if first else 2))
                for h in range(BANKS):
                    out = psS[par][:, h * 512:(h + 1) * 512]
                    nc.tensor.matmul(out, ones16[:, :], Brow[:, bass.ds(b * COLS + h * 512, 512)], start=True, stop=False)
                    for m in range(DC):
                        for xh, gh in ((0, 0), (0, 1), (1, 0)):
                            off = ((b * DC + m) * 2 + gh) * COLS + h * 512
                            last = nc.tensor.matmul(out, xT[:, par, xh, m * P:(m + 1) * P], G[:, bass.ds(off, 512)],
                                                    start=False, stop=m == DC - 1 and xh == 1)
                last.then_inc(scores_ready, 1)

            def transpose_p(i, par):
                pe.wait_ge(prob_done, i + 1)
                if past(i, 1):
                    pe.wait_ge(p_lo, i)
                src = xe if first else prob
                for u in range(NU):
                    last = nc.tensor.transpose(psP[:, u * P:(u + 1) * P], src[:, par, u * P:(u + 1) * P],
                                               consts[:, C_ID:C_ID + P])
                last.then_inc(pT_ready, 1)

            def values(i, par):
                b = batch(i)
                pe.wait_ge(p_lo, i + 1)
                if past(i, ob):
                    pe.wait_ge(out_done, (i - ob) * OUTK + 1)
                for u in range(NU):
                    for ph, uh in ((0, 0), (0, 1), (1, 0)):
                        off = ((b * NU + u) * 2 + uh) * D
                        last = nc.tensor.matmul(psO[par % ob][:, 0:D], pT[:, par, ph, u * P:(u + 1) * P], U[:, bass.ds(off, D)],
                                                start=u == 0 and ph == 0 and uh == 0, stop=u == NU - 1 and ph == 1)
                last.then_inc(pv_ready, 1)

            def transpose_n(i, par):
                pe.wait_ge(n_lo, i + 1)
                if past(i, 1):
                    pe.wait_ge(nT_done, i)
                for k in range(4):
                    last = nc.tensor.transpose(psX[:, k * P:(k + 1) * P],
                                               xs[:, par, k // 2, (k % 2) * P:(k % 2 + 1) * P], ident16[:, :])
                last.then_inc(nT_ready, 1)

            def router(i, par):
                pe.wait_ge(nT_done, i + 1)
                if past(i, 1):
                    pe.wait_ge(logit_done, i)
                k = 0
                for m in range(DC):
                    for xh in range(2):
                        for gh in range(2):
                            last = nc.tensor.matmul(psL[:, 0:EXPERTS], x2T[:, par, (xh * DC + m) * P:(xh * DC + m + 1) * P],
                                                    wg16[:, m, gh, :], start=k == 0, stop=k == 7)
                            k += 1
                last.then_inc(logit_ready, 1)

            stages = [(A + 1, transpose_x), (A + 4, transpose_p), (A + 2, scores)]
            if first:
                stages += [(8, router), (4, values), (7, transpose_n)]
            else:
                stages += [(A + 4, values)]
            skewed(pe, NT, FIRST, stages)

        @block.scalar
        def _(act):
            def exps(i, par):
                act.wait_ge(shifted, 2 * (i + 1))
                nc.scalar.activation(prob[:, par, :], prob[:, par, :], ACT.Exp, scale=UNSCALE).then_inc(exp_done, 1)

            def x_high(i, par):
                act.wait_ge(xT_ready, i + 1)
                if past(i, 2):
                    act.wait_ge(scores_ready, i - 1)
                nc.scalar.activation(xT[:, par, 0, :], psT[:, 0:D], ACT.Copy, scale=XS).then_inc(x_hi, 1)

            def p_high(i, par):
                act.wait_ge(pT_ready, i + 1)
                if past(i, 2):
                    act.wait_ge(pv_ready, i - 1)
                nc.scalar.activation(pT[:, par, 0, :], psP[:, :], ACT.Copy, scale=PS).then_inc(p_hi, 1)

            def n_high(i, par):
                act.wait_ge(out_done, (i + 1) * OUTK)
                if past(i, 2):
                    act.wait_ge(nT_ready, i - 1)
                    act.wait_ge(st_s[par], turns(i - 2, par))
                nc.scalar.activation(xs[:, par, 0, :], xn2[:, par, :], ACT.Copy, scale=XS).then_inc(n_hi, 1)

            def copy_n(i, par):
                act.wait_ge(nT_ready, i + 1)
                if past(i, 2):
                    act.wait_ge(logit_ready, i - 1)
                nc.scalar.activation(x2T[:, par, :], psX[:, 0:2 * D], ACT.Copy).then_inc(nT_done, 1)

            def weight_high(i, par):
                act.wait_ge(ld_w[par], turns(i, par))
                flat = W_all[:, :, :, :].rearrange("p n h c -> p (n h c)")
                nc.scalar.activation(stage[:, par, :], stage[:, par, :], ACT.Copy, scale=XS).then_inc(w_hi, 1)
                act.wait_ge(w_hi, i * 2 + 1)
                nc.scalar.activation(flat[:, bass.ds(i * 2048, 1024)], stage[:, par, :], ACT.Copy).then_inc(w_hi, 1)

            stages = [(A + 3, exps), (A + 1, x_high), (A + 4, p_high)]
            if first:
                stages += [(0, weight_high), (7, copy_n), (5, n_high)]
            skewed(act, NT, FIRST, stages)

        @block.gpsimd
        def _(pool):
            def normalise(i, par):
                pool.wait_ge(sum_done, SUMK * (i + 1))
                t = xe if first else prob
                v = t[:, par, :].rearrange("p (h k) -> p h k", k=KEYS)
                nc.gpsimd.tensor_tensor(v, v, rtotal[:, par, :].unsqueeze(2).to_broadcast([P, H, KEYS]),
                                        ALU.mult).then_inc(prob_done, 1)

            def weight_low(i, par):
                flat = W_all[:, :, :, :].rearrange("p n h c -> p (n h c)")
                pool.wait_ge(w_hi, (i + 1) * 2)
                nc.gpsimd.tensor_tensor(flat[:, bass.ds(i * 2048 + 1024, 1024)], stage[:, par, :],
                                        flat[:, bass.ds(i * 2048, 1024)], ALU.subtract).then_inc(w_lo, 1)

            def gather(i, par):
                if past(i, 2):
                    pool.wait_ge(ln_done, (i - 2) * LNK + 2)
                    pool.wait_ge(ld_e[par], 2 * turns(i - 2, par))
                flat = pos[:, :, :].rearrange("p t k -> p (t k)")
                nc.gpsimd.tensor_copy(idx[:, par, :], flat[:, bass.ds(i * 2, 2)]).then_inc(idx_done, 1)
                wait_apart(pool, env["passed"], idx_done, i + 1)
                for k in range(2):
                    nc.gpsimd.indirect_dma_start(
                        out=y_exp[:, par, k, :], out_offset=None, in_=d["y"][:, :],
                        in_offset=bass.IndirectOffsetOnAxis(ap=idx[:, par, k:k + 1], axis=0)).then_inc(ld_e[par], 16)

            def add_shared(i, par):
                pool.wait_ge(ld_x[par], turns(i, par))
                pool.wait_ge(ld_y[par], turns(i, par))
                if past(i, 2):
                    pool.wait_ge(ln_done, (i - 2) * LNK + 2)
                nc.gpsimd.tensor_tensor(acc[:, par, :], seg(xall, 0, i, D, D), y_sh[:, par, :], ALU.add).then_inc(shared_added, 1)

            def add_bo(i, par):
                pool.wait_ge(ln_done, (i + 1) * LNK)
                v = seg(xall, 0, i, D, D)
                nc.gpsimd.tensor_tensor(v, v, bo_row[:, :], ALU.add).then_inc(bo_added, 1)

            def power(src, dst, chain, count, done):
                def body(i, par):
                    pool.wait_ge(chain, count(i))
                    nc.gpsimd.tensor_tensor(dst[:, par, :], src[:, par, 1:2], consts[:, C_POW:C_POW + 1],
                                            ALU.pow).then_inc(done, 1)
                return body
            power_in = power(mv, rstd, ln_done, lambda i: i * LNK + (LNK - 1), rstd_in)
            power_out = power(mv2, rstd2, out_done, lambda i: i * OUTK + 4, rstd_out)
            if first:
                skewed(pool, NT, FIRST, [(4, normalise), (0, power_in), (5, power_out), (1, weight_low)])
            else:
                pool.wait_ge(ld_bo, 16)
                skewed(pool, NT, FIRST, [(A + 4, normalise), (A, power_in), (A + 5, power_out), (0, gather), (1, add_shared), (A + 1, add_bo)])

        @block.vector
        def _(dve):
            def x_of(i, par):
                return x_in[:, par, :] if first else seg(xall, 0, i, D, D)

            def weigh_first(i, par):
                dve.wait_ge(shared_added, i + 1)
                dve.wait_ge(ld_e[par], 2 * turns(i, par))
                wf = wts[:, :, :].rearrange("p t k -> p (t k)")
                nc.vector.scalar_tensor_tensor(out=acc[:, par, :], in0=y_exp[:, par, 0, :], scalar=wf[:, bass.ds(i * 2, 1)],
                                               in1=acc[:, par, :], op0=ALU.mult, op1=ALU.add).then_inc(ln_done, 1)

            def weigh_second(i, par):
                wf = wts[:, :, :].rearrange("p t k -> p (t k)")
                dve.wait_ge(ln_done, i * LNK + 1)
                nc.vector.scalar_tensor_tensor(out=x_of(i, par), in0=y_exp[:, par, 1, :], scalar=wf[:, bass.ds(i * 2 + 1, 1)],
                                               in1=acc[:, par, :], op0=ALU.mult, op1=ALU.add).then_inc(ln_done, 1)

            def moments_in(i, par):
                if first:
                    wait_apart(dve, env["passed"], ld_x[par], turns(i, par))
                else:
                    wait_apart(dve, env["passed"], ln_done, i * LNK + 2)
                nc.vector.bn_stats(stat[:, par, :], x_of(i, par)).then_inc(ln_done, 1)

            def mean_in(i, par):
                wait_apart(dve, env["passed"], ln_done, i * LNK + LNK - 3)
                nc.vector.bn_aggr(mv[:, par, :], stat[:, par, :]).then_inc(ln_done, 1)

            def eps_in(i, par):
                dve.wait_ge(ln_done, i * LNK + LNK - 2)
                nc.vector.tensor_scalar(mv[:, par, 1:2], mv[:, par, 1:2], EPS, None, ALU.add).then_inc(ln_done, 1)

            def normalise_in(i, par):
                src = x_of(i, par)
                dve.wait_ge(rstd_in, i + 1)
                if past(i, 2):
                    dve.wait_ge(xT_ready, i - 1)
                nc.vector.tensor_scalar(xn[:, par, :], src, mv[:, par, 0:1], rstd[:, par, :], ALU.subtract,
                                        ALU.mult).then_inc(ln_done, 1)

            def x_low(i, par):
                dve.wait_ge(x_hi, i + 1)
                nc.vector.scalar_tensor_tensor(out=xT[:, par, 1, :], in0=psT[:, 0:D], scalar=XS, in1=xT[:, par, 0, :],
                                               op0=ALU.mult, op1=ALU.subtract).then_inc(x_lo, 1)

            def largest(i, par):
                dve.wait_ge(scores_ready, i + 1)
                if not first and past(i, 2):
                    dve.wait_ge(pT_ready, i - 1)
                s = psS[par][:, :].rearrange("p (h k) -> p h k", k=KEYS)
                nc.vector.tensor_reduce(top[:, par, :], s, AX_X, ALU.max).then_inc(shifted, 1)

            def shift(i, par):
                s = psS[par][:, :].rearrange("p (h k) -> p h k", k=KEYS)
                dve.wait_ge(shifted, i * 2 + 1)
                nc.vector.tensor_tensor(prob[:, par, :].rearrange("p (h k) -> p h k", k=KEYS), s,
                                        top[:, par, :].unsqueeze(2).to_broadcast([P, H, KEYS]),
                                        ALU.subtract).then_inc(shifted, 1)

            def weighted(i, par):
                dve.wait_ge(exp_done, i + 1)
                if past(i, 2):
                    dve.wait_ge(pT_ready, i - 1)
                nc.vector.scalar_tensor_tensor(out=xe[:, par, :], in0=psS[par][:, :], scalar=UNSCALE, in1=prob[:, par, :],
                                               op0=ALU.mult, op1=ALU.mult).then_inc(sum_done, 1)

            def sums(i, par):
                if first:
                    dve.wait_ge(sum_done, i * SUMK + 1)
                    nc.vector.tensor_reduce(total[:, par, :], xe[:, par, :].rearrange("p (h k) -> p h k", k=KEYS), AX_X,
                                            ALU.add, apply_absolute_value=True).then_inc(sum_done, 1)
                else:
                    dve.wait_ge(exp_done, i + 1)
                    nc.vector.tensor_reduce(total[:, par, :], prob[:, par, :].rearrange("p (h k) -> p h k", k=KEYS), AX_X,
                                            ALU.add).then_inc(sum_done, 1)

            def plus_one(i, par):
                dve.wait_ge(sum_done, i * SUMK + 2)
                nc.vector.tensor_scalar(added[:, par, :], total[:, par, :], 1.0, None, ALU.add).then_inc(sum_done, 1)

            def invert(i, par):
                dve.wait_ge(sum_done, i * SUMK + SUMK - 1)
                nc.vector.reciprocal(rtotal[:, par, :], (added if first else total)[:, par, :]).then_inc(sum_done, 1)

            def p_low(i, par):
                dve.wait_ge(p_hi, i + 1)
                nc.vector.scalar_tensor_tensor(out=pT[:, par, 1, :], in0=psP[:, :], scalar=PS, in1=pT[:, par, 0, :],
                                               op0=ALU.mult, op1=ALU.subtract).then_inc(p_lo, 1)

            def output(i, par):
                dve.wait_ge(pv_ready, i + 1)
                base = i * OUTK
                if first:
                    dve.wait_ge(ld_res[par], turns(i, par))
                    if past(i, 2):
                        dve.wait_ge(st_x[par], turns(i - 2, par))
                    x, res = x_out[:, par, :], x_res[:, par, :]
                else:
                    dve.wait_ge(bo_added, i + 1)
                    x = res = seg(xall, 0, i, D, D)
                nc.vector.scalar_tensor_tensor(out=x, in0=psO[par % ob][:, 0:D], scalar=UNSCALE_P, in1=res,
                                               op0=ALU.mult, op1=ALU.add).then_inc(out_done, 1)

            def moments_out(i, par):
                wait_apart(dve, env["passed"], out_done, i * OUTK + 1)
                nc.vector.bn_stats(stat2[:, par, :], x_out[:, par, :] if first else seg(xall, 0, i, D, D)).then_inc(out_done, 1)

            def mean_out(i, par):
                wait_apart(dve, env["passed"], out_done, i * OUTK + 2)
                nc.vector.bn_aggr(mv2[:, par, :], stat2[:, par, :]).then_inc(out_done, 1)

            def eps_out(i, par):
                dve.wait_ge(out_done, i * OUTK + 3)
                nc.vector.tensor_scalar(mv2[:, par, 1:2], mv2[:, par, 1:2], EPS, None, ALU.add).then_inc(out_done, 1)

            def normalise_out(i, par):
                base = i * OUTK
                x, dst = (x_out[:, par, :], xn2[:, par, :]) if first else (seg(xall, 0, i, D, D), seg(xn4, 0, i, D, D))
                dve.wait_ge(rstd_out, i + 1)
                if first and past(i, 2):
                    dve.wait_ge(n_hi, i - 1)
                nc.vector.tensor_scalar(dst, x, mv2[:, par, 0:1], rstd2[:, par, :], ALU.subtract,
                                        ALU.mult).then_inc(out_done, 1)

            def magnitude(i, par):
                dve.wait_ge(out_done, i * OUTK + 5)
                dst = seg(xn4, 0, i, D, D)
                nc.vector.tensor_reduce(mx[:, bass.ds(i, 1)], dst, AX_X, ALU.max,
                                        apply_absolute_value=True).then_inc(out_done, 1)

            def n_low(i, par):
                dve.wait_ge(n_hi, i + 1)
                nc.vector.scalar_tensor_tensor(out=xs[:, par, 1, :], in0=xn2[:, par, :], scalar=XS, in1=xs[:, par, 0, :],
                                               op0=ALU.mult, op1=ALU.subtract).then_inc(n_lo, 1)

            def logit(i, par):
                dve.wait_ge(logit_ready, i + 1)
                nc.vector.tensor_scalar(seg(logits, 0, i, EXPERTS, EXPERTS), psL[:, 0:EXPERTS], UNSCALE, None,
                                        ALU.mult).then_inc(logit_done, 1)

            if first:
                stages = [(3, largest), (0, moments_in), (3, shift), (5, output), (0, mean_in), (5, moments_out),
                          (0, eps_in), (4, p_low), (5, mean_out), (1, x_low), (5, eps_out), (0, normalise_in),
                          (3, weighted), (9, logit), (3, sums), (6, n_low), (3, plus_one), (5, normalise_out),
                          (3, invert)]
            else:
                stages = [(5, largest), (2, weigh_first), (5, shift), (2, weigh_second), (7, output), (2, moments_in),
                          (7, moments_out), (2, mean_in), (7, mean_out), (2, eps_in), (7, eps_out), (6, p_low),
                          (3, x_low), (2, normalise_in), (5, sums), (7, normalise_out), (5, invert), (7, magnitude)]
            skewed(dve, NT, FIRST, stages)


def experts(nc, d, consts, ident16, env):
    logits, W_all, pos, wts = env["logits"], env["W_all"], env["pos"], env["wts"]
    flatW = W_all[:, :, :, :].rearrange("p n h c -> p (n h c)")
    with ExitStack() as ctx:
        def sb(name, shape, dt=F32):
            return ctx.enter_context(nc.sbuf_tensor(f"e_{name}", shape, dt))

        def pb(name, shape, dt=F32):
            return ctx.enter_context(nc.psum_tensor(f"e_{name}", shape, dt))

        def sem(name):
            return ctx.enter_context(nc.semaphore(f"e_{name}"))
        b1 = sb("b1", [P, NE * FC])
        b2 = sb("b2", [P, NE * D])
        stage = sb("stage", [P, 4, 1024])
        x_in = sb("x_in", [P, 2, 2, 2 * D], F16)
        xT = sb("xT", [P, 2, 4 * SLOT], F16)
        h32 = sb("h32", [P, 2, 2 * SLOT])
        h16 = sb("h16", [P, 2, 2, FC * SLOT], F16)
        y_out = sb("y_out", [P, 2, 2, D])
        table = sb("table", [1, NTILE], I32)
        idx = sb("idx", [P, 2, 4], I32)

        room = W_all[:, EARLY:PIECES, :, :].rearrange("p n h c -> p (n h c)")
        taken = [0]

        def sb(name, shape, dt=F32):
            halves = int(np.prod(shape[1:])) * (2 if dt == F32 else 1)
            v = room[0:shape[0], taken[0]:taken[0] + halves]
            taken[0] += halves
            v = v if dt == F16 else v.bitcast(dt)
            if len(shape) == 3:
                v = v.rearrange("p (a b) -> p a b", b=shape[2])
            return v
        rows = sb("rows", [P, 4, 2 * D], F16)
        R = {n: sb("r_" + n, [P, NT, EXPERTS]) for n in ("a", "b", "oh1", "oh2")}
        TE = {n: sb("t_" + n, [P, EXPERTS, NT]) for n in ("tot", "inc")}
        picked = sb("picked", [P, NT * EXPERTS], BF16)
        tri16 = sb("tri16", [P, P], BF16)
        one16 = sb("one16", [P, P], BF16)
        V = {n: sb("v_" + n, [P, NT]) for n in ("v1", "v2", "i", "e", "den")}
        E8 = {n: sb("e8_" + n, [P, EXPERTS]) for n in ("n", "pad", "end", "base")}
        posf = sb("posf", [P, NT, 2])
        cmp_ = sb("cmp", [1, ROUTED, EXPERTS])
        cnt = sb("cnt", [1, ROUTED])

        psX = pb("psX", [P, 8 * P], F16)
        psH = [pb(f"psH{k}", [P, 512]) for k in range(4)]
        psY = [pb(f"psY{k}", [P, 512]) for k in range(2)]
        psR = pb("psR", [P, 512])

        ld_b, ld_w, ld_row = sem("ld_b"), sem("ld_w"), [sem(f"ld_row{k}") for k in range(2)]
        ld_x = [sem(f"ld_x{k}") for k in range(2)]
        st_y = [sem(f"st_y{k}") for k in range(2)]
        scattered = [sem(f"scattered{k}") for k in range(2)]
        idx_done = sem("idx_done")
        route, picked_ready, counts_ready, exp_ready, table_ready = (sem(n) for n in (
            "route", "picked_ready", "counts_ready", "exp_ready", "table_ready"))
        w_lo = sem("w_lo")
        b1_scaled = sem("b1_scaled")
        xT_ready, xT_done = sem("xT_ready"), sem("xT_done")
        h_ready, relu_done, h_split = sem("h_ready"), sem("relu_done"), sem("h_split")
        y_ready, y_done = sem("y_ready"), sem("y_done")
        block = ctx.enter_context(nc.Block())
        FIRST = 6
        NU = FC // 2

        def expert_steps(eng, stages, extra):
            def step(t, parity):
                for lag, body in stages:
                    if not isinstance(t, int) or 0 <= t - lag < NTILE:
                        body(t - lag, (parity - lag) % 2)
            routed[0] = False
            for t in range(FIRST):
                if t in extra:
                    extra[t]()
                step(t, t % 2)
            run_steps(eng, FIRST, SHARED, step)
            eng.wait_ge(table_ready, 1)
            routed[0] = True
            run_steps(eng, SHARED, NTILE, step)
            for t in range(NTILE, NTILE + max(lag for lag, _ in stages)):
                step(t, t % 2)
        routed = [False]

        def expert(eng, i):
            if not routed[0]:
                return 0
            return eng.value_load(table[0:1, bass.ds(i, 1)], min_val=0, max_val=EXPERTS)

        @block.sync
        def _(sp):
            sp.dma_start(b1[:, :], d["b1"]).then_inc(ld_b, 16)
            sp.dma_start(b2[:, :], d["b2"]).then_inc(ld_b, 16)
            for n in range(PIECES - EARLY):
                sp.dma_start(stage[:, n, :], d["w"][(EARLY + n) * P:(EARLY + n + 1) * P, :]).then_inc(ld_w, 16)

            def load(i, par):
                if past(i, 2):
                    sp.wait_ge(xT_ready, i - 1)
                sp.dma_start(x_in[:, par, :, :], d["xs"][bass.ds(i * SLOT, SLOT), :].rearrange("(k p) c -> p k c", p=P)
                             ).then_inc(ld_x[par], 16)

            def store(i, par):
                sp.wait_ge(y_done, i + 1)
                sp.dma_start(d["y"][bass.ds(i * SLOT, SLOT), :].rearrange("(k p) c -> p k c", p=P), y_out[:, par, :, :]
                             ).then_inc(st_y[par], 16)
            LAG = 4

            def both(t, par):
                if not isinstance(t, int) or t < NTILE:
                    load(t, par)
                if not isinstance(t, int) or t >= LAG:
                    store(t - LAG, (par - LAG) % 2)
            for t in range(FIRST):
                both(t, t % 2)
            run_steps(sp, FIRST, SHARED, both)
            sp.wait_ge(w_lo, 3 * (PIECES - EARLY))
            run_steps(sp, SHARED, NTILE, both)
            for t in range(NTILE, NTILE + LAG):
                both(t, t % 2)
            for k in range(2):
                sp.wait_ge(st_y[k], ((NTILE + 1 - k) // 2) * 16)

        @block.gpsimd
        def _(pool):
            pool.wait_ge(table_ready, 1)
            flat = pos[:, :, :].rearrange("p t k -> p (t k)")

            def load_rows(g, par):
                if past(g, 2):
                    pool.wait_ge(scattered[par], 4 * turns(g - 2, par))
                pool.dma_start(rows[:, 2 * par:2 * par + 2, :],
                               d["xs"][bass.ds(g * 2 * P, 2 * P), :].rearrange("(k p) c -> p k c", p=P)
                               ).then_inc(ld_row[par], 16)

            def scatter(g, par):
                nc.gpsimd.tensor_copy(idx[:, par, :], flat[:, bass.ds(g * 4, 4)]).then_inc(idx_done, 1)
                pool.wait_ge(idx_done, g + 1)
                wait_apart(pool, env["passed"], ld_row[par], turns(g, par))
                for k in range(4):
                    nc.gpsimd.indirect_dma_start(
                        out=d["xs"][:, :], out_offset=bass.IndirectOffsetOnAxis(ap=idx[:, par, k:k + 1], axis=0),
                        in_=rows[:, 2 * par + k // 2, :], in_offset=None).then_inc(scattered[par], 16)
            skewed(pool, NT // 2, 4, [(0, load_rows), (1, scatter)])

            for k in range(2):
                pool.wait_ge(scattered[k], NT * 16)
            for n in range(PIECES - EARLY):
                pool.wait_ge(ld_w, 16 * (n + 1))
                nc.gpsimd.tensor_scalar(stage[:, n, :], stage[:, n, :], XS, 1.0, ALU.mult, ALU.mult).then_inc(w_lo, 1)
                pool.wait_ge(w_lo, n * 3 + 1)
                nc.gpsimd.tensor_copy(W_all[:, EARLY + n, 0, :], stage[:, n, :]).then_inc(w_lo, 1)
                pool.wait_ge(w_lo, n * 3 + 2)
                nc.gpsimd.tensor_tensor(W_all[:, EARLY + n, 1, :], stage[:, n, :], W_all[:, EARLY + n, 0, :],
                                        ALU.subtract).then_inc(w_lo, 1)

        @block.tensor
        def _(pe):
            def count():
                pe.wait_ge(picked_ready, 1)
                nc.tensor.matmul(psR[:, 0:256], tri16[:, :], picked[:, :], start=True, stop=True)
                nc.tensor.matmul(psR[:, 256:512], one16[:, :], picked[:, :], start=True, stop=True).then_inc(counts_ready, 1)

            def transpose_x(i, par):
                pe.wait_ge(ld_x[par], turns(i, par))
                if past(i, 1):
                    pe.wait_ge(xT_done, i)
                for c in range(4):
                    for k in range(2):
                        last = nc.tensor.transpose(psX[:, (c * 2 + k) * P:(c * 2 + k + 1) * P],
                                                   x_in[:, par, k, c * P:(c + 1) * P], ident16[:, :])
                last.then_inc(xT_ready, 1)

            def up(i, par):
                e = expert(pe, i)
                pe.wait_ge(xT_done, i + 1)
                for u in range(NU):
                    if past(i, 1):
                        pe.wait_ge(relu_done, (i - 1) * FC + 2 * u + 2)
                    for k in range(2):
                        f = 2 * u + k
                        for m in range(DC):
                            for wh, xh in ((0, 0), (0, 1), (1, 0)):
                                last = nc.tensor.matmul(
                                    psH[u][:, k * SLOT:(k + 1) * SLOT],
                                    flatW[:, bass.ds(e * 4096 + ((m * 2 + wh) * 1024 + f * P), P)],
                                    xT[:, par, (xh * DC + m) * SLOT:(xh * DC + m + 1) * SLOT],
                                    start=m == 0 and wh == 0 and xh == 0, stop=m == DC - 1 and wh == 1)
                    last.then_inc(h_ready, 1)

            def down(i, par):
                e = expert(pe, i)
                pe.wait_ge(h_split, 2 * NU * (i + 1))
                if past(i, 2):
                    pe.wait_ge(y_done, i - 1)
                for r in range(2):
                    for f in range(FC):
                        for hh, wh in ((0, 0), (0, 1), (1, 0)):
                            piece = 2 * NE + f // 4
                            last = nc.tensor.matmul(
                                psY[par][:, r * D:(r + 1) * D],
                                h16[:, par, hh, f * SLOT + r * P:f * SLOT + (r + 1) * P],
                                flatW[:, bass.ds(e * 4096 + ((piece * 2 + wh) * 1024 + (f % 4) * D), D)],
                                start=f == 0 and hh == 0 and wh == 0, stop=f == FC - 1 and hh == 1)
                last.then_inc(y_ready, 1)
            expert_steps(pe, [(2, up), (1, transpose_x), (3, down)], {4: count})

        @block.scalar
        def _(act):
            act.wait_ge(b1_scaled, 1)

            def exp_difference():
                act.wait_ge(exp_ready, 1)
                nc.scalar.activation(V["e"][:, :], V["den"][:, :], ACT.Exp).then_inc(exp_ready, 1)

            def copy_x(i, par):
                act.wait_ge(xT_ready, i + 1)
                if past(i, 2):
                    act.wait_ge(h_ready, (i - 1) * NU)
                nc.scalar.activation(xT[:, par, :], psX[:, :], ACT.Copy).then_inc(xT_done, 1)

            def relu(i, par):
                e = expert(act, i)
                for u in range(NU):
                    act.wait_ge(h_ready, i * NU + u + 1)
                    if u >= 2:
                        act.wait_ge(h_split, (i * NU + u - 1) * 2)
                    elif past(i, 1):
                        act.wait_ge(h_split, (i * NU + u - 1) * 2)
                    for k in range(2):
                        nc.scalar.activation(h32[:, u % 2, k * SLOT:(k + 1) * SLOT], psH[u][:, k * SLOT:(k + 1) * SLOT],
                                             ACT.Relu, bias=b1[:, bass.ds(e * FC + 2 * u + k, 1)],
                                             scale=1.0 / XS).then_inc(relu_done, 1)
            expert_steps(act, [(2, relu), (1, copy_x)], {4: exp_difference})

        @block.vector
        def _(dve):
            steps = [0]

            def then(ins):
                steps[0] += 1
                ins.then_inc(route, 1)
                dve.wait_ge(route, steps[0])
            per_e = [P, NT, EXPERTS]
            iota = consts[:, C_IOTA:C_IOTA + EXPERTS].unsqueeze(1).to_broadcast(per_e)
            a, b_ = R["a"], R["b"]
            nc.vector.tensor_copy(tri16[:, :], consts[:, C_TRI:C_TRI + P])
            nc.vector.memset(one16[:, :], 1.0)
            dve.wait_ge(ld_b, 32)
            nc.vector.tensor_scalar(b1[:, :], b1[:, :], XS, None, ALU.mult).then_inc(b1_scaled, 1)

            def choose():
                for n, (lg, oh, v) in enumerate(((logits, R["oh1"], V["v1"]), (b_, R["oh2"], V["v2"]))):
                    then(nc.vector.tensor_reduce(v[:, :], lg[:, :, :], AX_X, ALU.max))
                    then(nc.vector.tensor_tensor(a[:, :, :], lg[:, :, :], v[:, :].unsqueeze(2).to_broadcast(per_e), ALU.is_equal))
                    then(nc.vector.scalar_tensor_tensor(out=a[:, :, :], in0=a[:, :, :], scalar=-float(EXPERTS), in1=iota,
                                                        op0=ALU.mult, op1=ALU.add))
                    then(nc.vector.tensor_reduce(V["i"][:, :], a[:, :, :], AX_X, ALU.min))
                    then(nc.vector.tensor_tensor(oh[:, :, :], a[:, :, :], V["i"][:, :].unsqueeze(2).to_broadcast(per_e),
                                                 ALU.is_equal))
                    if n == 0:
                        then(nc.vector.scalar_tensor_tensor(out=b_[:, :, :], in0=oh[:, :, :], scalar=-1e30, in1=lg[:, :, :],
                                                            op0=ALU.mult, op1=ALU.add))
                nc.vector.tensor_tensor(picked[:, :].rearrange("p (t e) -> p t e", e=EXPERTS), R["oh1"][:, :, :],
                                        R["oh2"][:, :, :], ALU.add).then_inc(picked_ready, 1)
                nc.vector.tensor_tensor(V["den"][:, :], V["v2"][:, :], V["v1"][:, :], ALU.subtract).then_inc(exp_ready, 1)

            def place():
                dve.wait_ge(exp_ready, 2)
                then(nc.vector.tensor_scalar(V["den"][:, :], V["e"][:, :], 1.0, None, ALU.add))
                then(nc.vector.reciprocal(wts[:, :, 0], V["den"][:, :]))
                then(nc.vector.tensor_tensor(wts[:, :, 1], V["e"][:, :], wts[:, :, 0], ALU.mult))
                dve.wait_ge(counts_ready, 1)
                then(nc.vector.tensor_copy(TE["tot"][:, :, :], psR[:, 256:512].rearrange("p (t e) -> p e t", e=EXPERTS)))
                then(nc.vector.tensor_tensor_scan(TE["inc"][:, :, :].rearrange("p e t -> p (e t)"),
                                                  consts[:, C_RESET:C_RESET + EXPERTS * NT],
                                                  TE["tot"][:, :, :].rearrange("p e t -> p (e t)"), 0.0, ALU.mult, ALU.add))
                then(nc.vector.tensor_scalar(E8["n"][:, :], TE["inc"][:, :, NT - 1], 1.0 / SLOT, 0.5 - 0.5 / SLOT,
                                             ALU.mult, ALU.add))
                then(nc.vector.tensor_scalar(E8["n"][:, :], E8["n"][:, :], MAGIC, None, ALU.add))
                then(nc.vector.tensor_scalar(E8["pad"][:, :], E8["n"][:, :], MAGIC, float(SLOT), ALU.subtract, ALU.mult))
                then(nc.vector.tensor_tensor_scan(E8["end"][:, :], consts[:, C_ONE:C_ONE + EXPERTS], E8["pad"][:, :], 0.0,
                                                  ALU.mult, ALU.add))
                then(nc.vector.tensor_tensor(E8["base"][:, :], E8["end"][:, :], E8["pad"][:, :], ALU.subtract))
                then(nc.vector.tensor_tensor(TE["inc"][:, :, :], TE["inc"][:, :, :], TE["tot"][:, :, :], ALU.subtract))
                then(nc.vector.tensor_tensor(TE["inc"][:, :, :], TE["inc"][:, :, :],
                                             E8["base"][:, :].unsqueeze(2).to_broadcast([P, EXPERTS, NT]), ALU.add))
                then(nc.vector.tensor_tensor(a[:, :, :], psR[:, 0:256].rearrange("p (t e) -> p t e", e=EXPERTS),
                                             TE["inc"][:, :, :].rearrange("p e t -> p t e"), ALU.add))
                for k, oh in enumerate((R["oh1"], R["oh2"])):
                    then(nc.vector.tensor_tensor(b_[:, :, :], a[:, :, :], oh[:, :, :], ALU.mult))
                    then(nc.vector.tensor_reduce(posf[:, :, k], b_[:, :, :], AX_X, ALU.add))
                then(nc.vector.tensor_scalar(pos[:, :, :], posf[:, :, :], float(T), None, ALU.add))
                end = E8["end"][0:1, :].unsqueeze(1).to_broadcast([1, ROUTED, EXPERTS])
                thr = consts[0:1, C_THR:C_THR + ROUTED].unsqueeze(2).to_broadcast([1, ROUTED, EXPERTS])
                then(nc.vector.tensor_tensor(cmp_[:, :, :], end, thr, ALU.is_le))
                then(nc.vector.tensor_reduce(cnt[:, :], cmp_[:, :, :], AX_X, ALU.add))
                nc.vector.memset(table[:, 0:SHARED], 0)
                nc.vector.tensor_scalar(table[:, SHARED:NTILE], cnt[:, :], float(EXPERTS - 1), 1.0, ALU.min,
                                        ALU.add).then_inc(table_ready, 1)
            def split(i, par):
                if past(i, 2):
                    dve.wait_ge(y_ready, i - 1)
                for u in range(NU):
                    n = i * NU + u
                    sl = slice(2 * u * SLOT, (2 * u + 2) * SLOT)
                    dve.wait_ge(relu_done, (n + 1) * 2)
                    nc.vector.tensor_copy(h16[:, par, 0, sl], h32[:, u % 2, :]).then_inc(h_split, 1)
                    dve.wait_ge(h_split, n * 2 + 1)
                    nc.vector.tensor_tensor(h16[:, par, 1, sl], h32[:, u % 2, :], h16[:, par, 0, sl],
                                            ALU.subtract).then_inc(h_split, 1)

            def output(i, par):
                e = expert(dve, i)
                dve.wait_ge(y_ready, i + 1)
                if past(i, 2):
                    dve.wait_ge(st_y[par], turns(i - 2, par))
                for r in range(2):
                    last = nc.vector.scalar_tensor_tensor(out=y_out[:, par, r, :], in0=psY[par][:, r * D:(r + 1) * D],
                                                          scalar=UNSCALE, in1=b2[:, bass.ds(e * D, D)],
                                                          op0=ALU.mult, op1=ALU.add)
                last.then_inc(y_done, 1)
            expert_steps(dve, [(2, split), (3, output)], {3: choose, 5: place})


def quantised_ffn(nc, d, consts, ident16, env):
    xall, xn4, mx = env["xall"], env["xn4"], env["mx"]
    GT = 4
    GW = GT * P
    NG = NT // GT
    with ExitStack() as ctx:
        def sb(name, shape, dt=F32):
            return ctx.enter_context(nc.sbuf_tensor(f"f_{name}", shape, dt))

        def pb(name, shape, dt=F32):
            return ctx.enter_context(nc.psum_tensor(f"f_{name}", shape, dt))

        def sem(name):
            return ctx.enter_context(nc.semaphore(f"f_{name}"))
        hT = sb("hT", [P, IC, T])
        wgu = sb("wgu", [P, 2, DC, INTER], BF16)
        wdT = sb("wdT", [P, IC, D], BF16)
        srow = sb("srow", [P, 2, IC])
        sinv = sb("sinv", [P, 3, IC])
        dsc = sb("dsc", [P, DC])
        dscb = sb("dscb", [P, DC, P])
        drow = sb("drow", [P, D])
        clip = sb("clip", [P, 2])
        cs = sb("cs", [P, 12])
        maxh = sb("maxh", [P, 2, NG])
        silu_t = sb("silu_t", [P, 2, GW])
        psX = pb("psX", [P, DC * GW], BF16)
        psB = [pb(f"psB{k}", [P, 512]) for k in range(6)]
        loaded, chain = sem("loaded"), sem("chain")
        q_ready, qT_ready, qT_done = sem("q_ready"), sem("qT_ready"), sem("qT_done")
        max_ready, all_max, sig_ready, row_ready = (sem(n) for n in ("max_ready", "all_max", "sig_ready", "row_ready"))

        with ExitStack() as c2:
            wraw = c2.enter_context(nc.sbuf_tensor("f_wraw", [P, 2, IC, D], F32))
            wdraw = c2.enter_context(nc.sbuf_tensor("f_wdraw", [P, DC, INTER], F32))
            wq = c2.enter_context(nc.sbuf_tensor("f_wq", [P, 2, IC, D], BF16))
            wdq = c2.enter_context(nc.sbuf_tensor("f_wdq", [P, DC, INTER], BF16))
            block = c2.enter_context(nc.Block())
            items = [(0, c) for c in range(IC)] + [(1, c) for c in range(IC)] + [(2, m) for m in range(DC)]

            def height(c):
                return TAIL if c == IC - 1 else P
            jobs = [("gu", g, c) for g in range(2) for c in range(IC)] + [("d", 0, c) for c in range(IC)]

            @block.sync
            def _(sp):
                for g in range(2):
                    sp.dma_start(wraw[:, g, 0:IC - 1, :], d["wgu"][g][0:(IC - 1) * P, :].rearrange("(c p) h -> p c h", p=P)
                                 ).then_inc(loaded, 16)
                    sp.dma_start(wraw[0:TAIL, g, IC - 1, :], d["wgu"][g][(IC - 1) * P:INTER, :]).then_inc(loaded, 16)
                sp.dma_start(wdraw[:, :, :], d["wd"].rearrange("(m p) i -> p m i", p=P)).then_inc(loaded, 16)
                sp.dma_start(clip[:, :], d["clip"]).then_inc(loaded, 16)

            @block.vector
            def _(dve):
                n = [0]

                def then(ins):
                    n[0] += 1
                    ins.then_inc(chain, 1)
                    dve.wait_ge(chain, n[0])
                dve.wait_ge(loaded, 96)
                then(nc.vector.tensor_reduce(cs[:, 0:1], mx[:, :], AX_X, ALU.max))
                nc.vector.tensor_copy(cs[:, 11:12], cs[:, 0:1]).then_inc(max_ready, 1)
                for g in range(2):
                    then(nc.vector.tensor_reduce(srow[:, g, 0:IC - 1], wraw[:, g, 0:IC - 1, :], AX_X, ALU.max,
                                                 apply_absolute_value=True))
                    then(nc.vector.tensor_reduce(srow[0:TAIL, g, IC - 1:IC], wraw[0:TAIL, g, IC - 1, :], AX_X, ALU.max,
                                                 apply_absolute_value=True))
                then(nc.vector.tensor_reduce(dsc[:, :], wdraw[:, :, :], AX_X, ALU.max, apply_absolute_value=True))
                for g in range(2):
                    then(nc.vector.tensor_scalar(srow[:, g, 0:IC - 1], srow[:, g, 0:IC - 1], 1.0 / 127.0, None, ALU.mult))
                    then(nc.vector.tensor_scalar(srow[0:TAIL, g, IC - 1:IC], srow[0:TAIL, g, IC - 1:IC], 1.0 / 127.0, None,
                                                 ALU.mult))
                then(nc.vector.tensor_scalar(dsc[:, :], dsc[:, :], 1.0 / 127.0, None, ALU.mult))
                then(nc.vector.reciprocal(sinv[:, 0:2, 0:IC - 1], srow[:, 0:2, 0:IC - 1]))
                then(nc.vector.reciprocal(sinv[0:TAIL, 0:2, IC - 1], srow[0:TAIL, 0:2, IC - 1]))
                then(nc.vector.reciprocal(sinv[:, 2, 0:DC], dsc[:, :]))
                nc.vector.tensor_copy(dscb[:, :, :], dsc[:, :].unsqueeze(2).to_broadcast([P, DC, P])).then_inc(row_ready, 1)
                for w, c in items:
                    if w < 2:
                        hgt = height(c)
                        src, dst, sc = wraw[0:hgt, w, c, :], wq[0:hgt, w, c, :], sinv[0:hgt, w, c:c + 1]
                    else:
                        src, dst, sc = wdraw[:, c, :], wdq[:, c, :], sinv[:, 2, c:c + 1]
                    then(nc.vector.tensor_scalar(src, src, sc, MAGIC, ALU.mult, ALU.add))
                    nc.vector.tensor_scalar(dst, src, MAGIC, 127.0, ALU.subtract, ALU.min).then_inc(q_ready, 1)
                dve.wait_ge(row_ready, 2)
                nc.vector.tensor_copy(drow[:, :], psB[1][:, 0:D]).then_inc(row_ready, 1)
                dve.wait_ge(sig_ready, 1)
                then(nc.vector.tensor_scalar(cs[:, 4:6], cs[:, 2:4], 1.0, None, ALU.add))
                then(nc.vector.reciprocal(cs[:, 6:8], cs[:, 4:6]))
                dve.wait_ge(all_max, 1)
                then(nc.vector.tensor_scalar(cs[:, 8:9], cs[:, 6:7], cs[:, 1:2], None, ALU.mult))
                then(nc.vector.tensor_scalar(cs[:, 8:9], cs[:, 8:9], 1.0 / 127.0, None, ALU.mult))
                then(nc.vector.reciprocal(cs[:, 5:6], cs[:, 8:9]))
                for g in range(2):
                    then(nc.vector.tensor_scalar(srow[:, g, 0:IC - 1], srow[:, g, 0:IC - 1], cs[:, 8:9], None, ALU.mult))
                    then(nc.vector.tensor_scalar(srow[0:TAIL, g, IC - 1:IC], srow[0:TAIL, g, IC - 1:IC],
                                                 cs[0:TAIL, 8:9], None, ALU.mult))

            @block.gpsimd
            def _(pool):
                pool.wait_ge(max_ready, 1)
                nc.gpsimd.partition_all_reduce(cs[:, 1:2], cs[:, 11:12], P, RMAX).then_inc(all_max, 1)

            @block.tensor
            def _(pe):
                pe.wait_ge(row_ready, 1)
                for m in range(DC):
                    last = nc.tensor.matmul(psB[1][:, m * P:(m + 1) * P], dscb[:, m, :], consts[:, C_ID:C_ID + P],
                                            start=True, stop=True)
                last.then_inc(row_ready, 1)
                for n, (kind, g, c) in enumerate(jobs):
                    pe.wait_ge(q_ready, g * IC + c + 1 if kind == "gu" else len(items))
                    if n >= 1:
                        pe.wait_ge(qT_done, n)
                    hgt = height(c)
                    for m in range(DC):
                        if kind == "gu":
                            last = nc.tensor.transpose(psX[:, m * P:m * P + hgt], wq[0:hgt, g, c, m * P:(m + 1) * P],
                                                       env["ident_bf"][0:hgt, 0:hgt])
                        else:
                            last = nc.tensor.transpose(psX[0:hgt, m * P:(m + 1) * P], wdq[:, m, c * P:c * P + hgt],
                                                       env["ident_bf"][:, :])
                    last.then_inc(qT_ready, 1)

            @block.scalar
            def _(act):
                act.wait_ge(loaded, 96)
                nc.scalar.activation(cs[:, 2:4], clip[:, :], ACT.Exp, scale=-1.0).then_inc(sig_ready, 1)
                for n, (kind, g, c) in enumerate(jobs):
                    act.wait_ge(qT_ready, n + 1)
                    hgt = height(c)
                    if kind == "gu":
                        nc.scalar.activation(wgu[:, g, :, c * P:c * P + hgt],
                                             psX[:, 0:2 * P].rearrange("p (m i) -> p m i", m=DC)[:, :, 0:hgt],
                                             ACT.Copy).then_inc(qT_done, 1)
                    else:
                        nc.scalar.activation(wdT[0:hgt, c, :], psX[0:hgt, 0:D], ACT.Copy).then_inc(qT_done, 1)

        with ExitStack() as c2:
            q16 = c2.enter_context(nc.sbuf_tensor("f_q16", [P, 2, GT * D], BF16))
            rounded = c2.enter_context(nc.sbuf_tensor("f_rounded", [P, 2, GT * D], F32))
            xqT = c2.enter_context(nc.sbuf_tensor("f_xqT", [P, 2, DC * GW], BF16))
            x_quant, x_sub, xq_ready, xq_done = (c2.enter_context(nc.semaphore("f_" + n)) for n in
                                                 ("x_quant", "x_sub", "xq_ready", "xq_done"))
            gu_ready, silu_done, h_done = (c2.enter_context(nc.semaphore("f_" + n)) for n in
                                           ("gu_ready", "silu_done", "h_done"))
            block = c2.enter_context(nc.Block())
            FIRST = 4

            def group(tensor, g):
                return tensor.rearrange("p t c -> p (t c)")[:, bass.ds(g * (GT * D), GT * D)]

            @block.vector
            def _(dve):
                def quantise(g, par):
                    v = group(xn4[:, :, :], g)
                    nc.vector.tensor_scalar(v, v, cs[:, 5:6], 127.0, ALU.mult, ALU.min).then_inc(x_quant, 1)
                    dve.wait_ge(x_quant, g * 2 + 1)
                    if past(g, 2):
                        dve.wait_ge(x_sub, g - 1)
                    nc.vector.tensor_scalar(rounded[:, par, :], v, -128.0, MAGIC, ALU.max, ALU.add).then_inc(x_quant, 1)

                def gated(g, par):
                    flat = hT[:, :, :].rearrange("p c t -> p (c t)")
                    for c in range(IC):
                        n = g * IC + c
                        hgt = TAIL if c == IC - 1 else P
                        dve.wait_ge(silu_done, n + 1)
                        nc.vector.scalar_tensor_tensor(out=flat[0:hgt, bass.ds(g * GW + c * T, GW)],
                                                       in0=psB[(c % 3) * 2 + 1][0:hgt, :], scalar=srow[0:hgt, 1, c:c + 1],
                                                       in1=silu_t[0:hgt, c % 2, :], op0=ALU.mult,
                                                       op1=ALU.mult).then_inc(h_done, 1)
                    dve.wait_ge(h_done, (g + 1) * IC)
                    nc.vector.tensor_reduce(maxh[:, 0, bass.ds(g, 1)], hT[:, 0:IC - 1, bass.ds(g * GW, GW)], AX_XY, ALU.max,
                                            apply_absolute_value=True)
                    nc.vector.tensor_reduce(maxh[0:TAIL, 1, bass.ds(g, 1)], hT[0:TAIL, IC - 1, bass.ds(g * GW, GW)], AX_X,
                                            ALU.max, apply_absolute_value=True)
                nc.vector.memset(maxh[:, :, :], 0.0)
                skewed(dve, NG, FIRST, [(0, quantise), (2, gated)])

            @block.gpsimd
            def _(pool):
                def subtract(g, par):
                    if past(g, 2):
                        pool.wait_ge(xq_ready, g - 1)
                    wait_apart(pool, env["passed"], x_quant, (g + 1) * 2)
                    nc.gpsimd.tensor_scalar(q16[:, par, :], rounded[:, par, :], -MAGIC, 1.0,
                                            ALU.add, ALU.mult).then_inc(x_sub, 1)
                skewed(pool, NG, FIRST, [(0, subtract)])

            @block.tensor
            def _(pe):
                def transpose_q(g, par):
                    pe.wait_ge(x_sub, g + 1)
                    if past(g, 1):
                        pe.wait_ge(xq_done, g)
                    for m in range(DC):
                        for t in range(GT):
                            last = nc.tensor.transpose(psX[:, m * GW + t * P:m * GW + (t + 1) * P],
                                                       q16[:, par, t * D + m * P:t * D + (m + 1) * P],
                                                       env["ident_bf"][:, :])
                    last.then_inc(xq_ready, 1)

                def gate_up(g, par):
                    pe.wait_ge(xq_done, g + 1)
                    for c in range(IC):
                        n = g * IC + c
                        hgt = TAIL if c == IC - 1 else P
                        if c >= 3 or past(g, 1):
                            pe.wait_ge(h_done, n - 2)
                        for w in range(2):
                            for m in range(DC):
                                last = nc.tensor.matmul(psB[(c % 3) * 2 + w][0:hgt, :], wgu[:, w, m, c * P:c * P + hgt],
                                                        xqT[:, par, m * GW:(m + 1) * GW], start=m == 0, stop=m == DC - 1)
                        last.then_inc(gu_ready, 1)
                skewed(pe, NG, FIRST, [(1, transpose_q), (2, gate_up)])

            @block.scalar
            def _(act):
                def copy_q(g, par):
                    act.wait_ge(xq_ready, g + 1)
                    if past(g, 2):
                        act.wait_ge(gu_ready, (g - 1) * IC)
                    nc.scalar.activation(xqT[:, par, :], psX[:, :], ACT.Copy).then_inc(xq_done, 1)

                def silu(g, par):
                    for c in range(IC):
                        n = g * IC + c
                        hgt = TAIL if c == IC - 1 else P
                        act.wait_ge(gu_ready, n + 1)
                        if c >= 2 or past(g, 1):
                            act.wait_ge(h_done, n - 1)
                        nc.scalar.activation(silu_t[0:hgt, c % 2, :], psB[(c % 3) * 2][0:hgt, :], ACT.Silu,
                                             scale=srow[0:hgt, 0, c:c + 1]).then_inc(silu_done, 1)
                skewed(act, NG, FIRST, [(2, silu), (1, copy_q)])

        with ExitStack() as c2:
            hq = c2.enter_context(nc.sbuf_tensor("f_hq", [P, 2, IC, GW], BF16))
            final = c2.enter_context(nc.sbuf_tensor("f_final", [P, 2, GT * D], F32))
            orow = c2.enter_context(nc.sbuf_tensor("f_orow", [P, D], F32))
            negmagic = c2.enter_context(nc.sbuf_tensor("f_negmagic", [P, 1], F32))
            sc, all_h, h_quant, hq_done, o_ready, o_scaled, o_added = (c2.enter_context(nc.semaphore("f_" + n)) for n in (
                "sc", "all_h", "h_quant", "hq_done", "o_ready", "o_scaled", "o_added"))
            st_o = [c2.enter_context(nc.semaphore(f"f_st_o{k}")) for k in range(2)]
            block = c2.enter_context(nc.Block())
            FIRST = 6

            @block.sync
            def _(sp):
                def store(g, par):
                    sp.wait_ge(o_added, g + 1)
                    sp.dma_start(d["out"][bass.ds(g * GW, GW), :].rearrange("(t p) c -> p t c", p=P),
                                 final[:, par, :].rearrange("p (t c) -> p t c", t=GT)).then_inc(st_o[par], 16)
                skewed(sp, NG, FIRST, [(0, store)])
                for k in range(2):
                    sp.wait_ge(st_o[k], NG * 8)

            @block.gpsimd
            def _(pool):
                pool.wait_ge(sc, 1)
                nc.gpsimd.partition_all_reduce(cs[:, 10:11], cs[:, 9:10], P, RMAX).then_inc(all_h, 1)

                def add(g, par):
                    pool.wait_ge(o_scaled, (g + 1) * 2)
                    nc.gpsimd.tensor_tensor(final[:, par, :], final[:, par, :], group(xall[:, :, :], g),
                                            ALU.add).then_inc(o_added, 1)
                skewed(pool, NG, FIRST, [(2, add)])

            @block.vector
            def _(dve):
                nc.vector.memset(negmagic[:, :], -MAGIC)
                nc.vector.tensor_reduce(cs[:, 9:10], maxh[:, :, :], AX_XY, ALU.max).then_inc(sc, 1)
                dve.wait_ge(all_h, 1)
                nc.vector.tensor_scalar(cs[:, 11:12], cs[:, 7:8], cs[:, 10:11], None, ALU.mult).then_inc(sc, 1)
                dve.wait_ge(sc, 2)
                nc.vector.tensor_scalar(cs[:, 9:10], cs[:, 11:12], 1.0 / 127.0, None, ALU.mult).then_inc(sc, 1)
                dve.wait_ge(sc, 3)
                nc.vector.reciprocal(cs[:, 4:5], cs[:, 9:10])
                nc.vector.tensor_scalar(orow[:, :], drow[:, :], cs[:, 9:10], None, ALU.mult).then_inc(sc, 1)

                def quantise(g, par):
                    wide, tail = hT[:, 0:IC - 1, bass.ds(g * GW, GW)], hT[0:TAIL, IC - 1, bass.ds(g * GW, GW)]
                    nc.vector.tensor_scalar(wide, wide, cs[:, 4:5], 127.0, ALU.mult, ALU.min).then_inc(h_quant, 1)
                    nc.vector.tensor_scalar(tail, tail, cs[0:TAIL, 4:5], 127.0, ALU.mult, ALU.min).then_inc(h_quant, 1)
                    dve.wait_ge(h_quant, g * 4 + 2)
                    nc.vector.tensor_scalar(wide, wide, -128.0, MAGIC, ALU.max, ALU.add).then_inc(h_quant, 1)
                    nc.vector.tensor_scalar(tail, tail, -128.0, MAGIC, ALU.max, ALU.add).then_inc(h_quant, 1)

                def scale_out(g, par):
                    if past(g, 2):
                        dve.wait_ge(st_o[par], turns(g - 2, par))
                    for k in range(2):
                        dve.wait_ge(o_ready, g * 2 + k + 1)
                        nc.vector.tensor_tensor(final[:, par, k * 512:(k + 1) * 512].rearrange("p (t c) -> p t c", t=2),
                                                psB[par * 2 + k][:, :].rearrange("p (t c) -> p t c", t=2),
                                                orow[:, :].unsqueeze(1).to_broadcast([P, 2, D]),
                                                ALU.mult).then_inc(o_scaled, 1)
                dve.wait_ge(sc, 4)
                skewed(dve, NG, FIRST, [(0, quantise), (2, scale_out)])

            @block.scalar
            def _(act):
                act.wait_ge(sc, 1)

                def subtract(g, par):
                    act.wait_ge(h_quant, (g + 1) * 4)
                    if past(g, 2):
                        act.wait_ge(o_ready, (g - 1) * 2)
                    nc.scalar.activation(hq[:, par, 0:IC - 1, :], hT[:, 0:IC - 1, bass.ds(g * GW, GW)], ACT.Identity,
                                         bias=negmagic[:, :])
                    nc.scalar.activation(hq[0:TAIL, par, IC - 1, :], hT[0:TAIL, IC - 1, bass.ds(g * GW, GW)], ACT.Identity,
                                         bias=negmagic[0:TAIL, :]).then_inc(hq_done, 1)
                skewed(act, NG, FIRST, [(0, subtract)])

            @block.tensor
            def _(pe):
                def down(g, par):
                    pe.wait_ge(hq_done, g + 1)
                    if past(g, 2):
                        pe.wait_ge(o_scaled, (g - 1) * 2)
                    for t in range(GT):
                        for c in range(IC):
                            hgt = TAIL if c == IC - 1 else P
                            last = nc.tensor.matmul(psB[par * 2 + t // 2][:, (t % 2) * D:(t % 2 + 1) * D],
                                                    hq[0:hgt, par, c, t * P:(t + 1) * P], wdT[0:hgt, c, :],
                                                    start=c == 0, stop=c == IC - 1)
                        if t % 2:
                            last.then_inc(o_ready, 1)
                skewed(pe, NG, FIRST, [(1, down)])


def build(nc, d):
    outer = ExitStack()
    with outer:
        def sb(stack, name, shape, dt=F32):
            return stack.enter_context(nc.sbuf_tensor(name, shape, dt))
        consts = sb(outer, "consts_sb", [P, C_END])
        ident16 = sb(outer, "ident16", [P, P], F16)
        ident_bf = sb(outer, "ident_bf", [P, P], BF16)
        ones16 = sb(outer, "ones16", [P, P], F16)
        env = {"ident_bf": ident_bf, "passed": outer.enter_context(nc.semaphore("passed"))}
        env["pos"] = sb(outer, "pos", [P, NT, 2], I32)
        env["wts"] = sb(outer, "wts", [P, NT, 2])
        with ExitStack() as moe:
            env["logits"] = sb(moe, "logits", [P, NT, EXPERTS])
            env["zero16"] = sb(moe, "zero16", [P, 2 * D], F16)
            env["wg16"] = sb(moe, "wg16", [P, DC, 2, EXPERTS], F16)
            W_all = env["W_all"] = sb(moe, "W_all", [P, PIECES, 2, 1024], F16)
            l = LAYERS[0]
            U = W_all[:, EARLY:PIECES, :, :].rearrange("p n h c -> p (n h c)")[:, 0:B * l.nu * 2 * D]
            room = W_all[:, 0:4, :, :].rearrange("p n h c -> p (n h c)").bitcast(F32)
            with ExitStack() as a0:
                G = sb(a0, "G0", [P, B * DC * 2 * l.cols], F16)
                Brow = sb(a0, "Brow0", [P, B * l.cols], F16)
                prepare_attention(nc, 0, d, consts, G[:, :], U, Brow[:, :], env["wg16"], room)
                with nc.semaphore("consts_made") as made, nc.Block() as block:
                    @block.vector
                    def _(dve):
                        nc.vector.tensor_copy(ident16[:, :], consts[:, C_ID:C_ID + P]).then_inc(made, 1)
                        nc.vector.tensor_copy(ident_bf[:, :], consts[:, C_ID:C_ID + P]).then_inc(made, 1)
                        nc.vector.memset(ones16[:, :], XS).then_inc(made, 1)
                        nc.vector.memset(env["zero16"][:, :], 0.0).then_inc(made, 1)
                        dve.wait_ge(made, 4)
                attention(nc, 0, d, consts, ones16, ident16, G[:, :], U, Brow[:, :], env)
            experts(nc, d, consts, ident16, env)
        env["xall"] = sb(outer, "xall", [P, NT, D])
        env["xn4"] = sb(outer, "xn4", [P, NT, D])
        env["mx"] = sb(outer, "mx", [P, NT])
        l = LAYERS[1]
        with ExitStack() as a1:
            env["bo_row"] = sb(a1, "bo_row", [P, D])
            G = sb(a1, "G1", [P, B * DC * 2 * l.cols], F16)
            U = sb(a1, "U1", [P, B * l.nu * 2 * D], F16)
            Brow = sb(a1, "Brow1", [P, B * l.cols], F16)
            prepare_attention(nc, 1, d, consts, G[:, :], U[:, :], Brow[:, :], None, None)
            attention(nc, 1, d, consts, ones16, ident16, G[:, :], U[:, :], Brow[:, :], env)
        quantised_ffn(nc, d, consts, ident16, env)


def constants(np):
    c = np.zeros((P, C_END), np.float32)
    p = np.arange(P)
    c[:, C_ID:C_ID + P] = np.eye(P)
    c[:, C_TRI:C_TRI + P] = p[:, None] < p[None, :]
    c[0, C_SEL] = 1
    c[1, C_SEL + 1] = 1
    c[:, C_IOTA:C_IOTA + EXPERTS] = np.arange(EXPERTS)
    c[:, C_RESET:C_RESET + EXPERTS * NT] = np.tile(np.arange(NT) > 0, EXPERTS)
    c[:, C_THR:C_THR + ROUTED] = np.arange(ROUTED) * SLOT
    c[:, C_ONE:C_ONE + P] = 1
    c[:, C_POW] = -0.5
    return c


def head_mask(np, l):
    return ((np.arange(P) // l.dim)[:, None] == (np.arange(l.width) // KEYS)[None, :]).astype(np.float32)


def kernel(**inputs):
    import numpy as np
    import concourse.bacc as bacc
    from concourse.bass_utils import run_bass_kernel_spmd

    a = {k: np.asarray(v) for k, v in inputs.items()}

    def chunks(m):
        return np.ascontiguousarray(m.reshape(-1, P, m.shape[-1]).transpose(1, 0, 2))

    def column(v):
        return v.reshape(-1, P).T
    h0 = LAYERS[0].feat
    arrays = {
        "consts": constants(np),
        "x0": a["x"].reshape(T, D),
        "ctxT": chunks(a["ctx_1024"].reshape(B * KEYS, D).T),
        "wg": chunks(a["L0_ffn_Wg"]),
        "wk0": chunks(a["L0_xattn_key_down"].transpose(1, 0, 2).reshape(D, h0)),
        "wv0": chunks(a["L0_xattn_value_down"].transpose(1, 0, 2).reshape(D, h0)),
        "wq0": chunks(a["L0_xattn_query_down"].transpose(0, 2, 1).reshape(h0, D)),
        "wo0": chunks(a["L0_xattn_value_up"].reshape(h0, D)),
        "bias0": np.stack([column(a["L0_xattn_query_down_bias"].reshape(-1)), np.zeros((P, 4), np.float32),
                           np.zeros((P, 4), np.float32)], 1),
        "wk1": chunks(a["L1_xattn_Wk"].T),
        "wv1": chunks(a["L1_xattn_Wv"].T),
        "wq1": chunks(a["L1_xattn_Wq"]),
        "wo1": chunks(a["L1_xattn_Wo"].T),
        "bias1": np.stack([column(a["L1_xattn_b" + n]) for n in "qkv"], 1),
        "bo": np.broadcast_to(a["L1_xattn_bo"][None], (P, D)),
        "wgate": a["L1_ffn_w_gate"], "wup": a["L1_ffn_w_up"], "wd": a["L1_ffn_w_down"],
        "clip": np.broadcast_to(np.concatenate([a["L1_ffn_clip_x"], a["L1_ffn_clip_down"]])[None], (P, 2)),
    }
    w1 = np.concatenate([a["L0_ffn_Ws1"][None], a["L0_ffn_W1"]])
    w2 = np.concatenate([a["L0_ffn_Ws2"][None], a["L0_ffn_W2"]])
    w2 = w2.reshape(NE, 2, 4, P, D).transpose(0, 1, 3, 2, 4)
    arrays["w"] = np.concatenate([w1.reshape(2 * NE * P, FF), w2.reshape(2 * NE * P, FF)])
    b1 = np.concatenate([a["L0_ffn_bs1"][None], a["L0_ffn_b1"]])
    arrays["b1"] = b1.reshape(NE * FC, P).T
    b2 = np.concatenate([a["L0_ffn_bs2"][None], a["L0_ffn_b2"]])
    arrays["b2"] = np.broadcast_to(b2.reshape(1, NE * D), (P, NE * D))

    for n, l in enumerate(LAYERS):
        arrays[f"mask{n}"] = head_mask(np, l)

    nc = bacc.Bacc("TRN2", target_bir_lowering=False, num_devices=1)
    arrays = {k: np.ascontiguousarray(v) for k, v in arrays.items()}
    d = {k: nc.dram_tensor(f"in_{k}", v.shape, mybir.dt.from_np(v.dtype), kind="ExternalInput").ap()
         for k, v in arrays.items()}
    for n in ("wk", "wv", "wq", "wo", "bias", "mask"):
        d[n] = [d[n + "0"], d[n + "1"]]
    d["wgu"] = [d["wgate"], d["wup"]]
    d["x1"] = nc.dram_tensor("x1_dram", (T, D), F32, kind="Internal").ap()
    d["xs"] = nc.dram_tensor("xs_dram", (ROWS, 2 * D), F16, kind="Internal").ap()
    d["y"] = nc.dram_tensor("y_dram", (ROWS, D), F32, kind="Internal").ap()
    d["out"] = nc.dram_tensor("out_dram", (T, D), F32, kind="ExternalOutput").ap()
    build(nc, d)
    r = run_bass_kernel_spmd(nc, [{f"in_{k}": v for k, v in arrays.items()}], core_ids=[0])
    return r.results[0]["out_dram"].reshape(B, S, D)
```

```python
import concourse.bass as bass
from concourse import mybir
from contextlib import ExitStack
import numpy as np

F32 = mybir.dt.float32
F16 = mybir.dt.float16
BF16 = mybir.dt.bfloat16
I32 = mybir.dt.int32
ALU = mybir.AluOpType
ACT = mybir.ActivationFunctionType
AX_X = mybir.AxisListType.X
AX_XY = mybir.AxisListType.XY

RMAX = bass.bass_isa.ReduceOp.max

P = 128
B, S, D = 4, 1024, 256
KEYS = 64
T = B * S
NT = T // P
TPB = S // P
DC = D // P
EXPERTS, FF = 8, 1024
NE = EXPERTS + 1
FC = FF // P
SLOT = 256
SHARED = T // SLOT
ROUTED = (2 * T + EXPERTS * (SLOT - 1)) // SLOT
NTILE = SHARED + ROUTED
ROWS = NTILE * SLOT
ZEROS, ZK = (ROWS - T) // NT, 3
PIECES = 4 * NE
EARLY = 32
INTER = 704
IC = (INTER + P - 1) // P
TAIL = INTER - (IC - 1) * P
MAGIC = 1.5 * 2.0 ** 23
EPS = 1e-5

XS = 64.0
PS = 1024.0
UNSCALE = 1.0 / (XS * XS)
UNSCALE_P = 1.0 / (XS * PS)


class Layer:
    def __init__(self, heads, dim, scale):
        self.heads, self.dim = heads, dim
        self.feat = heads * dim
        self.nc_ = self.feat // P
        self.hpc = P // dim
        self.width = self.hpc * KEYS
        self.cols = heads * KEYS
        self.banks = self.cols // 512
        self.nu = self.cols // P
        self.gscale = XS * scale


LAYERS = [Layer(8, 64, 1.0), Layer(16, 16, 0.25)]

C_ID, C_TRI = 0, P
C_IOTA = C_TRI + P
C_RESET = C_IOTA + EXPERTS
C_THR = C_RESET + EXPERTS * NT
C_ONE = C_THR + ROUTED
C_POW = C_ONE + P
C_END = C_POW + 1


def run_steps(eng, lo, hi, step):
    pairs = (hi - lo) // 2
    if pairs:
        with eng.Fori(0, pairs) as j:
            step(j * 2 + lo, lo % 2)
            step(j * 2 + (lo + 1), (lo + 1) % 2)
    if (hi - lo) % 2:
        step(hi - 1, (hi - 1) % 2)


def skewed(eng, n, first, stages):
    def step(t, parity):
        for lag, body in stages:
            if not isinstance(t, int) or 0 <= t - lag < n:
                body(t - lag, (parity - lag) % 2)
    for t in range(first):
        step(t, t % 2)
    run_steps(eng, first, n, step)
    for t in range(n, n + max(lag for lag, _ in stages)):
        step(t, t % 2)


def past(i, depth):
    return not isinstance(i, int) or i >= depth


def wait_apart(eng, passed, sem, value):
    eng.wait_ge(sem, value)
    eng.sem_inc(passed, 1)


def turns(i, par):
    return (i - par) * 8 + 16


def height(c):
    return TAIL if c == IC - 1 else P


def prepare_attention(nc, L, d, consts, G, U, Brow, wg16, room, ffn=None):
    l = LAYERS[L]
    C, W, NU = l.nc_, l.width, l.nu
    gsplit = l.banks
    units = [("g", m, c) for m in range(DC) for c in range(gsplit)]
    units += [("b", c, 0) for c in range(gsplit)]
    units += [("u", k, 0) for k in range(NU // 2)]
    row_unit = DC * gsplit
    RING = 5
    NUn = len(units)
    G = G.rearrange("p (b m h c) -> p b m h c", b=B, m=DC, h=2)
    U = U.rearrange("p (b u h c) -> p b u h c", b=B, u=NU, h=2)
    Brow = Brow.rearrange("p (b c) -> p b c", b=B)
    with ExitStack() as ctx:
        def sb(name, shape, dt=F32):
            return ctx.enter_context(nc.sbuf_tensor(f"p{L}_{name}", shape, dt))

        def sem(name):
            return ctx.enter_context(nc.semaphore(f"p{L}_{name}"))
        wk, wv, wq, wo = (room[:, n * DC * l.feat:(n + 1) * DC * l.feat] for n in range(4))
        wk, wv = (w.rearrange("p (m f) -> p m f", m=DC) for w in (wk, wv))
        wq, wo = (w.rearrange("p (c d) -> p c d", c=C) for w in (wq, wo))
        ctxT = sb("ctxT", [P, DC, B * KEYS])
        bias = sb("bias", [P, 3, C])
        bqb = sb("bqb", [P, C, P])
        kvT = sb("kvT", [P, 2, C, B * KEYS])
        bd = sb("bd", [P, 2, 2, C, W])
        bhi = sb("bhi", [P, 2, 512], F16)
        wg = sb("wg", [P, DC, EXPERTS])
        mask_sb = sb("mask", [P, W])
        ps_kv = [ctx.enter_context(nc.psum_tensor(f"p{L}_pskv{i}", [P, 512], F32)) for i in range(2)]
        ps = [ctx.enter_context(nc.psum_tensor(f"p{L}_ps{i}", [P, 512], F32)) for i in range(RING)]
        kv_loaded, loaded, kv_ready, kv_done = sem("kv_loaded"), sem("loaded"), sem("kv_ready"), sem("kv_done")
        bq_done, k_ready, v_ready, unit_ready = sem("bq_done"), sem("k_ready"), sem("v_ready"), sem("unit_ready")
        hi_done, lo_done = sem("hi_done"), sem("lo_done")
        wg_hi = sem("wg_hi")
        n_loads = 3 + (2 if L == 0 else 0)
        if ffn is not None:
            xn4 = ffn["xn4"][:, :, :].rearrange("p t c -> p (t c)")
            ends = [0]
            for size in (2 * IC * D, DC * INTER, IC * D, DC * INTER // 2):
                ends.append(ends[-1] + size)
            wraw, wdraw, wint, wdint = (xn4[:, lo:hi] for lo, hi in zip(ends, ends[1:]))
            wraw = wraw.rearrange("p (g c h) -> p g c h", g=2, c=IC)
            wdraw = wdraw.rearrange("p (m i) -> p m i", m=DC)
            wint = wint.bitcast(BF16).rearrange("p (g c h) -> p g c h", g=2, c=IC)
            wdint = wdint.bitcast(BF16).rearrange("p (m i) -> p m i", m=DC)
            sinv = sb("sinv", [P, 3, IC])
            dsc = sb("dsc", [P, DC])
            dscb = sb("dscb", [P, DC, P])
            clip = sb("clip", [P, 2])
            psW = ctx.enter_context(nc.psum_tensor("p1_psW", [P, 1024], BF16))
            wgu, wdT, srow, drow, cs, ident_bf = (ffn[n] for n in ("wgu", "wdT", "srow", "drow", "cs", "ident_bf"))
            w_loaded, w_chain, w_scaled, w_rounded, w_quant, w_turned, w_copied, sig_ready = (sem(n) for n in (
                "w_loaded", "w_chain", "w_scaled", "w_rounded", "w_quant", "w_turned", "w_copied", "sig_ready"))
            items = [(g, c) for g in range(2) for c in range(IC)] + [(2, m) for m in range(DC)]
            jobs = [("gu", g, c) for g in range(2) for c in range(IC)] + [("d", 0, c) for c in range(IC)] + [("row", 0, 0)]

            def item(w, c):
                if w == 2:
                    return wdraw[:, c, :], wdint[:, c, :], sinv[:, 2, c:c + 1]
                hgt = height(c)
                return wraw[0:hgt, w, c, :], wint[0:hgt, w, c, :], sinv[0:hgt, w, c:c + 1]

            def job_at(b, n):
                j = (b - B // 2) * NUn + n
                return j if 0 <= j < len(jobs) else None
            assert job_at(B - 1, NUn - 1) is None or NUn * (B // 2) >= len(jobs)
        block = ctx.enter_context(nc.Block())
        mask = mask_sb[:, :].rearrange("p (h k) -> p h k", k=KEYS)

        @block.sync
        def _(sp):
            sp.dma_start(wk, d["wk"][L]).then_inc(kv_loaded, 16)
            sp.dma_start(ctxT[:, :, :], d["ctxT"]).then_inc(kv_loaded, 16)
            sp.dma_start(wv, d["wv"][L]).then_inc(kv_loaded, 16)
            sp.dma_start(bias[:, :, :], d["bias"][L]).then_inc(kv_loaded, 16)
            if ffn is not None:
                for g in range(2):
                    sp.dma_start(wraw[:, g, 0:IC - 1, :], d["wgu"][g][0:(IC - 1) * P, :].rearrange("(c p) h -> p c h", p=P)
                                 ).then_inc(w_loaded, 16)
                    sp.dma_start(wraw[0:TAIL, g, IC - 1, :], d["wgu"][g][(IC - 1) * P:INTER, :]).then_inc(w_loaded, 16)
                sp.dma_start(wdraw[:, :, :], d["wd"].rearrange("(m p) i -> p m i", p=P)).then_inc(w_loaded, 16)
                sp.dma_start(clip[:, :], d["clip"]).then_inc(w_loaded, 16)

        @block.tensor
        def _(pe):
            pe.wait_ge(kv_loaded, 64)
            for c in range(C):
                if c >= 2:
                    pe.wait_ge(kv_done, 2 * (c - 1))
                for j, w in enumerate((wk, wv)):
                    for m in range(DC):
                        last = nc.tensor.matmul(ps_kv[c % 2][:, j * 256:(j + 1) * 256], w[:, m, c * P:(c + 1) * P],
                                                ctxT[:, m, :], start=m == 0, stop=m == DC - 1)
                last.then_inc(kv_ready, 1)
            pe.wait_ge(bq_done, 1)
            pe.wait_ge(loaded, 16 * n_loads)

            def turn(j):
                kind, g, c = jobs[j]
                if kind == "row":
                    pe.wait_ge(w_scaled, 4)
                    for m in range(DC):
                        last = nc.tensor.matmul(ps_kv[0][:, m * P:(m + 1) * P], dscb[:, m, :], consts[:, C_ID:C_ID + P],
                                                start=True, stop=True)
                    last.then_inc(w_turned, 1)
                    return
                pe.wait_ge(w_quant, g * IC + c + 1 if kind == "gu" else len(items))
                if j >= 1:
                    pe.wait_ge(w_copied, j)
                hgt = height(c)
                for m in range(DC):
                    if kind == "gu":
                        last = nc.tensor.transpose(psW[:, m * P:m * P + hgt], wint[0:hgt, g, c, m * P:(m + 1) * P],
                                                   ident_bf[0:hgt, 0:hgt])
                    else:
                        last = nc.tensor.transpose(psW[0:hgt, m * P:(m + 1) * P], wdint[:, m, c * P:c * P + hgt],
                                                   ident_bf[:, :])
                last.then_inc(w_turned, 1)
            for b in range(B):
                pe.wait_ge(k_ready, b + 1)
                for n, (kind, x, y) in enumerate(units):
                    at = b * NUn + n
                    bank = ps[at % RING]
                    if at >= RING:
                        pe.wait_ge(lo_done, at - RING + 1)
                    if kind == "u" and x == 0:
                        pe.wait_ge(v_ready, b + 1)
                    if kind == "g" and l.banks == 1:
                        for c in range(C):
                            last = nc.tensor.matmul(bank[:, c * W:(c + 1) * W], wq[:, c, x * P:(x + 1) * P],
                                                    bd[:, b % 2, 0, c, :], start=True, stop=True)
                    elif kind == "g":
                        last = nc.tensor.matmul(bank[:, :], wq[:, y, x * P:(x + 1) * P], bd[:, b % 2, 0, y, :],
                                                start=True, stop=True)
                    elif kind == "b":
                        for c in (range(C) if l.banks == 1 else (x,)):
                            o = c * W if l.banks == 1 else 0
                            last = nc.tensor.matmul(bank[:, o:o + W], bqb[:, c, :], bd[:, b % 2, 0, c, :],
                                                    start=True, stop=True)
                    else:
                        for k in range(2):
                            u = 2 * x + k
                            c, o = (u * P) // W, (u * P) % W
                            last = nc.tensor.matmul(bank[:, k * D:(k + 1) * D], bd[:, b % 2, 1, c, o:o + P], wo[:, c, :],
                                                    start=True, stop=True)
                    last.then_inc(unit_ready, 1)
                    if ffn is not None and job_at(b, n) is not None:
                        turn(job_at(b, n))

        @block.scalar
        def _(act):
            act.dma_start(mask_sb[:, :], d["mask"][L]).then_inc(loaded, 16)
            act.dma_start(wq, d["wq"][L]).then_inc(loaded, 16)
            act.dma_start(wo, d["wo"][L]).then_inc(loaded, 16)
            if L == 0:
                act.dma_start(wg[:, :, :], d["wg"]).then_inc(loaded, 16)
                act.dma_start(consts[:, :], d["consts"]).then_inc(loaded, 16)
                act.wait_ge(loaded, 16 * n_loads)
                nc.scalar.activation(wg16[:, :, 0, :], wg[:, :, :], ACT.Copy, scale=XS).then_inc(wg_hi, 1)
            for b in range(B):
                for n, (kind, x, y) in enumerate(units):
                    at = b * NUn + n
                    if ffn is not None and at == NUn:
                        act.wait_ge(w_loaded, 96)
                        nc.scalar.activation(cs[:, 2:4], clip[:, :], ACT.Exp, scale=-1.0).then_inc(sig_ready, 1)
                    act.wait_ge(unit_ready, at + 1)
                    bank = ps[at % RING]
                    if kind == "g":
                        nc.scalar.activation(G[:, b, x, 0, y * 512:(y + 1) * 512], bank[:, :], ACT.Copy,
                                             scale=l.gscale).then_inc(hi_done, 1)
                    elif kind == "b":
                        k = b * gsplit + x
                        if k >= 2:
                            act.wait_ge(lo_done, (k - 2) // gsplit * NUn + row_unit + (k - 2) % gsplit + 1)
                        nc.scalar.activation(Brow[0:P // 2, b, x * 512:(x + 1) * 512], bank[0:P // 2, :], ACT.Copy,
                                             scale=l.gscale)
                        nc.scalar.activation(bhi[P // 2:P, k % 2, :], bank[P // 2:P, :], ACT.Copy,
                                             scale=l.gscale).then_inc(hi_done, 1)
                    else:
                        nc.scalar.activation(U[:, b, 2 * x:2 * x + 2, 0, :], bank[:, :].rearrange("p (k d) -> p k d", d=D),
                                             ACT.Copy, scale=XS).then_inc(hi_done, 1)
                    if ffn is None or job_at(b, n) is None:
                        continue
                    j = job_at(b, n)
                    kind, g, c = jobs[j]
                    hgt = height(c)
                    act.wait_ge(w_turned, j + 1)
                    if kind == "row":
                        nc.scalar.activation(drow[:, :], ps_kv[0][:, 0:D], ACT.Copy).then_inc(w_copied, 1)
                    elif kind == "gu":
                        nc.scalar.activation(wgu[:, g, :, c * P:c * P + hgt],
                                             psW[:, 0:2 * P].rearrange("p (m i) -> p m i", m=DC)[:, :, 0:hgt],
                                             ACT.Copy).then_inc(w_copied, 1)
                    else:
                        nc.scalar.activation(wdT[0:hgt, c, :], psW[0:hgt, 0:D], ACT.Copy).then_inc(w_copied, 1)

        @block.gpsimd
        def _(pool):
            pool.wait_ge(loaded, 16 * n_loads)
            pool.wait_ge(kv_done, 2 * C)

            def round_weights():
                pool.wait_ge(w_scaled, 4)
                for w, c in items:
                    src, _, inverse = item(w, c)
                    nc.gpsimd.tensor_scalar(src, src, inverse, MAGIC, ALU.mult, ALU.add).then_inc(w_rounded, 1)
            for b in range(B):
                if ffn is not None and b == 2:
                    round_weights()
                if b >= 2:
                    pool.wait_ge(unit_ready, (b - 1) * NUn)
                for c in range(C):
                    src = kvT[:, 1, c, b * KEYS:(b + 1) * KEYS].unsqueeze(1).to_broadcast([P, l.hpc, KEYS])
                    last = nc.gpsimd.tensor_tensor(bd[:, b % 2, 1, c, :].rearrange("p (h k) -> p h k", k=KEYS),
                                                   src, mask, ALU.mult)
                last.then_inc(v_ready, 1)

        @block.vector
        def _(dve):
            dve.wait_ge(kv_loaded, 64)
            for c in range(C):
                dve.wait_ge(kv_ready, c + 1)
                for j in range(2):
                    nc.vector.tensor_scalar(kvT[:, j, c, :], ps_kv[c % 2][:, j * 256:(j + 1) * 256],
                                            bias[:, 1 + j, c:c + 1], None, ALU.add).then_inc(kv_done, 1)
            nc.vector.tensor_copy(bqb[:, :, :], bias[:, 0, :].unsqueeze(2).to_broadcast([P, C, P])).then_inc(bq_done, 1)
            if L == 0:
                dve.wait_ge(wg_hi, 1)
                nc.vector.scalar_tensor_tensor(out=wg16[:, :, 1, :], in0=wg[:, :, :], scalar=XS, in1=wg16[:, :, 0, :],
                                               op0=ALU.mult, op1=ALU.subtract).then_inc(wg_hi, 1)
            dve.wait_ge(kv_done, 2 * C)
            dve.wait_ge(loaded, 16 * n_loads)

            def weight_scales():
                dve.wait_ge(w_loaded, 96)
                for g in range(2):
                    nc.vector.tensor_reduce(srow[:, g, 0:IC - 1], wraw[:, g, 0:IC - 1, :], AX_X, ALU.max,
                                            apply_absolute_value=True).then_inc(w_chain, 1)
                    nc.vector.tensor_reduce(srow[0:TAIL, g, IC - 1:IC], wraw[0:TAIL, g, IC - 1, :], AX_X, ALU.max,
                                            apply_absolute_value=True).then_inc(w_chain, 1)
                nc.vector.tensor_reduce(dsc[:, :], wdraw[:, :, :], AX_X, ALU.max, apply_absolute_value=True
                                        ).then_inc(w_chain, 1)
                dve.wait_ge(w_chain, 5)
                wide, tail = srow[:, :, 0:IC - 1], srow[0:TAIL, :, IC - 1]
                for v in (wide, tail, dsc[:, :]):
                    nc.vector.tensor_scalar(v, v, 1.0 / 127.0, None, ALU.mult).then_inc(w_chain, 1)
                dve.wait_ge(w_chain, 8)
                nc.vector.reciprocal(sinv[:, 0:2, 0:IC - 1], wide).then_inc(w_scaled, 1)
                nc.vector.reciprocal(sinv[0:TAIL, 0:2, IC - 1], tail).then_inc(w_scaled, 1)
                nc.vector.reciprocal(sinv[:, 2, 0:DC], dsc[:, :]).then_inc(w_scaled, 1)
                nc.vector.tensor_copy(dscb[:, :, :], dsc[:, :].unsqueeze(2).to_broadcast([P, DC, P])).then_inc(w_scaled, 1)

            def weight_integers():
                for n, (w, c) in enumerate(items):
                    src, dst, _ = item(w, c)
                    dve.wait_ge(w_rounded, n + 1)
                    nc.vector.tensor_scalar(dst, src, MAGIC, 127.0, ALU.subtract, ALU.min).then_inc(w_quant, 1)
                dve.wait_ge(sig_ready, 1)
                nc.vector.tensor_scalar(cs[:, 4:6], cs[:, 2:4], 1.0, None, ALU.add).then_inc(sig_ready, 1)
                dve.wait_ge(sig_ready, 2)
                nc.vector.reciprocal(cs[:, 6:8], cs[:, 4:6])

            def diagonal_k(b):
                if b >= 2:
                    dve.wait_ge(unit_ready, (b - 1) * NUn)
                for c in range(C):
                    src = kvT[:, 0, c, b * KEYS:(b + 1) * KEYS].unsqueeze(1).to_broadcast([P, l.hpc, KEYS])
                    last = nc.vector.tensor_tensor(bd[:, b % 2, 0, c, :].rearrange("p (h k) -> p h k", k=KEYS),
                                                   src, mask, ALU.mult)
                last.then_inc(k_ready, 1)
            diagonal_k(0)
            for b in range(B):
                if b + 1 < B:
                    diagonal_k(b + 1)
                if ffn is not None and b == 0:
                    weight_scales()
                if ffn is not None and b == 2:
                    weight_integers()
                for n, (kind, x, y) in enumerate(units):
                    at = b * NUn + n
                    dve.wait_ge(hi_done, at + 1)
                    bank = ps[at % RING]
                    if kind == "g":
                        nc.vector.scalar_tensor_tensor(out=G[:, b, x, 1, y * 512:(y + 1) * 512], in0=bank[:, :],
                                                       scalar=l.gscale, in1=G[:, b, x, 0, y * 512:(y + 1) * 512],
                                                       op0=ALU.mult, op1=ALU.subtract).then_inc(lo_done, 1)
                    elif kind == "b":
                        nc.vector.scalar_tensor_tensor(out=Brow[P // 2:P, b, x * 512:(x + 1) * 512],
                                                       in0=bank[P // 2:P, :], scalar=l.gscale,
                                                       in1=bhi[P // 2:P, (b * gsplit + x) % 2, :],
                                                       op0=ALU.mult, op1=ALU.subtract).then_inc(lo_done, 1)
                    else:
                        nc.vector.scalar_tensor_tensor(out=U[:, b, 2 * x:2 * x + 2, 1, :],
                                                       in0=bank[:, :].rearrange("p (k d) -> p k d", d=D), scalar=XS,
                                                       in1=U[:, b, 2 * x:2 * x + 2, 0, :],
                                                       op0=ALU.mult, op1=ALU.subtract).then_inc(lo_done, 1)


def attention(nc, L, d, consts, ones16, ident16, G, U, Brow, env):
    l = LAYERS[L]
    H, COLS, NU, BANKS = l.heads, l.cols, l.nu, l.banks
    first = L == 0
    with ExitStack() as ctx:
        def sb(name, shape, dt=F32):
            return ctx.enter_context(nc.sbuf_tensor(f"a{L}_{name}", shape, dt))

        def pb(name, shape, dt=F32):
            return ctx.enter_context(nc.psum_tensor(f"a{L}_{name}", shape, dt))

        def sem(name):
            return ctx.enter_context(nc.semaphore(f"a{L}_{name}"))

        stat = sb("stat", [P, 2, 6])
        mv = sb("mv", [P, 2, 2])
        rstd = sb("rstd", [P, 2, 1])
        stat2 = sb("stat2", [P, 2, 6])
        mv2 = sb("mv2", [P, 2, 2])
        rstd2 = sb("rstd2", [P, 2, 1])
        xn = sb("xn", [P, 2, D])
        xT = sb("xT", [P, 2, 2, D], F16)
        top = sb("top", [P, 2, H])
        ntop = sb("ntop", [P, 2, H])
        prob = sb("prob", [P, 2, COLS])
        total = sb("total", [P, 2, H])
        rtotal = sb("rtotal", [P, 2, H])
        pT = sb("pT", [P, 2, 2, COLS], F16)
        psT = pb("psT", [P, 512])
        ob = 2 if first else 1
        psO = [pb(f"psO{k}", [P, 512]) for k in range(ob)]
        psS = [pb(f"psS{k}", [P, COLS]) for k in range(2)]
        psP = pb("psP", [P, COLS])
        if first:
            x_in = sb("x_in", [P, 2, D])
            x_res = sb("x_res", [P, 2, D])
            x_out = sb("x_out", [P, 2, D])
            xe = sb("xe", [P, 2, COLS])
            added = sb("added", [P, 2, H])
            xn2 = sb("xn2", [P, 2, D])
            xs = sb("xs", [P, 2, 2, D], F16)
            x2T = sb("x2T", [P, 2, 2 * D], F16)
            stage = sb("stage", [P, 2, 1024])
            psX = pb("psX", [P, 4 * D], F16)
            psL = pb("psL", [P, 512])
            logits, W_all, zero16, wg16 = env["logits"], env["W_all"], env["zero16"], env["wg16"]
        else:
            y_sh = sb("y_sh", [P, 2, D])
            y_exp = sb("y_exp", [P, 2, 2, D])
            idx = sb("idx", [P, 2, 2], I32)
            acc = sb("acc", [P, 2, D])
            xall, xn4, mx = env["xall"], env["xn4"], env["mx"]
            pos, wts, bo_row = env["pos"], env["wts"], env["bo_row"]

        ld_x = [sem(f"ld_x{k}") for k in range(2)]
        LNK = 4 if first else 6
        SUMK = 4 if first else 1
        OUTK = 5 if first else 6
        ln_done = sem("ln_done")
        rstd_in, rstd_out = sem("rstd_in"), sem("rstd_out")
        xT_ready, x_hi, x_lo = sem("xT_ready"), sem("x_hi"), sem("x_lo")
        scores_ready, top_done = sem("scores_ready"), sem("top_done")
        exp_done, sum_done, prob_done = sem("exp_done"), sem("sum_done"), sem("prob_done")
        pT_ready, p_hi, p_lo = sem("pT_ready"), sem("p_hi"), sem("p_lo")
        pv_ready, out_done = sem("pv_ready"), sem("out_done")
        if first:
            ld_res = [sem(f"ld_res{k}") for k in range(2)]
            ld_w = [sem(f"ld_w{k}") for k in range(2)]
            st_x = [sem(f"st_x{k}") for k in range(2)]
            st_s = [sem(f"st_s{k}") for k in range(2)]
            st_zero = sem("st_zero")
            n_hi, n_lo = sem("n_hi"), sem("n_lo")
            nT_ready, nT_done, logit_ready, logit_done = sem("nT_ready"), sem("nT_done"), sem("logit_ready"), sem("logit_done")
            w_hi, w_lo = sem("w_hi"), sem("w_lo")
        else:
            ld_y = [sem(f"ld_y{k}") for k in range(2)]
            ld_e = [sem(f"ld_e{k}") for k in range(2)]
            ld_bo = sem("ld_bo")
            idx_done, shared_added, bo_added = sem("idx_done"), sem("shared_added"), sem("bo_added")

        block = ctx.enter_context(nc.Block())
        FIRST = 12
        A = 0 if first else 2

        def batch(i):
            return i // TPB

        def seg(tensor, flat, i, count, size):
            v = tensor[:, :, :].rearrange("p t c -> p (t c)")
            return v[:, bass.ds(i * count + flat, size)]

        @block.sync
        def _(sp):
            if first:
                assert ZEROS * NT == ROWS - T and ZEROS // ZK * ZK == ZEROS
            else:
                sp.dma_start(bo_row[:, :], d["bo"]).then_inc(ld_bo, 16)

            def load(i, par):
                rows = d["x0" if first else "x1"][bass.ds(i * P, P), :]
                if past(i, 2):
                    sp.wait_ge(ln_done, (i - 2) * LNK + (LNK if first else 2))
                if first:
                    sp.dma_start(x_in[:, par, :], rows).then_inc(ld_x[par], 16)
                else:
                    sp.dma_start(seg(xall, 0, i, D, D), rows).then_inc(ld_x[par], 16)
                    sp.dma_start(y_sh[:, par, :], d["y"][bass.ds(i * P, P), :]).then_inc(ld_y[par], 16)

            def load_res(i, par):
                if past(i, 2):
                    sp.wait_ge(out_done, (i - 2) * OUTK + 1)
                sp.dma_start(x_res[:, par, :], d["x0"][bass.ds(i * P, P), :]).then_inc(ld_res[par], 16)

            def load_piece(i, par):
                if past(i, 2):
                    sp.wait_ge(w_lo, i - 1)
                sp.dma_start(stage[:, par, :], d["w"][bass.ds(i * P, P), :]).then_inc(ld_w[par], 16)

            def clear(i, par):
                sp.dma_start(d["xs"][bass.ds(i * ZEROS + T, ZEROS), :].rearrange("(j p) c -> p j c", j=ZK),
                             zero16[0:ZEROS // ZK, :].unsqueeze(1).to_broadcast([ZEROS // ZK, ZK, 2 * D])
                             ).then_inc(st_zero, 16)

            def store_x(i, par):
                sp.wait_ge(out_done, i * OUTK + 1)
                sp.dma_start(d["x1"][bass.ds(i * P, P), :], x_out[:, par, :]).then_inc(st_x[par], 16)

            def store_n(i, par):
                sp.wait_ge(n_lo, i + 1)
                sp.dma_start(d["xs"][bass.ds(i * P, P), :], xs[:, par, :, :].rearrange("p h c -> p (h c)")).then_inc(st_s[par], 16)

            if first:
                skewed(sp, NT, FIRST, [(0, load), (5, load_res), (0, load_piece), (0, clear), (7, store_x), (8, store_n)])
                for k in range(2):
                    sp.wait_ge(st_x[k], NT * 8)
                    sp.wait_ge(st_s[k], NT * 8)
                sp.wait_ge(st_zero, NT * 16)
            else:
                skewed(sp, NT, FIRST, [(0, load)])

        @block.tensor
        def _(pe):
            def transpose_x(i, par):
                pe.wait_ge(ln_done, (i + 1) * LNK)
                if past(i, 1):
                    pe.wait_ge(x_lo, i)
                for m in range(DC):
                    last = nc.tensor.transpose(psT[:, m * P:(m + 1) * P], xn[:, par, m * P:(m + 1) * P],
                                               consts[:, C_ID:C_ID + P])
                last.then_inc(xT_ready, 1)

            def scores(i, par):
                b = batch(i)
                pe.wait_ge(x_lo, i + 1)
                if past(i, 2):
                    if first:
                        pe.wait_ge(sum_done, (i - 2) * SUMK + 1)
                    else:
                        pe.wait_ge(exp_done, i - 1)
                for h in range(BANKS):
                    out = psS[par][:, h * 512:(h + 1) * 512]
                    nc.tensor.matmul(out, ones16[:, :], Brow[:, bass.ds(b * COLS + h * 512, 512)], start=True, stop=False)
                    for m in range(DC):
                        for xh, gh in ((0, 0), (0, 1), (1, 0)):
                            off = ((b * DC + m) * 2 + gh) * COLS + h * 512
                            last = nc.tensor.matmul(out, xT[:, par, xh, m * P:(m + 1) * P], G[:, bass.ds(off, 512)],
                                                    start=False, stop=m == DC - 1 and xh == 1)
                last.then_inc(scores_ready, 1)

            def transpose_p(i, par):
                pe.wait_ge(prob_done, i + 1)
                if past(i, 1):
                    pe.wait_ge(p_lo, i)
                src = xe if first else prob
                for u in range(NU):
                    last = nc.tensor.transpose(psP[:, u * P:(u + 1) * P], src[:, par, u * P:(u + 1) * P],
                                               consts[:, C_ID:C_ID + P])
                last.then_inc(pT_ready, 1)

            def values(i, par):
                b = batch(i)
                pe.wait_ge(p_lo, i + 1)
                if past(i, ob):
                    pe.wait_ge(out_done, (i - ob) * OUTK + 1)
                for u in range(NU):
                    for ph, uh in ((0, 0), (0, 1), (1, 0)):
                        off = ((b * NU + u) * 2 + uh) * D
                        last = nc.tensor.matmul(psO[par % ob][:, 0:D], pT[:, par, ph, u * P:(u + 1) * P], U[:, bass.ds(off, D)],
                                                start=u == 0 and ph == 0 and uh == 0, stop=u == NU - 1 and ph == 1)
                last.then_inc(pv_ready, 1)

            def transpose_n(i, par):
                pe.wait_ge(n_lo, i + 1)
                if past(i, 1):
                    pe.wait_ge(nT_done, i)
                for k in range(4):
                    last = nc.tensor.transpose(psX[:, k * P:(k + 1) * P],
                                               xs[:, par, k // 2, (k % 2) * P:(k % 2 + 1) * P], ident16[:, :])
                last.then_inc(nT_ready, 1)

            def router(i, par):
                pe.wait_ge(nT_done, i + 1)
                if past(i, 1):
                    pe.wait_ge(logit_done, i)
                k = 0
                for m in range(DC):
                    for xh in range(2):
                        for gh in range(2):
                            last = nc.tensor.matmul(psL[:, 0:EXPERTS], x2T[:, par, (xh * DC + m) * P:(xh * DC + m + 1) * P],
                                                    wg16[:, m, gh, :], start=k == 0, stop=k == 7)
                            k += 1
                last.then_inc(logit_ready, 1)

            stages = [(A + 2, scores), (A + 1, transpose_x), (A + 4, transpose_p), (A + 5, values)]
            if first:
                stages = [(9, router)] + stages + [(8, transpose_n)]
            skewed(pe, NT, FIRST, stages)

        @block.scalar
        def _(act):
            def exps(i, par):
                act.wait_ge(top_done, 2 * (i + 1))
                if past(i, 2):
                    if first:
                        act.wait_ge(sum_done, (i - 2) * SUMK + 1)
                    else:
                        act.wait_ge(pT_ready, i - 1)
                for h in range(H):
                    of = slice(h * KEYS, (h + 1) * KEYS)
                    last = nc.scalar.activation(prob[:, par, of], psS[par][:, of], ACT.Exp, bias=ntop[:, par, h:h + 1],
                                                scale=UNSCALE, accum_out=None if first else total[:, par, h:h + 1])
                last.then_inc(exp_done, 1)

            def x_high(i, par):
                act.wait_ge(xT_ready, i + 1)
                if past(i, 2):
                    act.wait_ge(scores_ready, i - 1)
                nc.scalar.activation(xT[:, par, 0, :], psT[:, 0:D], ACT.Copy, scale=XS).then_inc(x_hi, 1)

            def p_high(i, par):
                act.wait_ge(pT_ready, i + 1)
                if past(i, 2):
                    act.wait_ge(pv_ready, i - 1)
                nc.scalar.activation(pT[:, par, 0, :], psP[:, :], ACT.Copy, scale=PS).then_inc(p_hi, 1)

            def n_high(i, par):
                act.wait_ge(out_done, (i + 1) * OUTK)
                if past(i, 2):
                    act.wait_ge(nT_ready, i - 1)
                    act.wait_ge(st_s[par], turns(i - 2, par))
                nc.scalar.activation(xs[:, par, 0, :], xn2[:, par, :], ACT.Copy, scale=XS).then_inc(n_hi, 1)

            def copy_n(i, par):
                act.wait_ge(nT_ready, i + 1)
                if past(i, 2):
                    act.wait_ge(logit_ready, i - 1)
                nc.scalar.activation(x2T[:, par, :], psX[:, 0:2 * D], ACT.Copy).then_inc(nT_done, 1)

            def weight_scale(i, par):
                act.wait_ge(ld_w[par], turns(i, par))
                nc.scalar.activation(stage[:, par, :], stage[:, par, :], ACT.Copy, scale=XS).then_inc(w_hi, 1)

            def weight_high(i, par):
                flat = W_all[:, :, :, :].rearrange("p n h c -> p (n h c)")
                act.wait_ge(w_hi, i * 2 + 1)
                nc.scalar.activation(flat[:, bass.ds(i * 2048, 1024)], stage[:, par, :], ACT.Copy).then_inc(w_hi, 1)

            stages = [(A + 5, p_high), (A + 2, x_high), (A + 3, exps)]
            if first:
                stages += [(7, n_high), (0, weight_scale), (0, weight_high), (8, copy_n)]
            skewed(act, NT, FIRST, stages)

        @block.gpsimd
        def _(pool):
            def normalise(i, par):
                pool.wait_ge(sum_done, SUMK * (i + 1))
                t = xe if first else prob
                v = t[:, par, :].rearrange("p (h k) -> p h k", k=KEYS)
                nc.gpsimd.tensor_tensor(v, v, rtotal[:, par, :].unsqueeze(2).to_broadcast([P, H, KEYS]),
                                        ALU.mult).then_inc(prob_done, 1)

            def weight_low(i, par):
                flat = W_all[:, :, :, :].rearrange("p n h c -> p (n h c)")
                pool.wait_ge(w_hi, (i + 1) * 2)
                nc.gpsimd.tensor_tensor(flat[:, bass.ds(i * 2048 + 1024, 1024)], stage[:, par, :],
                                        flat[:, bass.ds(i * 2048, 1024)], ALU.subtract).then_inc(w_lo, 1)

            def gather(i, par):
                if past(i, 2):
                    pool.wait_ge(ln_done, (i - 2) * LNK + 2)
                    pool.wait_ge(ld_e[par], 2 * turns(i - 2, par))
                flat = pos[:, :, :].rearrange("p t k -> p (t k)")
                nc.gpsimd.tensor_copy(idx[:, par, :], flat[:, bass.ds(i * 2, 2)]).then_inc(idx_done, 1)
                wait_apart(pool, env["passed"], idx_done, i + 1)
                for k in range(2):
                    nc.gpsimd.indirect_dma_start(
                        out=y_exp[:, par, k, :], out_offset=None, in_=d["y"][:, :],
                        in_offset=bass.IndirectOffsetOnAxis(ap=idx[:, par, k:k + 1], axis=0)).then_inc(ld_e[par], 16)

            def add_shared(i, par):
                pool.wait_ge(ld_x[par], turns(i, par))
                pool.wait_ge(ld_y[par], turns(i, par))
                if past(i, 2):
                    pool.wait_ge(ln_done, (i - 2) * LNK + 2)
                nc.gpsimd.tensor_tensor(acc[:, par, :], seg(xall, 0, i, D, D), y_sh[:, par, :], ALU.add).then_inc(shared_added, 1)

            def add_bo(i, par):
                pool.wait_ge(ln_done, (i + 1) * LNK)
                v = seg(xall, 0, i, D, D)
                nc.gpsimd.tensor_tensor(v, v, bo_row[:, :], ALU.add).then_inc(bo_added, 1)

            def power(src, dst, chain, count, done):
                def body(i, par):
                    pool.wait_ge(chain, count(i))
                    nc.gpsimd.tensor_tensor(dst[:, par, :], src[:, par, 1:2], consts[:, C_POW:C_POW + 1],
                                            ALU.pow).then_inc(done, 1)
                return body
            power_in = power(mv, rstd, ln_done, lambda i: i * LNK + (LNK - 1), rstd_in)
            power_out = power(mv2, rstd2, out_done, lambda i: i * OUTK + 4, rstd_out)
            if first:
                skewed(pool, NT, FIRST, [(4, normalise), (1, weight_low), (6, power_out), (0, power_in)])
            else:
                pool.wait_ge(ld_bo, 16)
                skewed(pool, NT, FIRST, [(A + 4, normalise), (A + 1, add_bo), (1, add_shared), (0, gather), (A + 6, power_out), (A, power_in)])

        @block.vector
        def _(dve):
            def x_of(i, par):
                return x_in[:, par, :] if first else seg(xall, 0, i, D, D)

            def weigh_first(i, par):
                dve.wait_ge(shared_added, i + 1)
                dve.wait_ge(ld_e[par], 2 * turns(i, par))
                wf = wts[:, :, :].rearrange("p t k -> p (t k)")
                nc.vector.scalar_tensor_tensor(out=acc[:, par, :], in0=y_exp[:, par, 0, :], scalar=wf[:, bass.ds(i * 2, 1)],
                                               in1=acc[:, par, :], op0=ALU.mult, op1=ALU.add).then_inc(ln_done, 1)

            def weigh_second(i, par):
                wf = wts[:, :, :].rearrange("p t k -> p (t k)")
                dve.wait_ge(ln_done, i * LNK + 1)
                nc.vector.scalar_tensor_tensor(out=x_of(i, par), in0=y_exp[:, par, 1, :], scalar=wf[:, bass.ds(i * 2 + 1, 1)],
                                               in1=acc[:, par, :], op0=ALU.mult, op1=ALU.add).then_inc(ln_done, 1)

            def moments_in(i, par):
                if first:
                    wait_apart(dve, env["passed"], ld_x[par], turns(i, par))
                else:
                    wait_apart(dve, env["passed"], ln_done, i * LNK + 2)
                nc.vector.bn_stats(stat[:, par, :], x_of(i, par)).then_inc(ln_done, 1)

            def mean_in(i, par):
                wait_apart(dve, env["passed"], ln_done, i * LNK + LNK - 3)
                nc.vector.bn_aggr(mv[:, par, :], stat[:, par, :]).then_inc(ln_done, 1)

            def eps_in(i, par):
                dve.wait_ge(ln_done, i * LNK + LNK - 2)
                nc.vector.tensor_scalar(mv[:, par, 1:2], mv[:, par, 1:2], EPS, None, ALU.add).then_inc(ln_done, 1)

            def normalise_in(i, par):
                src = x_of(i, par)
                dve.wait_ge(rstd_in, i + 1)
                if past(i, 2):
                    dve.wait_ge(xT_ready, i - 1)
                nc.vector.tensor_scalar(xn[:, par, :], src, mv[:, par, 0:1], rstd[:, par, :], ALU.subtract,
                                        ALU.mult).then_inc(ln_done, 1)

            def x_low(i, par):
                dve.wait_ge(x_hi, i + 1)
                nc.vector.scalar_tensor_tensor(out=xT[:, par, 1, :], in0=psT[:, 0:D], scalar=XS, in1=xT[:, par, 0, :],
                                               op0=ALU.mult, op1=ALU.subtract).then_inc(x_lo, 1)

            def largest(i, par):
                dve.wait_ge(scores_ready, i + 1)
                s = psS[par][:, :].rearrange("p (h k) -> p h k", k=KEYS)
                nc.vector.tensor_reduce(top[:, par, :], s, AX_X, ALU.max).then_inc(top_done, 1)

            def negate(i, par):
                dve.wait_ge(top_done, i * 2 + 1)
                nc.vector.tensor_scalar(ntop[:, par, :], top[:, par, :], -UNSCALE, None, ALU.mult).then_inc(top_done, 1)

            def weighted(i, par):
                dve.wait_ge(exp_done, i + 1)
                if past(i, 2):
                    dve.wait_ge(pT_ready, i - 1)
                nc.vector.scalar_tensor_tensor(out=xe[:, par, :], in0=psS[par][:, :], scalar=UNSCALE, in1=prob[:, par, :],
                                               op0=ALU.mult, op1=ALU.mult).then_inc(sum_done, 1)

            def sums(i, par):
                dve.wait_ge(sum_done, i * SUMK + 1)
                nc.vector.tensor_reduce(total[:, par, :], xe[:, par, :].rearrange("p (h k) -> p h k", k=KEYS), AX_X,
                                        ALU.add, apply_absolute_value=True).then_inc(sum_done, 1)

            def plus_one(i, par):
                dve.wait_ge(sum_done, i * SUMK + 2)
                nc.vector.tensor_scalar(added[:, par, :], total[:, par, :], 1.0, None, ALU.add).then_inc(sum_done, 1)

            def invert(i, par):
                if first:
                    dve.wait_ge(sum_done, i * SUMK + SUMK - 1)
                else:
                    dve.wait_ge(exp_done, i + 1)
                nc.vector.reciprocal(rtotal[:, par, :], (added if first else total)[:, par, :]).then_inc(sum_done, 1)

            def p_low(i, par):
                dve.wait_ge(p_hi, i + 1)
                nc.vector.scalar_tensor_tensor(out=pT[:, par, 1, :], in0=psP[:, :], scalar=PS, in1=pT[:, par, 0, :],
                                               op0=ALU.mult, op1=ALU.subtract).then_inc(p_lo, 1)

            def output(i, par):
                dve.wait_ge(pv_ready, i + 1)
                base = i * OUTK
                if first:
                    dve.wait_ge(ld_res[par], turns(i, par))
                    if past(i, 2):
                        dve.wait_ge(st_x[par], turns(i - 2, par))
                    x, res = x_out[:, par, :], x_res[:, par, :]
                else:
                    dve.wait_ge(bo_added, i + 1)
                    x = res = seg(xall, 0, i, D, D)
                nc.vector.scalar_tensor_tensor(out=x, in0=psO[par % ob][:, 0:D], scalar=UNSCALE_P, in1=res,
                                               op0=ALU.mult, op1=ALU.add).then_inc(out_done, 1)

            def moments_out(i, par):
                wait_apart(dve, env["passed"], out_done, i * OUTK + 1)
                nc.vector.bn_stats(stat2[:, par, :], x_out[:, par, :] if first else seg(xall, 0, i, D, D)).then_inc(out_done, 1)

            def mean_out(i, par):
                wait_apart(dve, env["passed"], out_done, i * OUTK + 2)
                nc.vector.bn_aggr(mv2[:, par, :], stat2[:, par, :]).then_inc(out_done, 1)

            def eps_out(i, par):
                dve.wait_ge(out_done, i * OUTK + 3)
                nc.vector.tensor_scalar(mv2[:, par, 1:2], mv2[:, par, 1:2], EPS, None, ALU.add).then_inc(out_done, 1)

            def normalise_out(i, par):
                base = i * OUTK
                x, dst = (x_out[:, par, :], xn2[:, par, :]) if first else (seg(xall, 0, i, D, D), seg(xn4, 0, i, D, D))
                dve.wait_ge(rstd_out, i + 1)
                if first and past(i, 2):
                    dve.wait_ge(n_hi, i - 1)
                nc.vector.tensor_scalar(dst, x, mv2[:, par, 0:1], rstd2[:, par, :], ALU.subtract,
                                        ALU.mult).then_inc(out_done, 1)

            def magnitude(i, par):
                dve.wait_ge(out_done, i * OUTK + 5)
                dst = seg(xn4, 0, i, D, D)
                nc.vector.tensor_reduce(mx[:, bass.ds(i, 1)], dst, AX_X, ALU.max,
                                        apply_absolute_value=True).then_inc(out_done, 1)

            def n_low(i, par):
                dve.wait_ge(n_hi, i + 1)
                nc.vector.scalar_tensor_tensor(out=xs[:, par, 1, :], in0=xn2[:, par, :], scalar=XS, in1=xs[:, par, 0, :],
                                               op0=ALU.mult, op1=ALU.subtract).then_inc(n_lo, 1)

            def logit(i, par):
                dve.wait_ge(logit_ready, i + 1)
                nc.vector.tensor_scalar(seg(logits, 0, i, EXPERTS, EXPERTS), psL[:, 0:EXPERTS], UNSCALE, None,
                                        ALU.mult).then_inc(logit_done, 1)

            if first:
                stages = [(3, largest), (8, n_low), (3, negate), (2, x_low), (5, p_low), (7, normalise_out), (6, output),
                          (1, normalise_in), (3, weighted), (6, moments_out), (0, moments_in), (3, sums), (6, mean_out),
                          (0, mean_in), (3, plus_one), (6, eps_out), (0, eps_in), (3, invert), (9, logit)]
            else:
                stages = [(5, largest), (3, normalise_in), (5, negate), (2, weigh_first), (4, x_low), (2, weigh_second),
                          (7, p_low), (9, normalise_out), (2, moments_in), (9, magnitude), (8, output), (2, mean_in),
                          (8, moments_out), (2, eps_in), (8, mean_out), (5, invert), (8, eps_out)]
            skewed(dve, NT, FIRST, stages)


def experts(nc, d, consts, ident16, env):
    logits, W_all, pos, wts = env["logits"], env["W_all"], env["pos"], env["wts"]
    flatW = W_all[:, :, :, :].rearrange("p n h c -> p (n h c)")
    with ExitStack() as ctx:
        def sb(name, shape, dt=F32):
            return ctx.enter_context(nc.sbuf_tensor(f"e_{name}", shape, dt))

        def pb(name, shape, dt=F32):
            return ctx.enter_context(nc.psum_tensor(f"e_{name}", shape, dt))

        def sem(name):
            return ctx.enter_context(nc.semaphore(f"e_{name}"))
        b1 = sb("b1", [P, NE * FC])
        b2 = sb("b2", [P, NE * D])
        STAGES = 3
        stage = sb("stage", [P, STAGES, 1024])
        rows = sb("rows", [P, 4, 2 * D], F16)
        x_in = sb("x_in", [P, 2, 2, 2 * D], F16)
        xT = sb("xT", [P, 2, 4 * SLOT], F16)
        h32 = sb("h32", [P, 2, 2 * SLOT])
        h16 = sb("h16", [P, 2, 2, FC * SLOT], F16)
        y_out = sb("y_out", [P, 2, 2, D])
        table = sb("table", [1, NTILE], I32)
        idx = sb("idx", [P, 2, 4], I32)

        room = W_all[:, EARLY:PIECES, :, :].rearrange("p n h c -> p (n h c)")
        taken = [0]

        def sb(name, shape, dt=F32):
            halves = int(np.prod(shape[1:])) * (2 if dt == F32 else 1)
            v = room[0:shape[0], taken[0]:taken[0] + halves]
            taken[0] += halves
            v = v if dt == F16 else v.bitcast(dt)
            if len(shape) == 3:
                v = v.rearrange("p (a b) -> p a b", b=shape[2])
            return v
        R = {n: sb("r_" + n, [P, NT, EXPERTS]) for n in ("a", "b", "oh1", "oh2")}
        TE = {n: sb("t_" + n, [P, EXPERTS, NT]) for n in ("tot", "inc")}
        picked = sb("picked", [P, NT * EXPERTS], BF16)
        tri16 = sb("tri16", [P, P], BF16)
        one16 = sb("one16", [P, P], BF16)
        V = {n: sb("v_" + n, [P, NT]) for n in ("v1", "v2", "i", "e", "den")}
        E8 = {n: sb("e8_" + n, [P, EXPERTS]) for n in ("n", "pad", "end", "base")}
        posf = sb("posf", [P, NT, 2])
        cmp_ = sb("cmp", [1, ROUTED, EXPERTS])
        cnt = sb("cnt", [1, ROUTED])

        assert taken[0] <= STAGES * 2048

        def raw(n):
            return stage[:, n, :] if n < STAGES else W_all[:, EARLY + n, :, :].rearrange("p h c -> p (h c)").bitcast(F32)

        psX = pb("psX", [P, 8 * P], F16)
        psH = [pb(f"psH{k}", [P, 512]) for k in range(4)]
        psY = [pb(f"psY{k}", [P, 512]) for k in range(2)]
        psR = pb("psR", [P, 512])

        ld_b, ld_w, ld_row = sem("ld_b"), sem("ld_w"), [sem(f"ld_row{k}") for k in range(2)]
        ld_x = [sem(f"ld_x{k}") for k in range(2)]
        st_y = [sem(f"st_y{k}") for k in range(2)]
        scattered = [sem(f"scattered{k}") for k in range(2)]
        idx_done = sem("idx_done")
        route, picked_ready, counts_ready, exp_ready, table_ready = (sem(n) for n in (
            "route", "picked_ready", "counts_ready", "exp_ready", "table_ready"))
        w_hi, w_lo = sem("w_hi"), sem("w_lo")
        b1_scaled = sem("b1_scaled")
        xT_ready, xT_done = sem("xT_ready"), sem("xT_done")
        h_ready, relu_done, h_split = sem("h_ready"), sem("relu_done"), sem("h_split")
        y_ready, y_done = sem("y_ready"), sem("y_done")
        block = ctx.enter_context(nc.Block())
        FIRST = 10
        NU = FC // 2

        def expert_steps(eng, stages, extra):
            def step(t, parity):
                for lag, body in stages:
                    if not isinstance(t, int) or 0 <= t - lag < NTILE:
                        body(t - lag, (parity - lag) % 2)
            routed[0] = False
            for t in range(FIRST):
                if t in extra:
                    extra[t]()
                step(t, t % 2)
            run_steps(eng, FIRST, SHARED, step)
            eng.wait_ge(table_ready, 1)
            routed[0] = True
            run_steps(eng, SHARED, NTILE, step)
            for t in range(NTILE, NTILE + max(lag for lag, _ in stages)):
                step(t, t % 2)
        routed = [False]

        def expert(eng, i):
            if not routed[0]:
                return 0
            return eng.value_load(table[0:1, bass.ds(i, 1)], min_val=0, max_val=EXPERTS)

        @block.sync
        def _(sp):
            def load(i, par):
                if past(i, 2):
                    sp.wait_ge(xT_ready, i - 1)
                sp.dma_start(x_in[:, par, :, :], d["xs"][bass.ds(i * SLOT, SLOT), :].rearrange("(k p) c -> p k c", p=P)
                             ).then_inc(ld_x[par], 16)

            def store(i, par):
                sp.wait_ge(y_done, i + 1)
                sp.dma_start(d["y"][bass.ds(i * SLOT, SLOT), :].rearrange("(k p) c -> p k c", p=P), y_out[:, par, :, :]
                             ).then_inc(st_y[par], 16)
            LAG = 4

            def both(t, par):
                if not isinstance(t, int) or t < NTILE:
                    load(t, par)
                if not isinstance(t, int) or t >= LAG:
                    store(t - LAG, (par - LAG) % 2)
            for t in range(FIRST):
                both(t, t % 2)
            run_steps(sp, FIRST, SHARED, both)
            for k in range(2):
                sp.wait_ge(scattered[k], NT * 16)
            sp.wait_ge(w_lo, PIECES - EARLY)
            run_steps(sp, SHARED, NTILE, both)
            for t in range(NTILE, NTILE + LAG):
                both(t, t % 2)
            for k in range(2):
                sp.wait_ge(st_y[k], ((NTILE + 1 - k) // 2) * 16)

        @block.gpsimd
        def _(pool):
            pool.dma_start(b1[:, :], d["b1"]).then_inc(ld_b, 16)
            pool.dma_start(b2[:, :], d["b2"]).then_inc(ld_b, 16)
            for n in range(PIECES - EARLY):
                pool.dma_start(raw(n), d["w"][(EARLY + n) * P:(EARLY + n + 1) * P, :]).then_inc(ld_w, 16)
            pool.wait_ge(table_ready, 1)
            flat = pos[:, :, :].rearrange("p t k -> p (t k)")

            def load_rows(g, par):
                if past(g, 2):
                    pool.wait_ge(scattered[par], 4 * turns(g - 2, par))
                pool.dma_start(rows[:, 2 * par:2 * par + 2, :],
                               d["xs"][bass.ds(g * 2 * P, 2 * P), :].rearrange("(k p) c -> p k c", p=P)
                               ).then_inc(ld_row[par], 16)

            def scatter(g, par):
                nc.gpsimd.tensor_copy(idx[:, par, :], flat[:, bass.ds(g * 4, 4)]).then_inc(idx_done, 1)
                pool.wait_ge(idx_done, g + 1)
                wait_apart(pool, env["passed"], ld_row[par], turns(g, par))
                for k in range(4):
                    nc.gpsimd.indirect_dma_start(
                        out=d["xs"][:, :], out_offset=bass.IndirectOffsetOnAxis(ap=idx[:, par, k:k + 1], axis=0),
                        in_=rows[:, 2 * par + k // 2, :], in_offset=None).then_inc(scattered[par], 16)
            skewed(pool, NT // 2, 4, [(0, load_rows), (1, scatter)])

        @block.tensor
        def _(pe):
            def count():
                pe.wait_ge(picked_ready, 1)
                nc.tensor.matmul(psR[:, 0:256], tri16[:, :], picked[:, :], start=True, stop=True)
                nc.tensor.matmul(psR[:, 256:512], one16[:, :], picked[:, :], start=True, stop=True).then_inc(counts_ready, 1)

            def transpose_x(i, par):
                pe.wait_ge(ld_x[par], turns(i, par))
                if past(i, 1):
                    pe.wait_ge(xT_done, i)
                for c in range(4):
                    for k in range(2):
                        last = nc.tensor.transpose(psX[:, (c * 2 + k) * P:(c * 2 + k + 1) * P],
                                                   x_in[:, par, k, c * P:(c + 1) * P], ident16[:, :])
                last.then_inc(xT_ready, 1)

            def up(i, par):
                e = expert(pe, i)
                pe.wait_ge(xT_done, i + 1)
                for u in range(NU):
                    if past(i, 1):
                        pe.wait_ge(relu_done, (i - 1) * FC + 2 * u + 2)
                    for k in range(2):
                        f = 2 * u + k
                        for m in range(DC):
                            for wh, xh in ((0, 0), (0, 1), (1, 0)):
                                last = nc.tensor.matmul(
                                    psH[u][:, k * SLOT:(k + 1) * SLOT],
                                    flatW[:, bass.ds(e * 4096 + ((m * 2 + wh) * 1024 + f * P), P)],
                                    xT[:, par, (xh * DC + m) * SLOT:(xh * DC + m + 1) * SLOT],
                                    start=m == 0 and wh == 0 and xh == 0, stop=m == DC - 1 and wh == 1)
                    last.then_inc(h_ready, 1)

            def down(i, par):
                e = expert(pe, i)
                pe.wait_ge(h_split, 2 * NU * (i + 1))
                if past(i, 2):
                    pe.wait_ge(y_done, i - 1)
                for r in range(2):
                    for f in range(FC):
                        for hh, wh in ((0, 0), (0, 1), (1, 0)):
                            piece = 2 * NE + f // 4
                            last = nc.tensor.matmul(
                                psY[par][:, r * D:(r + 1) * D],
                                h16[:, par, hh, f * SLOT + r * P:f * SLOT + (r + 1) * P],
                                flatW[:, bass.ds(e * 4096 + ((piece * 2 + wh) * 1024 + (f % 4) * D), D)],
                                start=f == 0 and hh == 0 and wh == 0, stop=f == FC - 1 and hh == 1)
                last.then_inc(y_ready, 1)
            expert_steps(pe, [(2, up), (1, transpose_x), (3, down)], {4: count})

        @block.scalar
        def _(act):
            act.wait_ge(b1_scaled, 1)

            def exp_difference():
                act.wait_ge(exp_ready, 1)
                nc.scalar.activation(V["e"][:, :], V["den"][:, :], ACT.Exp).then_inc(exp_ready, 1)

            def copy_x(i, par):
                act.wait_ge(xT_ready, i + 1)
                if past(i, 2):
                    act.wait_ge(h_ready, (i - 1) * NU)
                nc.scalar.activation(xT[:, par, :], psX[:, :], ACT.Copy).then_inc(xT_done, 1)

            def relu(i, par):
                e = expert(act, i)
                for u in range(NU):
                    act.wait_ge(h_ready, i * NU + u + 1)
                    if u >= 2:
                        act.wait_ge(h_split, (i * NU + u - 1) * 2)
                    elif past(i, 1):
                        act.wait_ge(h_split, (i * NU + u - 1) * 2)
                    for k in range(2):
                        nc.scalar.activation(h32[:, u % 2, k * SLOT:(k + 1) * SLOT], psH[u][:, k * SLOT:(k + 1) * SLOT],
                                             ACT.Relu, bias=b1[:, bass.ds(e * FC + 2 * u + k, 1)],
                                             scale=1.0 / XS).then_inc(relu_done, 1)

            def last_high(n):
                def body():
                    act.wait_ge(ld_w, 16 * (PIECES - EARLY))
                    act.wait_ge(table_ready, 1)
                    if n >= STAGES:
                        act.wait_ge(w_lo, n - STAGES + 1)
                    nc.scalar.activation(stage[:, n % STAGES, :], raw(n), ACT.Copy, scale=XS).then_inc(w_hi, 1)
                    act.wait_ge(w_hi, n * 2 + 1)
                    nc.scalar.activation(W_all[:, EARLY + n, 0, :], stage[:, n % STAGES, :], ACT.Copy).then_inc(w_hi, 1)
                return body
            extra = {4: exp_difference}
            extra.update((6 + n, last_high(n)) for n in range(PIECES - EARLY))
            expert_steps(act, [(2, relu), (1, copy_x)], extra)

        @block.vector
        def _(dve):
            steps = [0]

            def then(ins):
                steps[0] += 1
                ins.then_inc(route, 1)
                dve.wait_ge(route, steps[0])
            per_e = [P, NT, EXPERTS]
            iota = consts[:, C_IOTA:C_IOTA + EXPERTS].unsqueeze(1).to_broadcast(per_e)
            a, b_ = R["a"], R["b"]
            nc.vector.tensor_copy(tri16[:, :], consts[:, C_TRI:C_TRI + P])
            nc.vector.memset(one16[:, :], 1.0)
            dve.wait_ge(ld_b, 32)
            nc.vector.tensor_scalar(b1[:, :], b1[:, :], XS, None, ALU.mult).then_inc(b1_scaled, 1)

            def choose():
                for n, (lg, oh, v) in enumerate(((logits, R["oh1"], V["v1"]), (b_, R["oh2"], V["v2"]))):
                    then(nc.vector.tensor_reduce(v[:, :], lg[:, :, :], AX_X, ALU.max))
                    then(nc.vector.tensor_tensor(a[:, :, :], lg[:, :, :], v[:, :].unsqueeze(2).to_broadcast(per_e), ALU.is_equal))
                    then(nc.vector.scalar_tensor_tensor(out=a[:, :, :], in0=a[:, :, :], scalar=-float(EXPERTS), in1=iota,
                                                        op0=ALU.mult, op1=ALU.add))
                    then(nc.vector.tensor_reduce(V["i"][:, :], a[:, :, :], AX_X, ALU.min))
                    then(nc.vector.tensor_tensor(oh[:, :, :], a[:, :, :], V["i"][:, :].unsqueeze(2).to_broadcast(per_e),
                                                 ALU.is_equal))
                    if n == 0:
                        then(nc.vector.scalar_tensor_tensor(out=b_[:, :, :], in0=oh[:, :, :], scalar=-1e30, in1=lg[:, :, :],
                                                            op0=ALU.mult, op1=ALU.add))
                nc.vector.tensor_tensor(picked[:, :].rearrange("p (t e) -> p t e", e=EXPERTS), R["oh1"][:, :, :],
                                        R["oh2"][:, :, :], ALU.add).then_inc(picked_ready, 1)
                nc.vector.tensor_tensor(V["den"][:, :], V["v2"][:, :], V["v1"][:, :], ALU.subtract).then_inc(exp_ready, 1)

            def place():
                dve.wait_ge(exp_ready, 2)
                then(nc.vector.tensor_scalar(V["den"][:, :], V["e"][:, :], 1.0, None, ALU.add))
                then(nc.vector.reciprocal(wts[:, :, 0], V["den"][:, :]))
                then(nc.vector.tensor_tensor(wts[:, :, 1], V["e"][:, :], wts[:, :, 0], ALU.mult))
                dve.wait_ge(counts_ready, 1)
                then(nc.vector.tensor_copy(TE["tot"][:, :, :], psR[:, 256:512].rearrange("p (t e) -> p e t", e=EXPERTS)))
                then(nc.vector.tensor_tensor_scan(TE["inc"][:, :, :].rearrange("p e t -> p (e t)"),
                                                  consts[:, C_RESET:C_RESET + EXPERTS * NT],
                                                  TE["tot"][:, :, :].rearrange("p e t -> p (e t)"), 0.0, ALU.mult, ALU.add))
                then(nc.vector.tensor_scalar(E8["n"][:, :], TE["inc"][:, :, NT - 1], 1.0 / SLOT, 0.5 - 0.5 / SLOT,
                                             ALU.mult, ALU.add))
                then(nc.vector.tensor_scalar(E8["n"][:, :], E8["n"][:, :], MAGIC, None, ALU.add))
                then(nc.vector.tensor_scalar(E8["pad"][:, :], E8["n"][:, :], MAGIC, float(SLOT), ALU.subtract, ALU.mult))
                then(nc.vector.tensor_tensor_scan(E8["end"][:, :], consts[:, C_ONE:C_ONE + EXPERTS], E8["pad"][:, :], 0.0,
                                                  ALU.mult, ALU.add))
                then(nc.vector.tensor_tensor(E8["base"][:, :], E8["end"][:, :], E8["pad"][:, :], ALU.subtract))
                then(nc.vector.tensor_tensor(TE["inc"][:, :, :], TE["inc"][:, :, :], TE["tot"][:, :, :], ALU.subtract))
                then(nc.vector.tensor_tensor(TE["inc"][:, :, :], TE["inc"][:, :, :],
                                             E8["base"][:, :].unsqueeze(2).to_broadcast([P, EXPERTS, NT]), ALU.add))
                then(nc.vector.tensor_tensor(a[:, :, :], psR[:, 0:256].rearrange("p (t e) -> p t e", e=EXPERTS),
                                             TE["inc"][:, :, :].rearrange("p e t -> p t e"), ALU.add))
                for k, oh in enumerate((R["oh1"], R["oh2"])):
                    then(nc.vector.tensor_tensor(b_[:, :, :], a[:, :, :], oh[:, :, :], ALU.mult))
                    then(nc.vector.tensor_reduce(posf[:, :, k], b_[:, :, :], AX_X, ALU.add))
                then(nc.vector.tensor_scalar(pos[:, :, :], posf[:, :, :], float(T), None, ALU.add))
                end = E8["end"][0:1, :].unsqueeze(1).to_broadcast([1, ROUTED, EXPERTS])
                thr = consts[0:1, C_THR:C_THR + ROUTED].unsqueeze(2).to_broadcast([1, ROUTED, EXPERTS])
                then(nc.vector.tensor_tensor(cmp_[:, :, :], end, thr, ALU.is_le))
                then(nc.vector.tensor_reduce(cnt[:, :], cmp_[:, :, :], AX_X, ALU.add))
                nc.vector.memset(table[:, 0:SHARED], 0)
                nc.vector.tensor_scalar(table[:, SHARED:NTILE], cnt[:, :], float(EXPERTS - 1), 1.0, ALU.min,
                                        ALU.add).then_inc(table_ready, 1)
            def split(i, par):
                if past(i, 2):
                    dve.wait_ge(y_ready, i - 1)
                for u in range(NU):
                    n = i * NU + u
                    sl = slice(2 * u * SLOT, (2 * u + 2) * SLOT)
                    dve.wait_ge(relu_done, (n + 1) * 2)
                    nc.vector.tensor_copy(h16[:, par, 0, sl], h32[:, u % 2, :]).then_inc(h_split, 1)
                    dve.wait_ge(h_split, n * 2 + 1)
                    nc.vector.tensor_tensor(h16[:, par, 1, sl], h32[:, u % 2, :], h16[:, par, 0, sl],
                                            ALU.subtract).then_inc(h_split, 1)

            def output(i, par):
                e = expert(dve, i)
                dve.wait_ge(y_ready, i + 1)
                if past(i, 2):
                    dve.wait_ge(st_y[par], turns(i - 2, par))
                for r in range(2):
                    last = nc.vector.scalar_tensor_tensor(out=y_out[:, par, r, :], in0=psY[par][:, r * D:(r + 1) * D],
                                                          scalar=UNSCALE, in1=b2[:, bass.ds(e * D, D)],
                                                          op0=ALU.mult, op1=ALU.add)
                last.then_inc(y_done, 1)
            def last_low(n):
                def body():
                    dve.wait_ge(w_hi, (n + 1) * 2)
                    nc.vector.tensor_tensor(W_all[:, EARLY + n, 1, :], stage[:, n % STAGES, :], W_all[:, EARLY + n, 0, :],
                                            ALU.subtract).then_inc(w_lo, 1)
                return body
            extra = {3: choose, 5: place}
            extra.update((6 + n, last_low(n)) for n in range(PIECES - EARLY))
            expert_steps(dve, [(2, split), (3, output)], extra)


def quantised_ffn(nc, d, consts, ident16, env):
    xall, xn4, mx = env["xall"], env["xn4"], env["mx"]
    GT = 4
    GW = GT * P
    NG = NT // GT
    with ExitStack() as ctx:
        def sb(name, shape, dt=F32):
            return ctx.enter_context(nc.sbuf_tensor(f"f_{name}", shape, dt))

        def pb(name, shape, dt=F32):
            return ctx.enter_context(nc.psum_tensor(f"f_{name}", shape, dt))

        def sem(name):
            return ctx.enter_context(nc.semaphore(f"f_{name}"))
        hT = sb("hT", [P, IC, T])
        wgu, wdT, srow, drow, cs = (env[n] for n in ("wgu", "wdT", "srow", "drow", "cs"))
        maxh = sb("maxh", [P, 2, NG])
        psX = pb("psX", [P, DC * GW], BF16)
        psB = [pb(f"psB{k}", [P, 512]) for k in range(6)]
        chain, max_ready, all_max = sem("chain"), sem("max_ready"), sem("all_max")

        with ExitStack() as c2:
            q16 = c2.enter_context(nc.sbuf_tensor("f_q16", [P, 2, GT * D], BF16))
            silu_t = c2.enter_context(nc.sbuf_tensor("f_silu_t", [P, 3, GW], F32))
            up_t = c2.enter_context(nc.sbuf_tensor("f_up_t", [P, 2, GW], F32))
            xqT = c2.enter_context(nc.sbuf_tensor("f_xqT", [P, 2, DC * GW], BF16))
            x_quant, x_sub, xq_ready, xq_done = (c2.enter_context(nc.semaphore("f_" + n)) for n in
                                                 ("x_quant", "x_sub", "xq_ready", "xq_done"))
            gu_ready, silu_done, up_done, h_direct, h_copied = (c2.enter_context(nc.semaphore("f_" + n)) for n in (
                "gu_ready", "silu_done", "up_done", "h_direct", "h_copied"))
            block = c2.enter_context(nc.Block())
            FIRST = 6

            assert IC % 3 == 0
            DIRECT, COPIED = IC // 3, IC - IC // 3

            def direct(g, c):
                return g * DIRECT + c // 3

            def copied(g, c):
                return g * COPIED + c - 1 - c // 3

            def h_of(g, c, hgt):
                return hT[:, :, :].rearrange("p c t -> p (c t)")[0:hgt, bass.ds(g * GW + c * T, GW)]

            def group(tensor, g):
                return tensor.rearrange("p t c -> p (t c)")[:, bass.ds(g * (GT * D), GT * D)]

            @block.vector
            def _(dve):
                nc.vector.tensor_reduce(cs[:, 0:1], mx[:, :], AX_X, ALU.max).then_inc(max_ready, 1)
                dve.wait_ge(all_max, 1)
                nc.vector.tensor_scalar(cs[:, 9:10], cs[:, 6:7], cs[:, 1:2], None, ALU.mult).then_inc(chain, 1)
                dve.wait_ge(chain, 1)
                nc.vector.tensor_scalar(cs[:, 8:9], cs[:, 9:10], 1.0 / 127.0, None, ALU.mult).then_inc(chain, 1)
                dve.wait_ge(chain, 2)
                nc.vector.reciprocal(cs[:, 5:6], cs[:, 8:9]).then_inc(chain, 1)
                for v, c in ((srow[:, :, 0:IC - 1], cs[:, 8:9]), (srow[0:TAIL, :, IC - 1], cs[0:TAIL, 8:9])):
                    nc.vector.tensor_scalar(v, v, c, None, ALU.mult).then_inc(chain, 1)
                dve.wait_ge(chain, 5)

                def quantise(g, par):
                    v = group(xn4[:, :, :], g)
                    nc.vector.tensor_scalar(v, v, cs[:, 5:6], 127.0, ALU.mult, ALU.min).then_inc(x_quant, 1)
                    dve.wait_ge(x_quant, g * 2 + 1)
                    nc.vector.tensor_scalar(v, v, -128.0, MAGIC, ALU.max, ALU.add).then_inc(x_quant, 1)

                def gated(g, chunks):
                    for c in chunks:
                        dve.wait_ge(silu_done, g * IC + c + 1)
                        nc.vector.scalar_tensor_tensor(out=h_of(g, c, P), in0=psB[(c % 3) * 2 + 1][:, :],
                                                       scalar=srow[:, 1, c:c + 1], in1=silu_t[:, c % 3, :],
                                                       op0=ALU.mult, op1=ALU.mult).then_inc(h_direct, 1)

                def largest(g, par):
                    dve.wait_ge(h_direct, (g + 1) * DIRECT)
                    dve.wait_ge(h_copied, (g + 1) * COPIED)
                    nc.vector.tensor_reduce(maxh[:, 0, bass.ds(g, 1)], hT[:, 0:IC - 1, bass.ds(g * GW, GW)], AX_XY, ALU.max,
                                            apply_absolute_value=True)
                    nc.vector.tensor_reduce(maxh[0:TAIL, 1, bass.ds(g, 1)], hT[0:TAIL, IC - 1, bass.ds(g * GW, GW)], AX_X,
                                            ALU.max, apply_absolute_value=True)
                nc.vector.memset(maxh[:, :, :], 0.0)
                skewed(dve, NG, FIRST, [(3, lambda g, par: gated(g, range(0, IC // 2, 3))), (0, quantise),
                                        (3, lambda g, par: gated(g, range(IC // 2, IC, 3))), (4, largest)])

            @block.gpsimd
            def _(pool):
                pool.wait_ge(max_ready, 1)
                nc.gpsimd.partition_all_reduce(cs[:, 1:2], cs[:, 0:1], P, RMAX).then_inc(all_max, 1)

                def subtract(g, par):
                    if past(g, 2):
                        pool.wait_ge(xq_ready, g - 1)
                    wait_apart(pool, env["passed"], x_quant, (g + 1) * 2)
                    nc.gpsimd.tensor_scalar(q16[:, par, :], group(xn4[:, :, :], g), -MAGIC, 1.0,
                                            ALU.add, ALU.mult).then_inc(x_sub, 1)

                def multiply(g, par):
                    for c in range(IC):
                        if c % 3:
                            hgt = TAIL if c == IC - 1 else P
                            n = copied(g, c)
                            pool.wait_ge(up_done, n + 1)
                            nc.gpsimd.tensor_tensor(h_of(g, c, hgt), silu_t[0:hgt, c % 3, :],
                                                    up_t[0:hgt, (c - 1 - c // 3) % 2, :], ALU.mult).then_inc(h_copied, 1)
                skewed(pool, NG, FIRST, [(1, subtract), (3, multiply)])

            @block.tensor
            def _(pe):
                def transpose_q(g, par):
                    pe.wait_ge(x_sub, g + 1)
                    if past(g, 1):
                        pe.wait_ge(xq_done, g)
                    for m in range(DC):
                        for t in range(GT):
                            last = nc.tensor.transpose(psX[:, m * GW + t * P:m * GW + (t + 1) * P],
                                                       q16[:, par, t * D + m * P:t * D + (m + 1) * P],
                                                       env["ident_bf"][:, :])
                    last.then_inc(xq_ready, 1)

                def gate_up(g, par):
                    pe.wait_ge(xq_done, g + 1)
                    for c in range(IC):
                        n = g * IC + c
                        hgt = TAIL if c == IC - 1 else P
                        if c >= 3 or past(g, 1):
                            if c % 3:
                                pe.wait_ge(up_done, copied(g, c) - 1)
                            else:
                                pe.wait_ge(h_direct, direct(g, c))
                        for w in range(2):
                            for m in range(DC):
                                last = nc.tensor.matmul(psB[(c % 3) * 2 + w][0:hgt, :], wgu[:, w, m, c * P:c * P + hgt],
                                                        xqT[:, par, m * GW:(m + 1) * GW], start=m == 0, stop=m == DC - 1)
                        last.then_inc(gu_ready, 1)
                skewed(pe, NG, FIRST, [(2, transpose_q), (3, gate_up)])

            @block.scalar
            def _(act):
                def copy_q(g, par):
                    act.wait_ge(xq_ready, g + 1)
                    if past(g, 2):
                        act.wait_ge(gu_ready, (g - 1) * IC)
                    nc.scalar.activation(xqT[:, par, :], psX[:, :], ACT.Copy).then_inc(xq_done, 1)

                def silu(g, par):
                    for c in range(IC):
                        n = g * IC + c
                        hgt = TAIL if c == IC - 1 else P
                        act.wait_ge(gu_ready, n + 1)
                        if c >= 3 or past(g, 1):
                            if c % 3:
                                act.wait_ge(h_copied, copied(g, c) - 1)
                            else:
                                act.wait_ge(h_direct, direct(g, c))
                        nc.scalar.activation(silu_t[0:hgt, c % 3, :], psB[(c % 3) * 2][0:hgt, :], ACT.Silu,
                                             scale=srow[0:hgt, 0, c:c + 1]).then_inc(silu_done, 1)
                        if c % 3:
                            nc.scalar.activation(up_t[0:hgt, (c - 1 - c // 3) % 2, :], psB[(c % 3) * 2 + 1][0:hgt, :],
                                                 ACT.Copy, scale=srow[0:hgt, 1, c:c + 1]).then_inc(up_done, 1)
                skewed(act, NG, FIRST, [(2, copy_q), (3, silu)])

        with ExitStack() as c2:
            hq = c2.enter_context(nc.sbuf_tensor("f_hq", [P, 2, IC, GW], BF16))
            final = c2.enter_context(nc.sbuf_tensor("f_final", [P, 2, GT * D], F32))
            orow = c2.enter_context(nc.sbuf_tensor("f_orow", [P, D], F32))
            negmagic = c2.enter_context(nc.sbuf_tensor("f_negmagic", [P, 1], F32))
            sc, all_h, h_quant, hq_done, o_ready, o_scaled, o_added = (c2.enter_context(nc.semaphore("f_" + n)) for n in (
                "sc", "all_h", "h_quant", "hq_done", "o_ready", "o_scaled", "o_added"))
            st_o = [c2.enter_context(nc.semaphore(f"f_st_o{k}")) for k in range(2)]
            h_round = c2.enter_context(nc.semaphore("f_h_round"))
            block = c2.enter_context(nc.Block())
            FIRST = 6

            def halves(g):
                return hT[:, 0:IC - 1, bass.ds(g * GW, GW)], hT[0:TAIL, IC - 1, bass.ds(g * GW, GW)]

            @block.sync
            def _(sp):
                def store(g, par):
                    sp.wait_ge(o_added, g + 1)
                    sp.dma_start(d["out"][bass.ds(g * GW, GW), :].rearrange("(t p) c -> p t c", p=P),
                                 final[:, par, :].rearrange("p (t c) -> p t c", t=GT)).then_inc(st_o[par], 16)
                skewed(sp, NG, FIRST, [(0, store)])
                for k in range(2):
                    sp.wait_ge(st_o[k], NG * 8)

            @block.gpsimd
            def _(pool):
                pool.wait_ge(sc, 1)
                nc.gpsimd.partition_all_reduce(cs[:, 10:11], cs[:, 9:10], P, RMAX).then_inc(all_h, 1)

                def add(g, par):
                    pool.wait_ge(o_scaled, (g + 1) * 2)
                    nc.gpsimd.tensor_tensor(final[:, par, :], final[:, par, :], group(xall[:, :, :], g),
                                            ALU.add).then_inc(o_added, 1)

                def round_h(g, par):
                    for k, v in enumerate(halves(g)):
                        nc.gpsimd.tensor_scalar(v, v, cs[0:TAIL if k else P, 4:5], MAGIC, ALU.mult, ALU.add
                                                ).then_inc(h_round, 1)
                pool.wait_ge(sc, 4)
                skewed(pool, NG, FIRST, [(0, round_h), (3, add)])

            @block.vector
            def _(dve):
                nc.vector.memset(negmagic[:, :], -MAGIC)
                nc.vector.tensor_reduce(cs[:, 9:10], maxh[:, :, :], AX_XY, ALU.max).then_inc(sc, 1)
                dve.wait_ge(all_h, 1)
                nc.vector.tensor_scalar(cs[:, 11:12], cs[:, 7:8], cs[:, 10:11], None, ALU.mult).then_inc(sc, 1)
                dve.wait_ge(sc, 2)
                nc.vector.tensor_scalar(cs[:, 9:10], cs[:, 11:12], 1.0 / 127.0, None, ALU.mult).then_inc(sc, 1)
                dve.wait_ge(sc, 3)
                nc.vector.reciprocal(cs[:, 4:5], cs[:, 9:10])
                nc.vector.tensor_scalar(orow[:, :], drow[:, :], cs[:, 9:10], None, ALU.mult).then_inc(sc, 1)

                def clip_h(g, par):
                    dve.wait_ge(h_round, (g + 1) * 2)
                    for v in halves(g):
                        nc.vector.tensor_scalar(v, v, MAGIC - 128.0, MAGIC + 127.0, ALU.max, ALU.min).then_inc(h_quant, 1)

                def scale_out(g, par):
                    if past(g, 2):
                        dve.wait_ge(st_o[par], turns(g - 2, par))
                    for k in range(2):
                        dve.wait_ge(o_ready, g * 2 + k + 1)
                        nc.vector.tensor_tensor(final[:, par, k * 512:(k + 1) * 512].rearrange("p (t c) -> p t c", t=2),
                                                psB[par * 2 + k][:, :].rearrange("p (t c) -> p t c", t=2),
                                                orow[:, :].unsqueeze(1).to_broadcast([P, 2, D]),
                                                ALU.mult).then_inc(o_scaled, 1)
                dve.wait_ge(sc, 4)
                skewed(dve, NG, FIRST, [(1, clip_h), (3, scale_out)])

            @block.scalar
            def _(act):
                act.wait_ge(sc, 1)

                def subtract(g, par):
                    act.wait_ge(h_quant, (g + 1) * 2)
                    if past(g, 2):
                        act.wait_ge(o_ready, (g - 1) * 2)
                    nc.scalar.activation(hq[:, par, 0:IC - 1, :], hT[:, 0:IC - 1, bass.ds(g * GW, GW)], ACT.Identity,
                                         bias=negmagic[:, :])
                    nc.scalar.activation(hq[0:TAIL, par, IC - 1, :], hT[0:TAIL, IC - 1, bass.ds(g * GW, GW)], ACT.Identity,
                                         bias=negmagic[0:TAIL, :]).then_inc(hq_done, 1)
                skewed(act, NG, FIRST, [(1, subtract)])

            @block.tensor
            def _(pe):
                def down(g, par):
                    pe.wait_ge(hq_done, g + 1)
                    if past(g, 2):
                        pe.wait_ge(o_scaled, (g - 1) * 2)
                    for t in range(GT):
                        for c in range(IC):
                            hgt = TAIL if c == IC - 1 else P
                            last = nc.tensor.matmul(psB[par * 2 + t // 2][:, (t % 2) * D:(t % 2 + 1) * D],
                                                    hq[0:hgt, par, c, t * P:(t + 1) * P], wdT[0:hgt, c, :],
                                                    start=c == 0, stop=c == IC - 1)
                        if t % 2:
                            last.then_inc(o_ready, 1)
                skewed(pe, NG, FIRST, [(2, down)])


def build(nc, d):
    outer = ExitStack()
    with outer:
        def sb(stack, name, shape, dt=F32):
            return stack.enter_context(nc.sbuf_tensor(name, shape, dt))
        consts = sb(outer, "consts_sb", [P, C_END])
        ident16 = sb(outer, "ident16", [P, P], F16)
        ident_bf = sb(outer, "ident_bf", [P, P], BF16)
        ones16 = sb(outer, "ones16", [P, P], F16)
        env = {"ident_bf": ident_bf, "passed": outer.enter_context(nc.semaphore("passed"))}
        env["pos"] = sb(outer, "pos", [P, NT, 2], I32)
        env["wts"] = sb(outer, "wts", [P, NT, 2])
        with ExitStack() as moe:
            env["logits"] = sb(moe, "logits", [P, NT, EXPERTS])
            env["zero16"] = sb(moe, "zero16", [P, 2 * D], F16)
            env["wg16"] = sb(moe, "wg16", [P, DC, 2, EXPERTS], F16)
            W_all = env["W_all"] = sb(moe, "W_all", [P, PIECES, 2, 1024], F16)
            l = LAYERS[0]
            U = W_all[:, EARLY:PIECES, :, :].rearrange("p n h c -> p (n h c)")[:, 0:B * l.nu * 2 * D]
            room = W_all[:, 0:4, :, :].rearrange("p n h c -> p (n h c)").bitcast(F32)
            with ExitStack() as a0:
                G = sb(a0, "G0", [P, B * DC * 2 * l.cols], F16)
                Brow = sb(a0, "Brow0", [P, B * l.cols], F16)
                prepare_attention(nc, 0, d, consts, G[:, :], U, Brow[:, :], env["wg16"], room)
                with nc.semaphore("consts_made") as made, nc.Block() as block:
                    @block.vector
                    def _(dve):
                        nc.vector.tensor_copy(ident16[:, :], consts[:, C_ID:C_ID + P]).then_inc(made, 1)
                        nc.vector.tensor_copy(ident_bf[:, :], consts[:, C_ID:C_ID + P]).then_inc(made, 1)
                        nc.vector.memset(ones16[:, :], 0.0).then_inc(made, 1)
                        nc.vector.memset(env["zero16"][:, :], 0.0).then_inc(made, 1)
                        dve.wait_ge(made, 4)
                        nc.vector.memset(ones16[0:1, :], XS).then_inc(made, 1)
                        nc.vector.memset(ones16[P // 2:P // 2 + 1, :], XS).then_inc(made, 1)
                        dve.wait_ge(made, 6)
                attention(nc, 0, d, consts, ones16, ident16, G[:, :], U, Brow[:, :], env)
            experts(nc, d, consts, ident16, env)
        env["xall"] = sb(outer, "xall", [P, NT, D])
        env["xn4"] = sb(outer, "xn4", [P, NT, D])
        env["mx"] = sb(outer, "mx", [P, NT])
        env["wgu"] = sb(outer, "wgu", [P, 2, DC, INTER], BF16)
        env["wdT"] = sb(outer, "wdT", [P, IC, D], BF16)
        env["srow"] = sb(outer, "srow", [P, 2, IC])
        env["drow"] = sb(outer, "drow", [P, D])
        env["cs"] = sb(outer, "cs", [P, 12])
        l = LAYERS[1]
        with ExitStack() as a1:
            env["bo_row"] = sb(a1, "bo_row", [P, D])
            G = sb(a1, "G1", [P, B * DC * 2 * l.cols], F16)
            U = sb(a1, "U1", [P, B * l.nu * 2 * D], F16)
            Brow = sb(a1, "Brow1", [P, B * l.cols], F16)
            room = env["xall"][:, :, :].rearrange("p t c -> p (t c)")
            prepare_attention(nc, 1, d, consts, G[:, :], U[:, :], Brow[:, :], None, room, ffn=env)
            attention(nc, 1, d, consts, ones16, ident16, G[:, :], U[:, :], Brow[:, :], env)
        quantised_ffn(nc, d, consts, ident16, env)


def constants(np):
    c = np.zeros((P, C_END), np.float32)
    p = np.arange(P)
    c[:, C_ID:C_ID + P] = np.eye(P)
    c[:, C_TRI:C_TRI + P] = p[:, None] < p[None, :]
    c[:, C_IOTA:C_IOTA + EXPERTS] = np.arange(EXPERTS)
    c[:, C_RESET:C_RESET + EXPERTS * NT] = np.tile(np.arange(NT) > 0, EXPERTS)
    c[:, C_THR:C_THR + ROUTED] = np.arange(ROUTED) * SLOT
    c[:, C_ONE:C_ONE + P] = 1
    c[:, C_POW] = -0.5
    return c


def head_mask(np, l):
    return ((np.arange(P) // l.dim)[:, None] == (np.arange(l.width) // KEYS)[None, :]).astype(np.float32)


def kernel(**inputs):
    import numpy as np
    import concourse.bacc as bacc
    from concourse.bass_utils import run_bass_kernel_spmd

    a = {k: np.asarray(v) for k, v in inputs.items()}

    def chunks(m):
        return np.ascontiguousarray(m.reshape(-1, P, m.shape[-1]).transpose(1, 0, 2))

    def column(v):
        return v.reshape(-1, P).T
    h0 = LAYERS[0].feat
    arrays = {
        "consts": constants(np),
        "x0": a["x"].reshape(T, D),
        "ctxT": chunks(a["ctx_1024"].reshape(B * KEYS, D).T),
        "wg": chunks(a["L0_ffn_Wg"]),
        "wk0": chunks(a["L0_xattn_key_down"].transpose(1, 0, 2).reshape(D, h0)),
        "wv0": chunks(a["L0_xattn_value_down"].transpose(1, 0, 2).reshape(D, h0)),
        "wq0": chunks(a["L0_xattn_query_down"].transpose(0, 2, 1).reshape(h0, D)),
        "wo0": chunks(a["L0_xattn_value_up"].reshape(h0, D)),
        "bias0": np.stack([column(a["L0_xattn_query_down_bias"].reshape(-1)), np.zeros((P, 4), np.float32),
                           np.zeros((P, 4), np.float32)], 1),
        "wk1": chunks(a["L1_xattn_Wk"].T),
        "wv1": chunks(a["L1_xattn_Wv"].T),
        "wq1": chunks(a["L1_xattn_Wq"]),
        "wo1": chunks(a["L1_xattn_Wo"].T),
        "bias1": np.stack([column(a["L1_xattn_b" + n]) for n in "qkv"], 1),
        "bo": np.broadcast_to(a["L1_xattn_bo"][None], (P, D)),
        "wgate": a["L1_ffn_w_gate"], "wup": a["L1_ffn_w_up"], "wd": a["L1_ffn_w_down"],
        "clip": np.broadcast_to(np.concatenate([a["L1_ffn_clip_x"], a["L1_ffn_clip_down"]])[None], (P, 2)),
    }
    w1 = np.concatenate([a["L0_ffn_Ws1"][None], a["L0_ffn_W1"]])
    w2 = np.concatenate([a["L0_ffn_Ws2"][None], a["L0_ffn_W2"]])
    w2 = w2.reshape(NE, 2, 4, P, D).transpose(0, 1, 3, 2, 4)
    arrays["w"] = np.concatenate([w1.reshape(2 * NE * P, FF), w2.reshape(2 * NE * P, FF)])
    b1 = np.concatenate([a["L0_ffn_bs1"][None], a["L0_ffn_b1"]])
    arrays["b1"] = b1.reshape(NE * FC, P).T
    b2 = np.concatenate([a["L0_ffn_bs2"][None], a["L0_ffn_b2"]])
    arrays["b2"] = np.broadcast_to(b2.reshape(1, NE * D), (P, NE * D))

    for n, l in enumerate(LAYERS):
        arrays[f"mask{n}"] = head_mask(np, l)

    nc = bacc.Bacc("TRN2", target_bir_lowering=False, num_devices=1)
    arrays = {k: np.ascontiguousarray(v) for k, v in arrays.items()}
    d = {k: nc.dram_tensor(f"in_{k}", v.shape, mybir.dt.from_np(v.dtype), kind="ExternalInput").ap()
         for k, v in arrays.items()}
    for n in ("wk", "wv", "wq", "wo", "bias", "mask"):
        d[n] = [d[n + "0"], d[n + "1"]]
    d["wgu"] = [d["wgate"], d["wup"]]
    d["x1"] = nc.dram_tensor("x1_dram", (T, D), F32, kind="Internal").ap()
    d["xs"] = nc.dram_tensor("xs_dram", (ROWS, 2 * D), F16, kind="Internal").ap()
    d["y"] = nc.dram_tensor("y_dram", (ROWS, D), F32, kind="Internal").ap()
    d["out"] = nc.dram_tensor("out_dram", (T, D), F32, kind="ExternalOutput").ap()
    build(nc, d)
    r = run_bass_kernel_spmd(nc, [{f"in_{k}": v for k, v in arrays.items()}], core_ids=[0])
    return r.results[0]["out_dram"].reshape(B, S, D)
```

```python
import concourse.bass as bass
from concourse import mybir
from contextlib import ExitStack
import numpy as np

F32 = mybir.dt.float32
F16 = mybir.dt.float16
BF16 = mybir.dt.bfloat16
I32 = mybir.dt.int32
ALU = mybir.AluOpType
ACT = mybir.ActivationFunctionType
AX_X = mybir.AxisListType.X
AX_XY = mybir.AxisListType.XY

RMAX = bass.bass_isa.ReduceOp.max

P = 128
B, S, D = 4, 1024, 256
KEYS = 64
T = B * S
NT = T // P
TPB = S // P
DC = D // P
EXPERTS, FF = 8, 1024
NE = EXPERTS + 1
FC = FF // P
SLOT = 256
SHARED = T // SLOT
ROUTED = (2 * T + EXPERTS * (SLOT - 1)) // SLOT
NTILE = SHARED + ROUTED
ROWS = NTILE * SLOT
ZEROS, ZK = (ROWS - T) // NT, 3
PIECES = 4 * NE
FIRST_PIECES = (0, 1, 2 * NE, 2 * NE + 1)
REST = (2, 2 * NE + 2)
EARLY = 32
assert 2 * EXPERTS == SHARED
INTER = 704
IC = (INTER + P - 1) // P
TAIL = INTER - (IC - 1) * P
MAGIC = 1.5 * 2.0 ** 23
EPS = 1e-5

XS = 64.0
PS = 1024.0
UNSCALE = 1.0 / (XS * XS)
UNSCALE_P = 1.0 / (XS * PS)


class Layer:
    def __init__(self, heads, dim, scale):
        self.heads, self.dim = heads, dim
        self.feat = heads * dim
        self.nc_ = self.feat // P
        self.hpc = P // dim
        self.width = self.hpc * KEYS
        self.cols = heads * KEYS
        self.banks = self.cols // 512
        self.nu = self.cols // P
        self.gscale = XS * scale


LAYERS = [Layer(8, 64, 1.0), Layer(16, 16, 0.25)]

C_ID, C_TRI = 0, P
C_IOTA = C_TRI + P
C_RESET = C_IOTA + EXPERTS
C_THR = C_RESET + EXPERTS * NT
C_ONE = C_THR + ROUTED
C_POW = C_ONE + P
C_END = C_POW + 1


def run_steps(eng, lo, hi, step):
    pairs = (hi - lo) // 2
    if pairs:
        with eng.Fori(0, pairs) as j:
            step(j * 2 + lo, lo % 2)
            step(j * 2 + (lo + 1), (lo + 1) % 2)
    if (hi - lo) % 2:
        step(hi - 1, (hi - 1) % 2)


def skewed(eng, n, first, stages):
    def step(t, parity):
        for lag, body in stages:
            if not isinstance(t, int) or 0 <= t - lag < n:
                body(t - lag, (parity - lag) % 2)
    for t in range(first):
        step(t, t % 2)
    run_steps(eng, first, n, step)
    for t in range(n, n + max(lag for lag, _ in stages)):
        step(t, t % 2)


def past(i, depth):
    return not isinstance(i, int) or i >= depth


def wait_apart(eng, passed, sem, value):
    eng.wait_ge(sem, value)
    eng.sem_inc(passed, 1)


def turns(i, par):
    return (i - par) * 8 + 16


def height(c):
    return TAIL if c == IC - 1 else P


class Room:
    def __init__(self, words):
        self.words, self.at = words, 0

    def take(self, shape, dt=F32):
        n = int(np.prod(shape[1:])) // (1 if dt == F32 else 2)
        v = self.words[0:shape[0], self.at:self.at + n]
        self.at += n
        assert self.at <= self.words.shape[1]
        if dt != F32:
            v = v.bitcast(dt)
        names = "abcdef"[:len(shape) - 1]
        return v.rearrange(f"p ({' '.join(names)}) -> p {' '.join(names)}", **dict(zip(names, shape[1:])))


def early_inputs(stage):
    l = LAYERS[1]
    size, room = DC * l.feat, Room(stage[:, :, :].rearrange("p k c -> p (k c)"))
    return room.take([P, size]), room.take([P, size]), room.take([P, DC, B * KEYS]), room.take([P, 3, l.nc_])


def load_early(sp, L, d, wk, wv, ctxT, bias, loaded):
    sp.dma_start(wk.rearrange("p (m f) -> p m f", m=DC), d["wk"][L]).then_inc(loaded, 16)
    sp.dma_start(ctxT, d["ctxT"]).then_inc(loaded, 16)
    sp.dma_start(wv.rearrange("p (m f) -> p m f", m=DC), d["wv"][L]).then_inc(loaded, 16)
    sp.dma_start(bias, d["bias"][L]).then_inc(loaded, 16)


def prepare_attention(nc, mem, L, d, consts, G, U, Brow, env, wide, more):
    ffn, wg16 = (env, None) if L else (None, env["wg16"])
    l = LAYERS[L]
    C, W, NU = l.nc_, l.width, l.nu
    gsplit = l.banks
    units = [("g", m, c) for m in range(DC) for c in range(gsplit)]
    units += [("b", c, 0) for c in range(gsplit)]
    units += [("u", k, 0) for k in range(NU // 2)]
    row_unit = DC * gsplit
    RING = 5
    NUn = len(units)
    G = G.rearrange("p (b m h c) -> p b m h c", b=B, m=DC, h=2)
    U = U.rearrange("p (b u h c) -> p b u h c", b=B, u=NU, h=2)
    Brow = Brow.rearrange("p (b c) -> p b c", b=B)
    with ExitStack() as ctx:
        def sb(name, shape, dt=F32):
            return mem.enter_context(nc.sbuf_tensor(f"p{L}_{name}", shape, dt))

        def sem(name):
            return mem.enter_context(nc.semaphore(f"p{L}_{name}"))
        size = DC * l.feat
        if L == 0:
            wk, wv = wide.take([P, size]), wide.take([P, size])
            ctxT, bias = wide.take([P, DC, B * KEYS]), wide.take([P, 3, C])
        else:
            wk, wv, ctxT, bias = early_inputs(env["stage"])
        wq, wo = wide.take([P, size]), wide.take([P, size])
        wq, wo = (w.rearrange("p (c d) -> p c d", c=C) for w in (wq, wo))
        bqb = sb("bqb", [P, C, P]) if L else wide.take([P, C, P])
        kvT = wide.take([P, 2, C, B * KEYS])
        bd = wide.take([P, 2, 2, C, W])
        bhi = more.take([P, 2, 512], F16)
        if L == 0:
            wg = more.take([P, DC, EXPERTS])
        mask_sb = wide.take([P, W])
        ps_kv = [ctx.enter_context(nc.psum_tensor(f"p{L}_pskv{i}", [P, 512], F32)) for i in range(2)]
        ps = [ctx.enter_context(nc.psum_tensor(f"p{L}_ps{i}", [P, 512], F32)) for i in range(RING)]
        kv_loaded = env["kv_loaded1"] if L else sem("kv_loaded")
        loaded, kv_ready, kv_done = sem("loaded"), sem("kv_ready"), sem("kv_done")
        bq_done, k_ready, v_ready, unit_ready = sem("bq_done"), sem("k_ready"), sem("v_ready"), sem("unit_ready")
        hi_done, lo_done = sem("hi_done"), sem("lo_done")
        wg_hi, made = sem("wg_hi"), sem("made")
        env["made"] = made
        n_loads = 3 + (2 if L == 0 else 0)
        if ffn is not None:
            wraw = more.take([P, 2, IC, D])
            wdraw = more.take([P, DC, INTER])
            wint = more.take([P, 2, IC, D], BF16)
            wdint = more.take([P, DC, INTER], BF16)
            sinv = sb("sinv", [P, 3, IC])
            dsc = sb("dsc", [P, DC])
            dscb = more.take([P, DC, P])
            clip = sb("clip", [P, 2])
            psW = ctx.enter_context(nc.psum_tensor("p1_psW", [P, 1024], BF16))
            wgu, wdT, srow, drow, cs, ident_bf = (ffn[n] for n in ("wgu", "wdT", "srow", "drow", "cs", "ident_bf"))
            w_loaded, w_chain, w_scaled, w_rounded, w_quant, w_turned, w_copied, sig_ready = (sem(n) for n in (
                "w_loaded", "w_chain", "w_scaled", "w_rounded", "w_quant", "w_turned", "w_copied", "sig_ready"))
            items = [(g, c) for g in range(2) for c in range(IC)] + [(2, m) for m in range(DC)]
            jobs = [("gu", g, c) for g in range(2) for c in range(IC)] + [("d", 0, c) for c in range(IC)] + [("row", 0, 0)]

            def item(w, c):
                if w == 2:
                    return wdraw[:, c, :], wdint[:, c, :], sinv[:, 2, c:c + 1]
                hgt = height(c)
                return wraw[0:hgt, w, c, :], wint[0:hgt, w, c, :], sinv[0:hgt, w, c:c + 1]

            def job_at(b, n):
                j = (b - B // 2) * NUn + n
                return j if 0 <= j < len(jobs) else None
            assert NUn >= 10
            assert job_at(B - 1, NUn - 1) is None or NUn * (B // 2) >= len(jobs)
        mask = mask_sb[:, :].rearrange("p (h k) -> p h k", k=KEYS)

        def prepare_sync(sp):
            if L == 0:
                load_early(sp, 0, d, wk, wv, ctxT, bias, kv_loaded)
            if ffn is not None:
                for g in range(2):
                    sp.dma_start(wraw[:, g, 0:IC - 1, :], d["wgu"][g][0:(IC - 1) * P, :].rearrange("(c p) h -> p c h", p=P)
                                 ).then_inc(w_loaded, 16)
                    sp.dma_start(wraw[0:TAIL, g, IC - 1, :], d["wgu"][g][(IC - 1) * P:INTER, :]).then_inc(w_loaded, 16)
                sp.dma_start(wdraw[:, :, :], d["wd"].rearrange("(m p) i -> p m i", p=P)).then_inc(w_loaded, 16)
                sp.dma_start(clip[:, :], d["clip"]).then_inc(w_loaded, 16)

        def prepare_tensor(pe):
            pe.wait_ge(kv_loaded, 64)
            for c in range(C):
                if c >= 2:
                    pe.wait_ge(kv_done, 2 * (c - 1))
                for j, w in enumerate((wk, wv)):
                    for m in range(DC):
                        at = m * l.feat + c * P
                        last = nc.tensor.matmul(ps_kv[c % 2][:, j * 256:(j + 1) * 256], w[:, at:at + P],
                                                ctxT[:, m, :], start=m == 0, stop=m == DC - 1)
                last.then_inc(kv_ready, 1)
            pe.wait_ge(bq_done, 1)
            pe.wait_ge(loaded, 16 * n_loads)

            def turn(j):
                kind, g, c = jobs[j]
                if kind == "row":
                    pe.wait_ge(w_scaled, 4)
                    for m in range(DC):
                        last = nc.tensor.matmul(ps_kv[0][:, m * P:(m + 1) * P], dscb[:, m, :], consts[:, C_ID:C_ID + P],
                                                start=True, stop=True)
                    last.then_inc(w_turned, 1)
                    return
                pe.wait_ge(w_quant, g * IC + c + 1 if kind == "gu" else len(items))
                if j >= 1:
                    pe.wait_ge(w_copied, j)
                hgt = height(c)
                for m in range(DC):
                    if kind == "gu":
                        last = nc.tensor.transpose(psW[:, m * P:m * P + hgt], wint[0:hgt, g, c, m * P:(m + 1) * P],
                                                   ident_bf[0:hgt, 0:hgt])
                    else:
                        last = nc.tensor.transpose(psW[0:hgt, m * P:(m + 1) * P], wdint[:, m, c * P:c * P + hgt],
                                                   ident_bf[:, :])
                last.then_inc(w_turned, 1)
            for b in range(B):
                pe.wait_ge(k_ready, b + 1)
                for n, (kind, x, y) in enumerate(units):
                    at = b * NUn + n
                    bank = ps[at % RING]
                    if at >= RING:
                        pe.wait_ge(lo_done, at - RING + 1)
                    if kind == "u" and x == 0:
                        pe.wait_ge(v_ready, b + 1)
                    if kind == "g" and l.banks == 1:
                        for c in range(C):
                            last = nc.tensor.matmul(bank[:, c * W:(c + 1) * W], wq[:, c, x * P:(x + 1) * P],
                                                    bd[:, b % 2, 0, c, :], start=True, stop=True)
                    elif kind == "g":
                        last = nc.tensor.matmul(bank[:, :], wq[:, y, x * P:(x + 1) * P], bd[:, b % 2, 0, y, :],
                                                start=True, stop=True)
                    elif kind == "b":
                        for c in (range(C) if l.banks == 1 else (x,)):
                            o = c * W if l.banks == 1 else 0
                            last = nc.tensor.matmul(bank[:, o:o + W], bqb[:, c, :], bd[:, b % 2, 0, c, :],
                                                    start=True, stop=True)
                    else:
                        for k in range(2):
                            u = 2 * x + k
                            c, o = (u * P) // W, (u * P) % W
                            last = nc.tensor.matmul(bank[:, k * D:(k + 1) * D], bd[:, b % 2, 1, c, o:o + P], wo[:, c, :],
                                                    start=True, stop=True)
                    last.then_inc(unit_ready, 1)
                    if ffn is not None and job_at(b, n) is not None:
                        turn(job_at(b, n))
            pe.wait_ge(hi_done, B * NUn)
            pe.wait_ge(lo_done, B * NUn)
            if L == 0:
                pe.wait_ge(wg_hi, 2)
                pe.wait_ge(made, 6)
            else:
                pe.wait_ge(w_copied, len(jobs))

        def prepare_scalar(act):
            act.dma_start(mask_sb[:, :], d["mask"][L]).then_inc(loaded, 16)
            act.dma_start(wq, d["wq"][L]).then_inc(loaded, 16)
            act.dma_start(wo, d["wo"][L]).then_inc(loaded, 16)
            if L == 0:
                act.dma_start(wg[:, :, :], d["wg"]).then_inc(loaded, 16)
                act.dma_start(consts[:, :], d["consts"]).then_inc(loaded, 16)
                act.wait_ge(loaded, 16 * n_loads)
                nc.scalar.activation(wg16[:, :, 0, :], wg[:, :, :], ACT.Copy, scale=XS).then_inc(wg_hi, 1)
            for b in range(B):
                for n, (kind, x, y) in enumerate(units):
                    at = b * NUn + n
                    if ffn is not None and at == NUn:
                        act.wait_ge(w_loaded, 96)
                        nc.scalar.activation(cs[:, 2:4], clip[:, :], ACT.Exp, scale=-1.0).then_inc(sig_ready, 1)
                    act.wait_ge(unit_ready, at + 1)
                    bank = ps[at % RING]
                    if kind == "g":
                        nc.scalar.activation(G[:, b, x, 0, y * 512:(y + 1) * 512], bank[:, :], ACT.Copy,
                                             scale=l.gscale).then_inc(hi_done, 1)
                    elif kind == "b":
                        k = b * gsplit + x
                        if k >= 2:
                            act.wait_ge(lo_done, (k - 2) // gsplit * NUn + row_unit + (k - 2) % gsplit + 1)
                        nc.scalar.activation(Brow[0:P // 2, b, x * 512:(x + 1) * 512], bank[0:P // 2, :], ACT.Copy,
                                             scale=l.gscale)
                        nc.scalar.activation(bhi[P // 2:P, k % 2, :], bank[P // 2:P, :], ACT.Copy,
                                             scale=l.gscale).then_inc(hi_done, 1)
                    else:
                        nc.scalar.activation(U[:, b, 2 * x:2 * x + 2, 0, :], bank[:, :].rearrange("p (k d) -> p k d", d=D),
                                             ACT.Copy, scale=XS).then_inc(hi_done, 1)
                    if ffn is None or job_at(b, n) is None:
                        continue
                    j = job_at(b, n)
                    kind, g, c = jobs[j]
                    hgt = height(c)
                    act.wait_ge(w_turned, j + 1)
                    if kind == "row":
                        nc.scalar.activation(drow[:, :], ps_kv[0][:, 0:D], ACT.Copy).then_inc(w_copied, 1)
                    elif kind == "gu":
                        nc.scalar.activation(wgu[:, g, :, c * P:c * P + hgt],
                                             psW[:, 0:2 * P].rearrange("p (m i) -> p m i", m=DC)[:, :, 0:hgt],
                                             ACT.Copy).then_inc(w_copied, 1)
                    else:
                        nc.scalar.activation(wdT[0:hgt, c, :], psW[0:hgt, 0:D], ACT.Copy).then_inc(w_copied, 1)

        def prepare_gpsimd(pool):
            pool.wait_ge(loaded, 16 * n_loads)
            pool.wait_ge(kv_done, 2 * C)

            def round_weights():
                pool.wait_ge(w_scaled, 4)
                for w, c in items:
                    src, _, inverse = item(w, c)
                    nc.gpsimd.tensor_scalar(src, src, inverse, MAGIC, ALU.mult, ALU.add).then_inc(w_rounded, 1)
            for b in range(B):
                if ffn is not None and b == 2:
                    round_weights()
                if b >= 2:
                    pool.wait_ge(unit_ready, (b - 1) * NUn)
                for c in range(C):
                    src = kvT[:, 1, c, b * KEYS:(b + 1) * KEYS].unsqueeze(1).to_broadcast([P, l.hpc, KEYS])
                    last = nc.gpsimd.tensor_tensor(bd[:, b % 2, 1, c, :].rearrange("p (h k) -> p h k", k=KEYS),
                                                   src, mask, ALU.mult)
                last.then_inc(v_ready, 1)

        def prepare_vector(dve):
            dve.wait_ge(kv_loaded, 64)
            for c in range(C):
                dve.wait_ge(kv_ready, c + 1)
                for j in range(2):
                    nc.vector.tensor_scalar(kvT[:, j, c, :], ps_kv[c % 2][:, j * 256:(j + 1) * 256],
                                            bias[:, 1 + j, c:c + 1], None, ALU.add).then_inc(kv_done, 1)
            nc.vector.tensor_copy(bqb[:, :, :], bias[:, 0, :].unsqueeze(2).to_broadcast([P, C, P])).then_inc(bq_done, 1)
            if L == 0:
                dve.wait_ge(wg_hi, 1)
                nc.vector.scalar_tensor_tensor(out=wg16[:, :, 1, :], in0=wg[:, :, :], scalar=XS, in1=wg16[:, :, 0, :],
                                               op0=ALU.mult, op1=ALU.subtract).then_inc(wg_hi, 1)
            dve.wait_ge(kv_done, 2 * C)
            dve.wait_ge(loaded, 16 * n_loads)
            if L == 0:
                nc.vector.tensor_copy(env["ident16"][:, :], consts[:, C_ID:C_ID + P]).then_inc(made, 1)
                nc.vector.tensor_copy(env["ident_bf"][:, :], consts[:, C_ID:C_ID + P]).then_inc(made, 1)
                nc.vector.memset(env["ones16"][:, :], 0.0).then_inc(made, 1)
                nc.vector.memset(env["zero16"][:, :], 0.0).then_inc(made, 1)
                dve.wait_ge(made, 4)
                nc.vector.memset(env["ones16"][0:1, :], XS).then_inc(made, 1)
                nc.vector.memset(env["ones16"][P // 2:P // 2 + 1, :], XS).then_inc(made, 1)

            def scale_step(n):
                wide_rows, tail_rows = srow[:, :, 0:IC - 1], srow[0:TAIL, :, IC - 1]
                if n == 0:
                    dve.wait_ge(w_loaded, 96)
                if n < 4:
                    g, hgt = n // 2, TAIL if n % 2 else P
                    chunks = slice(IC - 1, IC) if n % 2 else slice(0, IC - 1)
                    nc.vector.tensor_reduce(srow[0:hgt, g, chunks], wraw[0:hgt, g, chunks, :], AX_X, ALU.max,
                                            apply_absolute_value=True).then_inc(w_chain, 1)
                elif n == 4:
                    nc.vector.tensor_reduce(dsc[:, :], wdraw[:, :, :], AX_X, ALU.max, apply_absolute_value=True
                                            ).then_inc(w_chain, 1)
                elif n == 6:
                    dve.wait_ge(w_chain, 5)
                    for v in (wide_rows, tail_rows, dsc[:, :]):
                        nc.vector.tensor_scalar(v, v, 1.0 / 127.0, None, ALU.mult).then_inc(w_chain, 1)
                elif n == 8:
                    dve.wait_ge(w_chain, 8)
                    nc.vector.reciprocal(sinv[:, 0:2, 0:IC - 1], wide_rows).then_inc(w_scaled, 1)
                    nc.vector.reciprocal(sinv[0:TAIL, 0:2, IC - 1], tail_rows).then_inc(w_scaled, 1)
                    nc.vector.reciprocal(sinv[:, 2, 0:DC], dsc[:, :]).then_inc(w_scaled, 1)
                    nc.vector.tensor_copy(dscb[:, :, :], dsc[:, :].unsqueeze(2).to_broadcast([P, DC, P])
                                          ).then_inc(w_scaled, 1)

            def integer_step(n):
                if 3 <= n:
                    for k in range(2 * (n - 3), min(2 * (n - 2), len(items))):
                        src, dst, _ = item(*items[k])
                        dve.wait_ge(w_rounded, k + 1)
                        nc.vector.tensor_scalar(dst, src, MAGIC, 127.0, ALU.subtract, ALU.min).then_inc(w_quant, 1)

            def sigmoid():
                dve.wait_ge(sig_ready, 1)
                nc.vector.tensor_scalar(cs[:, 4:6], cs[:, 2:4], 1.0, None, ALU.add).then_inc(sig_ready, 1)
                dve.wait_ge(sig_ready, 2)
                nc.vector.reciprocal(cs[:, 6:8], cs[:, 4:6])

            def diagonal_k(b):
                if b >= 2:
                    dve.wait_ge(unit_ready, (b - 1) * NUn)
                for c in range(C):
                    src = kvT[:, 0, c, b * KEYS:(b + 1) * KEYS].unsqueeze(1).to_broadcast([P, l.hpc, KEYS])
                    last = nc.vector.tensor_tensor(bd[:, b % 2, 0, c, :].rearrange("p (h k) -> p h k", k=KEYS),
                                                   src, mask, ALU.mult)
                last.then_inc(k_ready, 1)
            diagonal_k(0)
            for b in range(B):
                if b + 1 < B:
                    diagonal_k(b + 1)
                if ffn is not None and b == 2:
                    sigmoid()
                for n, (kind, x, y) in enumerate(units):
                    at = b * NUn + n
                    dve.wait_ge(hi_done, at + 1)
                    bank = ps[at % RING]
                    if kind == "g":
                        nc.vector.scalar_tensor_tensor(out=G[:, b, x, 1, y * 512:(y + 1) * 512], in0=bank[:, :],
                                                       scalar=l.gscale, in1=G[:, b, x, 0, y * 512:(y + 1) * 512],
                                                       op0=ALU.mult, op1=ALU.subtract).then_inc(lo_done, 1)
                    elif kind == "b":
                        nc.vector.scalar_tensor_tensor(out=Brow[P // 2:P, b, x * 512:(x + 1) * 512],
                                                       in0=bank[P // 2:P, :], scalar=l.gscale,
                                                       in1=bhi[P // 2:P, (b * gsplit + x) % 2, :],
                                                       op0=ALU.mult, op1=ALU.subtract).then_inc(lo_done, 1)
                    else:
                        nc.vector.scalar_tensor_tensor(out=U[:, b, 2 * x:2 * x + 2, 1, :],
                                                       in0=bank[:, :].rearrange("p (k d) -> p k d", d=D), scalar=XS,
                                                       in1=U[:, b, 2 * x:2 * x + 2, 0, :],
                                                       op0=ALU.mult, op1=ALU.subtract).then_inc(lo_done, 1)
                    if ffn is not None and b == 0:
                        scale_step(n)
                    if ffn is not None and b == 1:
                        integer_step(n)
    return {"sync": prepare_sync, "tensor": prepare_tensor, "scalar": prepare_scalar, "gpsimd": prepare_gpsimd,
            "vector": prepare_vector}


def attention(nc, L, d, consts, ones16, ident16, G, U, Brow, env, prepare):
    l = LAYERS[L]
    H, COLS, NU, BANKS = l.heads, l.cols, l.nu, l.banks
    first = L == 0
    with ExitStack() as ctx:
        def sb(name, shape, dt=F32):
            return ctx.enter_context(nc.sbuf_tensor(f"a{L}_{name}", shape, dt))

        def pb(name, shape, dt=F32):
            return ctx.enter_context(nc.psum_tensor(f"a{L}_{name}", shape, dt))

        def sem(name):
            return ctx.enter_context(nc.semaphore(f"a{L}_{name}"))

        stat = sb("stat", [P, 2, 6])
        mv = sb("mv", [P, 2, 2])
        rstd = sb("rstd", [P, 2, 1])
        stat2 = sb("stat2", [P, 2, 6])
        mv2 = sb("mv2", [P, 2, 2])
        rstd2 = sb("rstd2", [P, 2, 1])
        nmean = sb("nmean", [P, 2, 1])
        nmean2 = sb("nmean2", [P, 2, 1])
        xn = sb("xn", [P, 2, D])
        xT = sb("xT", [P, 2, 2, D], F16)
        top = sb("top", [P, 2, H])
        ntop = sb("ntop", [P, 2, H])
        prob = sb("prob", [P, 2, COLS])
        total = sb("total", [P, 2, H])
        rtotal = sb("rtotal", [P, 2, H])
        pT = sb("pT", [P, 2, 2, COLS], F16)
        psT = pb("psT", [P, 512])
        ob = 2 if first else 1
        psO = [pb(f"psO{k}", [P, 512]) for k in range(ob)]
        psS = [pb(f"psS{k}", [P, COLS]) for k in range(2)]
        psP = pb("psP", [P, COLS])
        if first:
            x_in = sb("x_in", [P, 2, D])
            x_res = sb("x_res", [P, 2, D])
            x_out = sb("x_out", [P, 2, D])
            xe = sb("xe", [P, 2, COLS])
            added = sb("added", [P, 2, H])
            xn2 = sb("xn2", [P, 2, D])
            xs = sb("xs", [P, 2, 2, D], F16)
            x2T = sb("x2T", [P, 2, 2 * D], F16)
            stage = env["stage"]
            psX = pb("psX", [P, 4 * D], F16)
            psL = pb("psL", [P, 512])
            logits, W_all, zero16, wg16 = env["logits"], env["W_all"], env["zero16"], env["wg16"]
        else:
            y_sh = sb("y_sh", [P, 2, D])
            y_exp = sb("y_exp", [P, 2, 2, D])
            idx = sb("idx", [P, 2, 2], I32)
            acc = sb("acc", [P, 2, D])
            xall, xn4, mx = env["xall"], env["xn4"], env["mx"]
            pos, wts, bo_row = env["pos"], env["wts"], env["bo_row"]

        ld_x = [sem(f"ld_x{k}") for k in range(2)]
        LNK = 4 if first else 6
        SUMK = 4 if first else 1
        OUTK = 5 if first else 6
        ln_done = sem("ln_done")
        rstd_in, rstd_out = sem("rstd_in"), sem("rstd_out")
        xT_ready, x_hi, x_lo = sem("xT_ready"), sem("x_hi"), sem("x_lo")
        scores_ready, top_done = sem("scores_ready"), sem("top_done")
        exp_done, sum_done, prob_done = sem("exp_done"), sem("sum_done"), sem("prob_done")
        pT_ready, p_hi, p_lo = sem("pT_ready"), sem("p_hi"), sem("p_lo")
        pv_ready, out_done = sem("pv_ready"), sem("out_done")
        if first:
            ld_res = [sem(f"ld_res{k}") for k in range(2)]
            ld_w = [sem(f"ld_w{k}") for k in range(2)]
            st_x = [sem(f"st_x{k}") for k in range(2)]
            st_s = [sem(f"st_s{k}") for k in range(2)]
            st_zero = sem("st_zero")
            n_hi, n_lo = sem("n_hi"), sem("n_lo")
            nT_ready, nT_done, logit_ready, logit_done = sem("nT_ready"), sem("nT_done"), sem("logit_ready"), sem("logit_done")
            w_hi, w_lo = sem("w_hi"), sem("w_lo")
            xn_done, xn2_done = sem("xn_done"), sem("xn2_done")
        else:
            ld_y = [sem(f"ld_y{k}") for k in range(2)]
            ld_e = [sem(f"ld_e{k}") for k in range(2)]
            ld_bo = sem("ld_bo")
            idx_done, shared_added, bo_added = sem("idx_done"), sem("shared_added"), sem("bo_added")

        block = ctx.enter_context(nc.Block())
        FIRST = 12
        A = 0 if first else 2

        def batch(i):
            return i // TPB

        def seg(tensor, flat, i, count, size):
            v = tensor[:, :, :].rearrange("p t c -> p (t c)")
            return v[:, bass.ds(i * count + flat, size)]

        @block.sync
        def _(sp):
            prepare["sync"](sp)
            if first:
                assert ZEROS * NT == ROWS - T and ZEROS // ZK * ZK == ZEROS
                sp.wait_ge(env["made"], 4)
            else:
                sp.dma_start(bo_row[:, :], d["bo"]).then_inc(ld_bo, 16)

            def load(i, par):
                rows = d["x0" if first else "x1"][bass.ds(i * P, P), :]
                if past(i, 2):
                    if first:
                        sp.wait_ge(xn_done, i - 1)
                    else:
                        sp.wait_ge(ln_done, (i - 2) * LNK + 2)
                if first:
                    sp.dma_start(x_in[:, par, :], rows).then_inc(ld_x[par], 16)
                else:
                    sp.dma_start(seg(xall, 0, i, D, D), rows).then_inc(ld_x[par], 16)
                    sp.dma_start(y_sh[:, par, :], d["y"][bass.ds(i * P, P), :]).then_inc(ld_y[par], 16)

            def load_res(i, par):
                if past(i, 2):
                    sp.wait_ge(out_done, (i - 2) * OUTK + 1)
                sp.dma_start(x_res[:, par, :], d["x0"][bass.ds(i * P, P), :]).then_inc(ld_res[par], 16)

            def load_piece(i, par):
                if not isinstance(i, int) or i >= len(FIRST_PIECES):
                    return
                if past(i, 2):
                    sp.wait_ge(w_lo, i - 1)
                sp.dma_start(stage[:, par, :], d["w"][FIRST_PIECES[i] * P:(FIRST_PIECES[i] + 1) * P, :]
                             ).then_inc(ld_w[par], 16)

            def clear(i, par):
                sp.dma_start(d["xs"][bass.ds(i * ZEROS + T, ZEROS), :].rearrange("(j p) c -> p j c", j=ZK),
                             zero16[0:ZEROS // ZK, :].unsqueeze(1).to_broadcast([ZEROS // ZK, ZK, 2 * D])
                             ).then_inc(st_zero, 16)

            def store_x(i, par):
                sp.wait_ge(out_done, i * OUTK + 1)
                sp.dma_start(d["x1"][bass.ds(i * P, P), :], x_out[:, par, :]).then_inc(st_x[par], 16)

            def store_n(i, par):
                sp.wait_ge(n_lo, i + 1)
                sp.dma_start(d["xs"][bass.ds(i * P, P), :], xs[:, par, :, :].rearrange("p h c -> p (h c)")).then_inc(st_s[par], 16)

            if first:
                skewed(sp, NT, FIRST, [(0, load), (5, load_res), (0, load_piece), (0, clear), (7, store_x), (8, store_n)])
                for k in range(2):
                    sp.wait_ge(st_x[k], NT * 8)
                    sp.wait_ge(st_s[k], NT * 8)
                sp.wait_ge(st_zero, NT * 16)
            else:
                skewed(sp, NT, FIRST, [(0, load)])

        @block.tensor
        def _(pe):
            prepare["tensor"](pe)
            def transpose_x(i, par):
                if first:
                    pe.wait_ge(xn_done, i + 1)
                else:
                    pe.wait_ge(ln_done, (i + 1) * LNK)
                if past(i, 1):
                    pe.wait_ge(x_lo, i)
                for m in range(DC):
                    last = nc.tensor.transpose(psT[:, m * P:(m + 1) * P], xn[:, par, m * P:(m + 1) * P],
                                               consts[:, C_ID:C_ID + P])
                last.then_inc(xT_ready, 1)

            def scores(i, par):
                b = batch(i)
                pe.wait_ge(x_lo, i + 1)
                if past(i, 2):
                    if first:
                        pe.wait_ge(sum_done, (i - 2) * SUMK + 1)
                    else:
                        pe.wait_ge(exp_done, i - 1)
                for h in range(BANKS):
                    out = psS[par][:, h * 512:(h + 1) * 512]
                    nc.tensor.matmul(out, ones16[:, :], Brow[:, bass.ds(b * COLS + h * 512, 512)], start=True, stop=False)
                    for m in range(DC):
                        for xh, gh in ((0, 0), (0, 1), (1, 0)):
                            off = ((b * DC + m) * 2 + gh) * COLS + h * 512
                            last = nc.tensor.matmul(out, xT[:, par, xh, m * P:(m + 1) * P], G[:, bass.ds(off, 512)],
                                                    start=False, stop=m == DC - 1 and xh == 1)
                last.then_inc(scores_ready, 1)

            def transpose_p(i, par):
                pe.wait_ge(prob_done, i + 1)
                if past(i, 1):
                    pe.wait_ge(p_lo, i)
                src = xe if first else prob
                for u in range(NU):
                    last = nc.tensor.transpose(psP[:, u * P:(u + 1) * P], src[:, par, u * P:(u + 1) * P],
                                               consts[:, C_ID:C_ID + P])
                last.then_inc(pT_ready, 1)

            def values(i, par):
                b = batch(i)
                pe.wait_ge(p_lo, i + 1)
                if past(i, ob):
                    pe.wait_ge(out_done, (i - ob) * OUTK + 1)
                for u in range(NU):
                    for ph, uh in ((0, 0), (0, 1), (1, 0)):
                        off = ((b * NU + u) * 2 + uh) * D
                        last = nc.tensor.matmul(psO[par % ob][:, 0:D], pT[:, par, ph, u * P:(u + 1) * P], U[:, bass.ds(off, D)],
                                                start=u == 0 and ph == 0 and uh == 0, stop=u == NU - 1 and ph == 1)
                last.then_inc(pv_ready, 1)

            def transpose_n(i, par):
                pe.wait_ge(n_lo, i + 1)
                if past(i, 1):
                    pe.wait_ge(nT_done, i)
                for k in range(4):
                    last = nc.tensor.transpose(psX[:, k * P:(k + 1) * P],
                                               xs[:, par, k // 2, (k % 2) * P:(k % 2 + 1) * P], ident16[:, :])
                last.then_inc(nT_ready, 1)

            def router(i, par):
                pe.wait_ge(nT_done, i + 1)
                if past(i, 1):
                    pe.wait_ge(logit_done, i)
                k = 0
                for m in range(DC):
                    for xh in range(2):
                        for gh in range(2):
                            last = nc.tensor.matmul(psL[:, 0:EXPERTS], x2T[:, par, (xh * DC + m) * P:(xh * DC + m + 1) * P],
                                                    wg16[:, m, gh, :], start=k == 0, stop=k == 7)
                            k += 1
                last.then_inc(logit_ready, 1)

            stages = [(A + 2, scores), (A + 1, transpose_x), (A + 4, transpose_p), (A + 5, values)]
            if first:
                stages = [(2, scores), (1, transpose_x), (4, transpose_p), (9, router), (5, values), (8, transpose_n)]
            skewed(pe, NT, FIRST, stages)

        @block.scalar
        def _(act):
            prepare["scalar"](act)
            def exps(i, par):
                act.wait_ge(top_done, 2 * (i + 1))
                if past(i, 2):
                    if first:
                        act.wait_ge(sum_done, (i - 2) * SUMK + 1)
                    else:
                        act.wait_ge(pT_ready, i - 1)
                for h in range(H):
                    of = slice(h * KEYS, (h + 1) * KEYS)
                    last = nc.scalar.activation(prob[:, par, of], psS[par][:, of], ACT.Exp, bias=ntop[:, par, h:h + 1],
                                                scale=UNSCALE, accum_out=None if first else total[:, par, h:h + 1])
                last.then_inc(exp_done, 1)

            def x_high(i, par):
                act.wait_ge(xT_ready, i + 1)
                if past(i, 2):
                    act.wait_ge(scores_ready, i - 1)
                nc.scalar.activation(xT[:, par, 0, :], psT[:, 0:D], ACT.Copy, scale=XS).then_inc(x_hi, 1)

            def p_high(i, par):
                act.wait_ge(pT_ready, i + 1)
                if past(i, 2):
                    act.wait_ge(pv_ready, i - 1)
                nc.scalar.activation(pT[:, par, 0, :], psP[:, :], ACT.Copy, scale=PS).then_inc(p_hi, 1)

            def n_high(i, par):
                act.wait_ge(xn2_done, i + 1)
                if past(i, 2):
                    act.wait_ge(nT_ready, i - 1)
                    act.wait_ge(st_s[par], turns(i - 2, par))
                nc.scalar.activation(xs[:, par, 0, :], xn2[:, par, :], ACT.Copy).then_inc(n_hi, 1)

            def copy_n(i, par):
                act.wait_ge(nT_ready, i + 1)
                if past(i, 2):
                    act.wait_ge(logit_ready, i - 1)
                nc.scalar.activation(x2T[:, par, :], psX[:, 0:2 * D], ACT.Copy).then_inc(nT_done, 1)

            def weight_scale(i, par):
                if isinstance(i, int) and i < len(FIRST_PIECES):
                    act.wait_ge(ld_w[par], turns(i, par))
                    nc.scalar.activation(stage[:, par, :], stage[:, par, :], ACT.Copy, scale=XS).then_inc(w_hi, 1)

            def weight_high(i, par):
                if isinstance(i, int) and i < len(FIRST_PIECES):
                    act.wait_ge(w_hi, i * 2 + 1)
                    nc.scalar.activation(W_all[:, FIRST_PIECES[i], 0, :], stage[:, par, :], ACT.Copy).then_inc(w_hi, 1)

            stages = [(A + 5, p_high), (A + 2, x_high), (A + 3, exps)]
            if first:
                stages = [(5, p_high), (2, x_high), (3, exps), (9, copy_n), (7, n_high), (0, weight_scale), (0, weight_high)]
            skewed(act, NT, FIRST, stages)

        @block.gpsimd
        def _(pool):
            prepare["gpsimd"](pool)
            def normalise(i, par):
                pool.wait_ge(sum_done, SUMK * (i + 1))
                t = xe if first else prob
                v = t[:, par, :].rearrange("p (h k) -> p h k", k=KEYS)
                nc.gpsimd.tensor_tensor(v, v, rtotal[:, par, :].unsqueeze(2).to_broadcast([P, H, KEYS]),
                                        ALU.mult).then_inc(prob_done, 1)

            def weight_low(i, par):
                if isinstance(i, int) and i < len(FIRST_PIECES):
                    pool.wait_ge(w_hi, (i + 1) * 2)
                    nc.gpsimd.tensor_tensor(W_all[:, FIRST_PIECES[i], 1, :], stage[:, par, :],
                                            W_all[:, FIRST_PIECES[i], 0, :], ALU.subtract).then_inc(w_lo, 1)

            def normalise_in(i, par):
                if past(i, 2):
                    pool.wait_ge(xT_ready, i - 1)
                pool.wait_ge(ln_done, (i + 1) * LNK)
                wait_apart(pool, env["passed"], rstd_in, i + 1)
                nc.gpsimd.tensor_scalar(xn[:, par, :], x_in[:, par, :], nmean[:, par, :], rstd[:, par, :], ALU.add,
                                        ALU.mult).then_inc(xn_done, 1)

            def normalise_out(i, par):
                if past(i, 2):
                    pool.wait_ge(n_lo, i - 1)
                pool.wait_ge(out_done, (i + 1) * OUTK)
                wait_apart(pool, env["passed"], rstd_out, i + 1)
                nc.gpsimd.tensor_scalar(xn2[:, par, :], x_out[:, par, :], nmean2[:, par, :], rstd2[:, par, :], ALU.add,
                                        ALU.mult).then_inc(xn2_done, 1)

            def n_low(i, par):
                pool.wait_ge(n_hi, i + 1)
                nc.gpsimd.tensor_tensor(xs[:, par, 1, :], xn2[:, par, :], xs[:, par, 0, :], ALU.subtract).then_inc(n_lo, 1)

            def gather(i, par):
                if past(i, 2):
                    pool.wait_ge(ln_done, (i - 2) * LNK + 2)
                    pool.wait_ge(ld_e[par], 2 * turns(i - 2, par))
                flat = pos[:, :, :].rearrange("p t k -> p (t k)")
                nc.gpsimd.tensor_copy(idx[:, par, :], flat[:, bass.ds(i * 2, 2)]).then_inc(idx_done, 1)
                wait_apart(pool, env["passed"], idx_done, i + 1)
                for k in range(2):
                    nc.gpsimd.indirect_dma_start(
                        out=y_exp[:, par, k, :], out_offset=None, in_=d["y"][:, :],
                        in_offset=bass.IndirectOffsetOnAxis(ap=idx[:, par, k:k + 1], axis=0)).then_inc(ld_e[par], 16)

            def add_shared(i, par):
                pool.wait_ge(ld_x[par], turns(i, par))
                pool.wait_ge(ld_y[par], turns(i, par))
                if past(i, 2):
                    pool.wait_ge(ln_done, (i - 2) * LNK + 2)
                nc.gpsimd.tensor_tensor(acc[:, par, :], seg(xall, 0, i, D, D), y_sh[:, par, :], ALU.add).then_inc(shared_added, 1)

            def add_bo(i, par):
                pool.wait_ge(ln_done, (i + 1) * LNK)
                v = seg(xall, 0, i, D, D)
                nc.gpsimd.tensor_tensor(v, v, bo_row[:, :], ALU.add).then_inc(bo_added, 1)

            def power(src, dst, chain, count, done):
                def body(i, par):
                    pool.wait_ge(chain, count(i))
                    nc.gpsimd.tensor_tensor(dst[:, par, :], src[:, par, 1:2], consts[:, C_POW:C_POW + 1],
                                            ALU.pow).then_inc(done, 1)
                return body
            power_in = power(mv, rstd, ln_done, lambda i: i * LNK + (3 if first else 5), rstd_in)
            power_out = power(mv2, rstd2, out_done, lambda i: i * OUTK + 4, rstd_out)
            if first:
                skewed(pool, NT, FIRST, [(8, n_low), (1, normalise_in), (4, normalise), (7, normalise_out), (1, weight_low),
                                         (6, power_out), (0, power_in)])
            else:
                pool.wait_ge(ld_bo, 16)
                skewed(pool, NT, FIRST, [(A + 4, normalise), (A + 1, add_bo), (1, add_shared), (0, gather), (A + 6, power_out), (A, power_in)])

        @block.vector
        def _(dve):
            prepare["vector"](dve)
            def x_of(i, par):
                return x_in[:, par, :] if first else seg(xall, 0, i, D, D)

            def weigh_first(i, par):
                dve.wait_ge(shared_added, i + 1)
                dve.wait_ge(ld_e[par], 2 * turns(i, par))
                wf = wts[:, :, :].rearrange("p t k -> p (t k)")
                nc.vector.scalar_tensor_tensor(out=acc[:, par, :], in0=y_exp[:, par, 0, :], scalar=wf[:, bass.ds(i * 2, 1)],
                                               in1=acc[:, par, :], op0=ALU.mult, op1=ALU.add).then_inc(ln_done, 1)

            def weigh_second(i, par):
                wf = wts[:, :, :].rearrange("p t k -> p (t k)")
                dve.wait_ge(ln_done, i * LNK + 1)
                nc.vector.scalar_tensor_tensor(out=x_of(i, par), in0=y_exp[:, par, 1, :], scalar=wf[:, bass.ds(i * 2 + 1, 1)],
                                               in1=acc[:, par, :], op0=ALU.mult, op1=ALU.add).then_inc(ln_done, 1)

            def moments_in(i, par):
                if first:
                    wait_apart(dve, env["passed"], ld_x[par], turns(i, par))
                else:
                    wait_apart(dve, env["passed"], ln_done, i * LNK + 2)
                nc.vector.bn_stats(stat[:, par, :], x_of(i, par)).then_inc(ln_done, 1)

            def mean_in(i, par):
                wait_apart(dve, env["passed"], ln_done, i * LNK + (1 if first else 3))
                nc.vector.bn_aggr(mv[:, par, :], stat[:, par, :]).then_inc(ln_done, 1)

            def eps_in(i, par):
                dve.wait_ge(ln_done, i * LNK + (2 if first else 4))
                nc.vector.tensor_scalar(mv[:, par, 1:2], mv[:, par, 1:2], EPS, None, ALU.add).then_inc(ln_done, 1)
                if first:
                    nc.vector.tensor_scalar(nmean[:, par, :], mv[:, par, 0:1], -1.0, None, ALU.mult).then_inc(ln_done, 1)

            def normalise_in(i, par):
                src = x_of(i, par)
                dve.wait_ge(rstd_in, i + 1)
                if past(i, 2):
                    dve.wait_ge(xT_ready, i - 1)
                nc.vector.tensor_scalar(xn[:, par, :], src, mv[:, par, 0:1], rstd[:, par, :], ALU.subtract,
                                        ALU.mult).then_inc(ln_done, 1)

            def x_low(i, par):
                dve.wait_ge(x_hi, i + 1)
                nc.vector.scalar_tensor_tensor(out=xT[:, par, 1, :], in0=psT[:, 0:D], scalar=XS, in1=xT[:, par, 0, :],
                                               op0=ALU.mult, op1=ALU.subtract).then_inc(x_lo, 1)

            def largest(i, par):
                dve.wait_ge(scores_ready, i + 1)
                s = psS[par][:, :].rearrange("p (h k) -> p h k", k=KEYS)
                nc.vector.tensor_reduce(top[:, par, :], s, AX_X, ALU.max).then_inc(top_done, 1)

            def negate(i, par):
                dve.wait_ge(top_done, i * 2 + 1)
                nc.vector.tensor_scalar(ntop[:, par, :], top[:, par, :], -UNSCALE, None, ALU.mult).then_inc(top_done, 1)

            def weighted(i, par):
                dve.wait_ge(exp_done, i + 1)
                if past(i, 2):
                    dve.wait_ge(pT_ready, i - 1)
                nc.vector.scalar_tensor_tensor(out=xe[:, par, :], in0=psS[par][:, :], scalar=UNSCALE, in1=prob[:, par, :],
                                               op0=ALU.mult, op1=ALU.mult).then_inc(sum_done, 1)

            def sums(i, par):
                dve.wait_ge(sum_done, i * SUMK + 1)
                nc.vector.tensor_reduce(total[:, par, :], xe[:, par, :].rearrange("p (h k) -> p h k", k=KEYS), AX_X,
                                        ALU.add, apply_absolute_value=True).then_inc(sum_done, 1)

            def plus_one(i, par):
                dve.wait_ge(sum_done, i * SUMK + 2)
                nc.vector.tensor_scalar(added[:, par, :], total[:, par, :], 1.0, None, ALU.add).then_inc(sum_done, 1)

            def invert(i, par):
                if first:
                    dve.wait_ge(sum_done, i * SUMK + SUMK - 1)
                else:
                    dve.wait_ge(exp_done, i + 1)
                nc.vector.reciprocal(rtotal[:, par, :], (added if first else total)[:, par, :]).then_inc(sum_done, 1)

            def p_low(i, par):
                dve.wait_ge(p_hi, i + 1)
                nc.vector.scalar_tensor_tensor(out=pT[:, par, 1, :], in0=psP[:, :], scalar=PS, in1=pT[:, par, 0, :],
                                               op0=ALU.mult, op1=ALU.subtract).then_inc(p_lo, 1)

            def output(i, par):
                dve.wait_ge(pv_ready, i + 1)
                if first:
                    dve.wait_ge(ld_res[par], turns(i, par))
                    if past(i, 2):
                        dve.wait_ge(st_x[par], turns(i - 2, par))
                        dve.wait_ge(xn2_done, i - 1)
                    x, res = x_out[:, par, :], x_res[:, par, :]
                else:
                    dve.wait_ge(bo_added, i + 1)
                    x = res = seg(xall, 0, i, D, D)
                nc.vector.scalar_tensor_tensor(out=x, in0=psO[par % ob][:, 0:D], scalar=UNSCALE_P, in1=res,
                                               op0=ALU.mult, op1=ALU.add).then_inc(out_done, 1)

            def moments_out(i, par):
                wait_apart(dve, env["passed"], out_done, i * OUTK + 1)
                nc.vector.bn_stats(stat2[:, par, :], x_out[:, par, :] if first else seg(xall, 0, i, D, D)).then_inc(out_done, 1)

            def mean_out(i, par):
                wait_apart(dve, env["passed"], out_done, i * OUTK + 2)
                nc.vector.bn_aggr(mv2[:, par, :], stat2[:, par, :]).then_inc(out_done, 1)

            def eps_out(i, par):
                dve.wait_ge(out_done, i * OUTK + 3)
                if first:
                    nc.vector.tensor_scalar(mv2[:, par, 1:2], mv2[:, par, 1:2], EPS, 1.0 / (XS * XS), ALU.add,
                                            ALU.mult).then_inc(out_done, 1)
                    nc.vector.tensor_scalar(nmean2[:, par, :], mv2[:, par, 0:1], -1.0, None, ALU.mult).then_inc(out_done, 1)
                else:
                    nc.vector.tensor_scalar(mv2[:, par, 1:2], mv2[:, par, 1:2], EPS, None, ALU.add).then_inc(out_done, 1)

            def normalise_out(i, par):
                dve.wait_ge(rstd_out, i + 1)
                nc.vector.tensor_scalar(seg(xn4, 0, i, D, D), seg(xall, 0, i, D, D), mv2[:, par, 0:1], rstd2[:, par, :],
                                        ALU.subtract, ALU.mult).then_inc(out_done, 1)

            def magnitude(i, par):
                dve.wait_ge(out_done, i * OUTK + 5)
                dst = seg(xn4, 0, i, D, D)
                nc.vector.tensor_reduce(mx[:, bass.ds(i, 1)], dst, AX_X, ALU.max,
                                        apply_absolute_value=True).then_inc(out_done, 1)

            def logit(i, par):
                dve.wait_ge(logit_ready, i + 1)
                nc.vector.tensor_scalar(seg(logits, 0, i, EXPERTS, EXPERTS), psL[:, 0:EXPERTS], UNSCALE, None,
                                        ALU.mult).then_inc(logit_done, 1)

            if first:
                stages = [(3, largest), (3, negate), (2, x_low), (5, p_low), (6, output), (0, moments_in),
                          (6, moments_out), (0, mean_in), (3, weighted), (6, mean_out), (0, eps_in), (3, sums),
                          (6, eps_out), (3, plus_one), (9, logit), (3, invert)]
            else:
                stages = [(5, largest), (3, normalise_in), (5, negate), (2, weigh_first), (4, x_low), (2, weigh_second),
                          (7, p_low), (9, normalise_out), (2, moments_in), (9, magnitude), (8, output), (2, mean_in),
                          (8, moments_out), (2, eps_in), (8, mean_out), (5, invert), (8, eps_out)]
            skewed(dve, NT, FIRST, stages)


def experts(nc, d, consts, ident16, env):
    logits, W_all, pos, wts = env["logits"], env["W_all"], env["pos"], env["wts"]
    flatW = W_all[:, :, :, :].rearrange("p n h c -> p (n h c)")
    with ExitStack() as ctx:
        def sb(name, shape, dt=F32):
            return ctx.enter_context(nc.sbuf_tensor(f"e_{name}", shape, dt))

        def pb(name, shape, dt=F32):
            return ctx.enter_context(nc.psum_tensor(f"e_{name}", shape, dt))

        def sem(name):
            return ctx.enter_context(nc.semaphore(f"e_{name}"))
        b1 = sb("b1", [P, NE * FC])
        b2 = sb("b2", [P, NE * D])
        stage = env["stage"]
        SG = 4
        rows = sb("rows", [P, 2 * SG, 2 * D], F16)
        x_in = sb("x_in", [P, 2, 2, 2 * D], F16)
        xT = sb("xT", [P, 2, 4 * SLOT], F16)
        h32 = sb("h32", [P, 2, 2 * SLOT])
        h16 = sb("h16", [P, 2, 2, FC * SLOT], F16)
        y_out = sb("y_out", [P, 2, 2, D])
        table = sb("table", [1, NTILE], I32)
        idx = sb("idx", [P, 2, 2 * SG], I32)

        room = W_all[:, EARLY:PIECES, :, :].rearrange("p n h c -> p (n h c)")
        taken = [0]

        def sb(name, shape, dt=F32):
            halves = int(np.prod(shape[1:])) * (2 if dt == F32 else 1)
            v = room[0:shape[0], taken[0]:taken[0] + halves]
            taken[0] += halves
            v = v if dt == F16 else v.bitcast(dt)
            if len(shape) == 3:
                v = v.rearrange("p (a b) -> p a b", b=shape[2])
            return v
        R = {n: sb("r_" + n, [P, NT, EXPERTS]) for n in ("a", "b", "oh1", "oh2")}
        TE = {n: sb("t_" + n, [P, EXPERTS, NT]) for n in ("tot", "inc")}
        picked = sb("picked", [P, NT * EXPERTS], BF16)
        tri16 = sb("tri16", [P, P], BF16)
        one16 = sb("one16", [P, P], BF16)
        V = {n: sb("v_" + n, [P, NT]) for n in ("v1", "v2", "i", "e", "den")}
        E8 = {n: sb("e8_" + n, [P, EXPERTS]) for n in ("n", "pad", "end", "base")}
        posf = sb("posf", [P, NT, 2])
        cmp_ = sb("cmp", [1, ROUTED, EXPERTS])
        cnt = sb("cnt", [1, ROUTED])

        psX = pb("psX", [P, 8 * P], F16)
        psH = [pb(f"psH{k}", [P, 512]) for k in range(4)]
        psY = [pb(f"psY{k}", [P, 512]) for k in range(2)]
        psR = pb("psR", [P, 512])

        ld_b, ld_row = sem("ld_b"), [sem(f"ld_row{k}") for k in range(2)]
        ld_w = [sem(f"ld_w{k}") for k in range(2)]
        ld_x = [sem(f"ld_x{k}") for k in range(2)]
        st_y = [sem(f"st_y{k}") for k in range(2)]
        scattered = [sem(f"scattered{k}") for k in range(2)]
        idx_done = sem("idx_done")
        route, picked_ready, counts_ready, exp_ready, table_ready = (sem(n) for n in (
            "route", "picked_ready", "counts_ready", "exp_ready", "table_ready"))
        w_hi = [sem(f"w_hi{k}") for k in range(2)]
        w_lo = [sem(f"w_lo{k}") for k in range(2)]
        b1_scaled = sem("b1_scaled")
        xT_ready, xT_done = sem("xT_ready"), sem("xT_done")
        h_ready, relu_done, h_split = sem("h_ready"), sem("relu_done"), sem("h_split")
        y_ready, y_done = sem("y_ready"), sem("y_done")
        block = ctx.enter_context(nc.Block())
        FIRST = 8
        NU = FC // 2

        def expert_steps(eng, stages, extra):
            def step(t, parity):
                for lag, body in stages:
                    if not isinstance(t, int) or 0 <= t - lag < NTILE:
                        body(t - lag, (parity - lag) % 2)
            def peeled(lo, hi):
                for t in range(lo, hi):
                    if t in extra:
                        extra[t]()
                    step(t, t % 2)
                if hi in extra:
                    extra[hi]()
            routed[0] = False
            peeled(0, FIRST)
            run_steps(eng, FIRST, SHARED, step)
            eng.wait_ge(table_ready, 1)
            routed[0] = True
            peeled(SHARED, SHARED + 2)
            run_steps(eng, SHARED + 2, NTILE, step)
            for t in range(NTILE, NTILE + max(lag for lag, _ in stages)):
                step(t, t % 2)
        routed = [False]

        def with_shared(i):
            return i < SHARED if isinstance(i, int) else not routed[0]

        def expert(eng, i):
            if not routed[0]:
                return 0
            return eng.value_load(table[0:1, bass.ds(i, 1)], min_val=0, max_val=EXPERTS)

        @block.sync
        def _(sp):
            def load(i, par):
                if past(i, 2):
                    sp.wait_ge(xT_ready, i - 1)
                sp.dma_start(x_in[:, par, :, :], d["xs"][bass.ds(i * SLOT, SLOT), :].rearrange("(k p) c -> p k c", p=P)
                             ).then_inc(ld_x[par], 16)

            def store(i, par):
                sp.wait_ge(y_done, i + 1)
                sp.dma_start(d["y"][bass.ds(i * SLOT, SLOT), :].rearrange("(k p) c -> p k c", p=P), y_out[:, par, :, :]
                             ).then_inc(st_y[par], 16)
            LAG = 4

            def both(t, par):
                if not isinstance(t, int) or t < NTILE:
                    load(t, par)
                if not isinstance(t, int) or t >= LAG:
                    store(t - LAG, (par - LAG) % 2)

            def load_pieces(t):
                for k in range(2):
                    if past(t, 1):
                        sp.wait_ge(w_lo[k], t)
                    sp.dma_start(stage[:, k, :], d["w"][bass.ds((REST[k] + t) * P, P), :]).then_inc(ld_w[k], 16)

            def with_pieces(t, par):
                both(t, par)
                if past(t, 1):
                    load_pieces(t - 1)
            for t in range(FIRST):
                with_pieces(t, t % 2)
            run_steps(sp, FIRST, SHARED, with_pieces)
            load_pieces(SHARED - 1)
            for k in range(2):
                sp.wait_ge(scattered[k], NT * 16)
            run_steps(sp, SHARED, NTILE, both)
            for t in range(NTILE, NTILE + LAG):
                both(t, t % 2)
            for k in range(2):
                sp.wait_ge(w_lo[k], SHARED)
            load_early(sp, 1, d, *early_inputs(stage), env["kv_loaded1"])
            for k in range(2):
                sp.wait_ge(st_y[k], ((NTILE + 1 - k) // 2) * 16)

        @block.gpsimd
        def _(pool):
            pool.dma_start(b1[:, :], d["b1"]).then_inc(ld_b, 16)
            pool.dma_start(b2[:, :], d["b2"]).then_inc(ld_b, 16)
            pool.wait_ge(table_ready, 1)
            flat = pos[:, :, :].rearrange("p t k -> p (t k)")

            def load_rows(g, par):
                if past(g, 2):
                    pool.wait_ge(scattered[par], 2 * SG * turns(g - 2, par))
                pool.dma_start(rows[:, SG * par:SG * (par + 1), :],
                               d["xs"][bass.ds(g * SG * P, SG * P), :].rearrange("(k p) c -> p k c", p=P)
                               ).then_inc(ld_row[par], 16)

            def scatter(g, par):
                nc.gpsimd.tensor_copy(idx[:, par, :], flat[:, bass.ds(g * 2 * SG, 2 * SG)]).then_inc(idx_done, 1)
                pool.wait_ge(idx_done, g + 1)
                wait_apart(pool, env["passed"], ld_row[par], turns(g, par))
                for k in range(2 * SG):
                    nc.gpsimd.indirect_dma_start(
                        out=d["xs"][:, :], out_offset=bass.IndirectOffsetOnAxis(ap=idx[:, par, k:k + 1], axis=0),
                        in_=rows[:, SG * par + k // 2, :], in_offset=None).then_inc(scattered[par], 16)
            skewed(pool, NT // SG, 4, [(0, load_rows), (1, scatter)])

        @block.tensor
        def _(pe):
            def count():
                pe.wait_ge(picked_ready, 1)
                nc.tensor.matmul(psR[:, 0:256], tri16[:, :], picked[:, :], start=True, stop=True)
                nc.tensor.matmul(psR[:, 256:512], one16[:, :], picked[:, :], start=True, stop=True).then_inc(counts_ready, 1)

            def transpose_x(i, par):
                pe.wait_ge(ld_x[par], turns(i, par))
                if past(i, 1):
                    pe.wait_ge(xT_done, i)
                for c in range(4):
                    for k in range(2):
                        last = nc.tensor.transpose(psX[:, (c * 2 + k) * P:(c * 2 + k + 1) * P],
                                                   x_in[:, par, k, c * P:(c + 1) * P], ident16[:, :])
                last.then_inc(xT_ready, 1)

            def up(i, par):
                e = expert(pe, i)
                pe.wait_ge(xT_done, i + 1)
                for u in range(NU):
                    if past(i, 1):
                        pe.wait_ge(relu_done, (i - 1) * FC + 2 * u + 2)
                    for k in range(2):
                        f = 2 * u + k
                        for m in range(DC):
                            for wh, xh in ((0, 0), (0, 1), (1, 0)):
                                last = nc.tensor.matmul(
                                    psH[u][:, k * SLOT:(k + 1) * SLOT],
                                    flatW[:, bass.ds(e * 4096 + ((m * 2 + wh) * 1024 + f * P), P)],
                                    xT[:, par, (xh * DC + m) * SLOT:(xh * DC + m + 1) * SLOT],
                                    start=m == 0 and wh == 0 and xh == 0, stop=m == DC - 1 and wh == 1)
                    last.then_inc(h_ready, 1)

            def down(i, par):
                e = expert(pe, i)
                pe.wait_ge(h_split, 2 * NU * (i + 1))
                if past(i, 2):
                    pe.wait_ge(y_done, i - 1)
                for r in range(2):
                    for f in range(FC):
                        for hh, wh in ((0, 0), (0, 1), (1, 0)):
                            piece = 2 * NE + f // 4
                            last = nc.tensor.matmul(
                                psY[par][:, r * D:(r + 1) * D],
                                h16[:, par, hh, f * SLOT + r * P:f * SLOT + (r + 1) * P],
                                flatW[:, bass.ds(e * 4096 + ((piece * 2 + wh) * 1024 + (f % 4) * D), D)],
                                start=f == 0 and hh == 0 and wh == 0, stop=f == FC - 1 and hh == 1)
                last.then_inc(y_ready, 1)

            def all_split():
                for k in range(2):
                    pe.wait_ge(w_lo[k], SHARED)
            expert_steps(pe, [(1, transpose_x), (2, up), (3, down)], {4: count, SHARED + 2: all_split})

        @block.scalar
        def _(act):
            def exp_difference():
                act.wait_ge(exp_ready, 1)
                nc.scalar.activation(V["e"][:, :], V["den"][:, :], ACT.Exp).then_inc(exp_ready, 1)

            def copy_x(i, par):
                act.wait_ge(xT_ready, i + 1)
                if past(i, 2):
                    act.wait_ge(h_ready, (i - 1) * NU)
                nc.scalar.activation(xT[:, par, :], psX[:, :], ACT.Copy).then_inc(xT_done, 1)

            def relu(i, par):
                e = expert(act, i)
                for u in range(NU):
                    act.wait_ge(h_ready, i * NU + u + 1)
                    if u >= 2:
                        act.wait_ge(h_split, (i * NU + u - 1) * 2)
                    elif past(i, 1):
                        act.wait_ge(h_split, (i * NU + u - 1) * 2)
                    for k in range(2):
                        nc.scalar.activation(h32[:, u % 2, k * SLOT:(k + 1) * SLOT], psH[u][:, k * SLOT:(k + 1) * SLOT],
                                             ACT.Relu, bias=b1[:, bass.ds(e * FC + 2 * u + k, 1)],
                                             scale=1.0 / XS).then_inc(relu_done, 1)

            def weights_high(t, par):
                if not with_shared(t):
                    return
                for k in range(2):
                    act.wait_ge(ld_w[k], (t + 1) * 16)
                    nc.scalar.activation(stage[:, k, :], stage[:, k, :], ACT.Copy, scale=XS).then_inc(w_hi[k], 1)
                for k in range(2):
                    act.wait_ge(w_hi[k], t * 2 + 1)
                    nc.scalar.activation(flatW[:, bass.ds((REST[k] + t) * 2048, 1024)], stage[:, k, :], ACT.Copy
                                         ).then_inc(w_hi[k], 1)
            expert_steps(act, [(1, copy_x), (2, weights_high), (2, relu)],
                         {2: lambda: act.wait_ge(b1_scaled, 1), 4: exp_difference,
                          FIRST: lambda: act.wait_ge(table_ready, 1)})

        @block.vector
        def _(dve):
            steps = [0]

            def then(ins):
                steps[0] += 1
                ins.then_inc(route, 1)
                dve.wait_ge(route, steps[0])
            per_e = [P, NT, EXPERTS]
            iota = consts[:, C_IOTA:C_IOTA + EXPERTS].unsqueeze(1).to_broadcast(per_e)
            a, b_ = R["a"], R["b"]
            nc.vector.tensor_copy(tri16[:, :], consts[:, C_TRI:C_TRI + P])
            nc.vector.memset(one16[:, :], 1.0)
            dve.wait_ge(ld_b, 32)
            nc.vector.tensor_scalar(b1[:, :], b1[:, :], XS, None, ALU.mult).then_inc(b1_scaled, 1)

            def choose():
                for n, (lg, oh, v) in enumerate(((logits, R["oh1"], V["v1"]), (b_, R["oh2"], V["v2"]))):
                    then(nc.vector.tensor_reduce(v[:, :], lg[:, :, :], AX_X, ALU.max))
                    then(nc.vector.tensor_tensor(a[:, :, :], lg[:, :, :], v[:, :].unsqueeze(2).to_broadcast(per_e), ALU.is_equal))
                    then(nc.vector.scalar_tensor_tensor(out=a[:, :, :], in0=a[:, :, :], scalar=-float(EXPERTS), in1=iota,
                                                        op0=ALU.mult, op1=ALU.add))
                    then(nc.vector.tensor_reduce(V["i"][:, :], a[:, :, :], AX_X, ALU.min))
                    then(nc.vector.tensor_tensor(oh[:, :, :], a[:, :, :], V["i"][:, :].unsqueeze(2).to_broadcast(per_e),
                                                 ALU.is_equal))
                    if n == 0:
                        then(nc.vector.scalar_tensor_tensor(out=b_[:, :, :], in0=oh[:, :, :], scalar=-1e30, in1=lg[:, :, :],
                                                            op0=ALU.mult, op1=ALU.add))
                nc.vector.tensor_tensor(picked[:, :].rearrange("p (t e) -> p t e", e=EXPERTS), R["oh1"][:, :, :],
                                        R["oh2"][:, :, :], ALU.add).then_inc(picked_ready, 1)
                nc.vector.tensor_tensor(V["den"][:, :], V["v2"][:, :], V["v1"][:, :], ALU.subtract).then_inc(exp_ready, 1)

            def place():
                dve.wait_ge(exp_ready, 2)
                then(nc.vector.tensor_scalar(V["den"][:, :], V["e"][:, :], 1.0, None, ALU.add))
                then(nc.vector.reciprocal(wts[:, :, 0], V["den"][:, :]))
                then(nc.vector.tensor_tensor(wts[:, :, 1], V["e"][:, :], wts[:, :, 0], ALU.mult))
                dve.wait_ge(counts_ready, 1)
                then(nc.vector.tensor_copy(TE["tot"][:, :, :], psR[:, 256:512].rearrange("p (t e) -> p e t", e=EXPERTS)))
                then(nc.vector.tensor_tensor_scan(TE["inc"][:, :, :].rearrange("p e t -> p (e t)"),
                                                  consts[:, C_RESET:C_RESET + EXPERTS * NT],
                                                  TE["tot"][:, :, :].rearrange("p e t -> p (e t)"), 0.0, ALU.mult, ALU.add))
                then(nc.vector.tensor_scalar(E8["n"][:, :], TE["inc"][:, :, NT - 1], 1.0 / SLOT, 0.5 - 0.5 / SLOT,
                                             ALU.mult, ALU.add))
                then(nc.vector.tensor_scalar(E8["n"][:, :], E8["n"][:, :], MAGIC, None, ALU.add))
                then(nc.vector.tensor_scalar(E8["pad"][:, :], E8["n"][:, :], MAGIC, float(SLOT), ALU.subtract, ALU.mult))
                then(nc.vector.tensor_tensor_scan(E8["end"][:, :], consts[:, C_ONE:C_ONE + EXPERTS], E8["pad"][:, :], 0.0,
                                                  ALU.mult, ALU.add))
                then(nc.vector.tensor_tensor(E8["base"][:, :], E8["end"][:, :], E8["pad"][:, :], ALU.subtract))
                then(nc.vector.tensor_tensor(TE["inc"][:, :, :], TE["inc"][:, :, :], TE["tot"][:, :, :], ALU.subtract))
                then(nc.vector.tensor_tensor(TE["inc"][:, :, :], TE["inc"][:, :, :],
                                             E8["base"][:, :].unsqueeze(2).to_broadcast([P, EXPERTS, NT]), ALU.add))
                then(nc.vector.tensor_tensor(a[:, :, :], psR[:, 0:256].rearrange("p (t e) -> p t e", e=EXPERTS),
                                             TE["inc"][:, :, :].rearrange("p e t -> p t e"), ALU.add))
                for k, oh in enumerate((R["oh1"], R["oh2"])):
                    then(nc.vector.tensor_tensor(b_[:, :, :], a[:, :, :], oh[:, :, :], ALU.mult))
                    then(nc.vector.tensor_reduce(posf[:, :, k], b_[:, :, :], AX_X, ALU.add))
                then(nc.vector.tensor_scalar(pos[:, :, :], posf[:, :, :], float(T), None, ALU.add))
                end = E8["end"][0:1, :].unsqueeze(1).to_broadcast([1, ROUTED, EXPERTS])
                thr = consts[0:1, C_THR:C_THR + ROUTED].unsqueeze(2).to_broadcast([1, ROUTED, EXPERTS])
                then(nc.vector.tensor_tensor(cmp_[:, :, :], end, thr, ALU.is_le))
                then(nc.vector.tensor_reduce(cnt[:, :], cmp_[:, :, :], AX_X, ALU.add))
                nc.vector.memset(table[:, 0:SHARED], 0)
                nc.vector.tensor_scalar(table[:, SHARED:NTILE], cnt[:, :], float(EXPERTS - 1), 1.0, ALU.min,
                                        ALU.add).then_inc(table_ready, 1)
            def split(i, par):
                if past(i, 2):
                    dve.wait_ge(y_ready, i - 1)
                for u in range(NU):
                    n = i * NU + u
                    sl = slice(2 * u * SLOT, (2 * u + 2) * SLOT)
                    dve.wait_ge(relu_done, (n + 1) * 2)
                    nc.vector.tensor_copy(h16[:, par, 0, sl], h32[:, u % 2, :]).then_inc(h_split, 1)
                    dve.wait_ge(h_split, n * 2 + 1)
                    nc.vector.tensor_tensor(h16[:, par, 1, sl], h32[:, u % 2, :], h16[:, par, 0, sl],
                                            ALU.subtract).then_inc(h_split, 1)

            def output(i, par):
                e = expert(dve, i)
                dve.wait_ge(y_ready, i + 1)
                if past(i, 2):
                    dve.wait_ge(st_y[par], turns(i - 2, par))
                for r in range(2):
                    last = nc.vector.scalar_tensor_tensor(out=y_out[:, par, r, :], in0=psY[par][:, r * D:(r + 1) * D],
                                                          scalar=UNSCALE, in1=b2[:, bass.ds(e * D, D)],
                                                          op0=ALU.mult, op1=ALU.add)
                last.then_inc(y_done, 1)
            def weights_low(t, par):
                if not with_shared(t):
                    return
                for k in range(2):
                    dve.wait_ge(w_hi[k], (t + 1) * 2)
                    nc.vector.tensor_tensor(flatW[:, bass.ds((REST[k] + t) * 2048 + 1024, 1024)], stage[:, k, :],
                                            flatW[:, bass.ds((REST[k] + t) * 2048, 1024)], ALU.subtract).then_inc(w_lo[k], 1)
            expert_steps(dve, [(2, weights_low), (2, split), (3, output)], {3: choose, 5: place})


def quantised_ffn(nc, d, consts, ident16, env):
    xall, xn4, mx = env["xall"], env["xn4"], env["mx"]
    GT = 4
    GW = GT * P
    NG = NT // GT
    with ExitStack() as ctx:
        def sb(name, shape, dt=F32):
            return ctx.enter_context(nc.sbuf_tensor(f"f_{name}", shape, dt))

        def pb(name, shape, dt=F32):
            return ctx.enter_context(nc.psum_tensor(f"f_{name}", shape, dt))

        def sem(name):
            return ctx.enter_context(nc.semaphore(f"f_{name}"))
        hT = sb("hT", [P, IC, T])
        wgu, wdT, srow, drow, cs = (env[n] for n in ("wgu", "wdT", "srow", "drow", "cs"))
        maxh = sb("maxh", [P, 3, NG])
        psX = pb("psX", [P, DC * GW], BF16)
        psB = [pb(f"psB{k}", [P, 512]) for k in range(6)]
        chain, max_ready, all_max = sem("chain"), sem("max_ready"), sem("all_max")

        with ExitStack() as c2:
            q16 = c2.enter_context(nc.sbuf_tensor("f_q16", [P, 2, GT * D], BF16))
            silu_t = c2.enter_context(nc.sbuf_tensor("f_silu_t", [P, 3, GW], F32))
            up_t = c2.enter_context(nc.sbuf_tensor("f_up_t", [P, 2, GW], F32))
            xqT = c2.enter_context(nc.sbuf_tensor("f_xqT", [P, 2, DC * GW], BF16))
            x_quant, x_sub, xq_ready, xq_done = (c2.enter_context(nc.semaphore("f_" + n)) for n in
                                                 ("x_quant", "x_sub", "xq_ready", "xq_done"))
            gu_ready, silu_done, up_done, h_direct, h_copied = (c2.enter_context(nc.semaphore("f_" + n)) for n in (
                "gu_ready", "silu_done", "up_done", "h_direct", "h_copied"))
            block = c2.enter_context(nc.Block())
            FIRST = 6

            assert IC % 3 == 0
            DIRECT, COPIED = IC // 3, IC - IC // 3

            def direct(g, c):
                return g * DIRECT + c // 3

            def copied(g, c):
                return g * COPIED + c - 1 - c // 3

            def h_of(g, c, hgt):
                return hT[:, :, :].rearrange("p c t -> p (c t)")[0:hgt, bass.ds(g * GW + c * T, GW)]

            def group(tensor, g):
                return tensor.rearrange("p t c -> p (t c)")[:, bass.ds(g * (GT * D), GT * D)]

            @block.vector
            def _(dve):
                nc.vector.tensor_reduce(cs[:, 0:1], mx[:, :], AX_X, ALU.max).then_inc(max_ready, 1)
                dve.wait_ge(all_max, 1)
                nc.vector.tensor_scalar(cs[:, 9:10], cs[:, 6:7], cs[:, 1:2], None, ALU.mult).then_inc(chain, 1)
                dve.wait_ge(chain, 1)
                nc.vector.tensor_scalar(cs[:, 8:9], cs[:, 9:10], 1.0 / 127.0, None, ALU.mult).then_inc(chain, 1)
                dve.wait_ge(chain, 2)
                nc.vector.reciprocal(cs[:, 5:6], cs[:, 8:9]).then_inc(chain, 1)
                for v, c in ((srow[:, :, 0:IC - 1], cs[:, 8:9]), (srow[0:TAIL, :, IC - 1], cs[0:TAIL, 8:9])):
                    nc.vector.tensor_scalar(v, v, c, None, ALU.mult).then_inc(chain, 1)
                dve.wait_ge(chain, 5)

                def quantise(g, par):
                    v = group(xn4[:, :, :], g)
                    nc.vector.tensor_scalar(v, v, cs[:, 5:6], 127.0, ALU.mult, ALU.min).then_inc(x_quant, 1)
                    dve.wait_ge(x_quant, g * 2 + 1)
                    nc.vector.tensor_scalar(v, v, -128.0, MAGIC, ALU.max, ALU.add).then_inc(x_quant, 1)

                def gated(g, chunks):
                    for c in chunks:
                        dve.wait_ge(silu_done, g * IC + c + 2)
                        nc.vector.scalar_tensor_tensor(out=h_of(g, c, P), in0=psB[(c % 3) * 2 + 1][:, :],
                                                       scalar=srow[:, 1, c:c + 1], in1=silu_t[:, c % 3, :],
                                                       op0=ALU.mult, op1=ALU.mult).then_inc(h_direct, 1)

                def largest(part, chunks, rows):
                    def body(g, par):
                        dve.wait_ge(h_direct, direct(g, chunks[-1] // 3 * 3) + 1)
                        dve.wait_ge(h_copied, copied(g, chunks[-1]) + 1)
                        nc.vector.tensor_reduce(maxh[0:rows, part, bass.ds(g, 1)],
                                                hT[0:rows, chunks[0]:chunks[-1] + 1, bass.ds(g * GW, GW)], AX_XY, ALU.max,
                                                apply_absolute_value=True)
                    return body
                nc.vector.memset(maxh[:, :, :], 0.0)
                skewed(dve, NG, FIRST, [(3, lambda g, par: gated(g, range(0, IC // 2, 3))), (0, quantise),
                                        (4, largest(1, range(3, IC - 1), P)), (4, largest(2, [IC - 1], TAIL)),
                                        (3, lambda g, par: gated(g, range(IC // 2, IC, 3))),
                                        (3, largest(0, range(3), P))])

            @block.gpsimd
            def _(pool):
                pool.wait_ge(max_ready, 1)
                nc.gpsimd.partition_all_reduce(cs[:, 1:2], cs[:, 0:1], P, RMAX).then_inc(all_max, 1)

                def subtract(g, par):
                    if past(g, 2):
                        pool.wait_ge(xq_ready, g - 1)
                    wait_apart(pool, env["passed"], x_quant, (g + 1) * 2)
                    nc.gpsimd.tensor_scalar(q16[:, par, :], group(xn4[:, :, :], g), -MAGIC, 1.0,
                                            ALU.add, ALU.mult).then_inc(x_sub, 1)

                def multiply(g, par):
                    for c in range(IC):
                        if c % 3:
                            hgt = TAIL if c == IC - 1 else P
                            n = copied(g, c)
                            pool.wait_ge(up_done, n + 1)
                            nc.gpsimd.tensor_tensor(h_of(g, c, hgt), silu_t[0:hgt, c % 3, :],
                                                    up_t[0:hgt, (c - 1 - c // 3) % 2, :], ALU.mult).then_inc(h_copied, 1)
                skewed(pool, NG, FIRST, [(1, subtract), (3, multiply)])

            @block.tensor
            def _(pe):
                def transpose_q(g, par):
                    pe.wait_ge(x_sub, g + 1)
                    if past(g, 1):
                        pe.wait_ge(xq_done, g)
                    for m in range(DC):
                        for t in range(GT):
                            last = nc.tensor.transpose(psX[:, m * GW + t * P:m * GW + (t + 1) * P],
                                                       q16[:, par, t * D + m * P:t * D + (m + 1) * P],
                                                       env["ident_bf"][:, :])
                    last.then_inc(xq_ready, 1)

                def gate_up(g, par):
                    pe.wait_ge(xq_done, g + 1)
                    for c in range(IC):
                        hgt = TAIL if c == IC - 1 else P
                        if c >= 3 or past(g, 1):
                            if c % 3:
                                pe.wait_ge(up_done, copied(g, c) - 1)
                            else:
                                pe.wait_ge(h_direct, direct(g, c))
                        for w in range(2):
                            for m in range(DC):
                                last = nc.tensor.matmul(psB[(c % 3) * 2 + w][0:hgt, :], wgu[:, w, m, c * P:c * P + hgt],
                                                        xqT[:, par, m * GW:(m + 1) * GW], start=m == 0, stop=m == DC - 1)
                        last.then_inc(gu_ready, 1)
                skewed(pe, NG, FIRST, [(2, transpose_q), (3, gate_up)])

            @block.scalar
            def _(act):
                nc.scalar.activation(silu_t[:, 0, 0:1], drow[:, 0:1], ACT.Silu).then_inc(silu_done, 1)

                def copy_q(g, par):
                    act.wait_ge(xq_ready, g + 1)
                    if past(g, 2):
                        act.wait_ge(gu_ready, (g - 1) * IC)
                    nc.scalar.activation(xqT[:, par, :], psX[:, :], ACT.Copy).then_inc(xq_done, 1)

                def silu(g, par):
                    for c in range(IC):
                        n = g * IC + c
                        hgt = TAIL if c == IC - 1 else P
                        act.wait_ge(gu_ready, n + 1)
                        if c >= 3 or past(g, 1):
                            if c % 3:
                                act.wait_ge(h_copied, copied(g, c) - 1)
                            else:
                                act.wait_ge(h_direct, direct(g, c))
                        nc.scalar.activation(silu_t[0:hgt, c % 3, :], psB[(c % 3) * 2][0:hgt, :], ACT.Silu,
                                             scale=srow[0:hgt, 0, c:c + 1]).then_inc(silu_done, 1)
                        if c % 3:
                            nc.scalar.activation(up_t[0:hgt, (c - 1 - c // 3) % 2, :], psB[(c % 3) * 2 + 1][0:hgt, :],
                                                 ACT.Copy, scale=srow[0:hgt, 1, c:c + 1]).then_inc(up_done, 1)
                skewed(act, NG, FIRST, [(2, copy_q), (3, silu)])

        with ExitStack() as c2:
            hq = c2.enter_context(nc.sbuf_tensor("f_hq", [P, 2, IC, GW], BF16))
            final = c2.enter_context(nc.sbuf_tensor("f_final", [P, 2, GT * D], F32))
            orow = c2.enter_context(nc.sbuf_tensor("f_orow", [P, D], F32))
            negmagic = c2.enter_context(nc.sbuf_tensor("f_negmagic", [P, 1], F32))
            sc, all_h, h_quant, hq_done, o_ready, o_scaled, o_added = (c2.enter_context(nc.semaphore("f_" + n)) for n in (
                "sc", "all_h", "h_quant", "hq_done", "o_ready", "o_scaled", "o_added"))
            st_o = [c2.enter_context(nc.semaphore(f"f_st_o{k}")) for k in range(2)]
            h_round = c2.enter_context(nc.semaphore("f_h_round"))
            block = c2.enter_context(nc.Block())
            FIRST = 6

            def halves(g):
                return hT[:, 0:IC - 1, bass.ds(g * GW, GW)], hT[0:TAIL, IC - 1, bass.ds(g * GW, GW)]

            @block.sync
            def _(sp):
                def store(g, par):
                    sp.wait_ge(o_added, g + 1)
                    sp.dma_start(d["out"][bass.ds(g * GW, GW), :].rearrange("(t p) c -> p t c", p=P),
                                 final[:, par, :].rearrange("p (t c) -> p t c", t=GT)).then_inc(st_o[par], 16)
                skewed(sp, NG, FIRST, [(0, store)])
                for k in range(2):
                    sp.wait_ge(st_o[k], NG * 8)

            @block.gpsimd
            def _(pool):
                pool.wait_ge(sc, 1)
                nc.gpsimd.partition_all_reduce(cs[:, 10:11], cs[:, 9:10], P, RMAX).then_inc(all_h, 1)

                def round_h(g, par):
                    for k, v in enumerate(halves(g)):
                        nc.gpsimd.tensor_scalar(v, v, cs[0:TAIL if k else P, 4:5], MAGIC, ALU.mult, ALU.add
                                                ).then_inc(h_round, 1)
                pool.wait_ge(sc, 4)
                skewed(pool, NG, FIRST, [(0, round_h)])

            @block.vector
            def _(dve):
                nc.vector.memset(negmagic[:, :], -MAGIC)
                nc.vector.tensor_reduce(cs[:, 9:10], maxh[:, :, :], AX_XY, ALU.max).then_inc(sc, 1)
                dve.wait_ge(all_h, 1)
                nc.vector.tensor_scalar(cs[:, 11:12], cs[:, 7:8], cs[:, 10:11], None, ALU.mult).then_inc(sc, 1)
                dve.wait_ge(sc, 2)
                nc.vector.tensor_scalar(cs[:, 9:10], cs[:, 11:12], 1.0 / 127.0, None, ALU.mult).then_inc(sc, 1)
                dve.wait_ge(sc, 3)
                nc.vector.reciprocal(cs[:, 4:5], cs[:, 9:10]).then_inc(sc, 1)
                nc.vector.tensor_scalar(orow[:, :], drow[:, :], cs[:, 9:10], None, ALU.mult).then_inc(sc, 1)

                def clip_h(g, par):
                    for k, v in enumerate(halves(g)):
                        dve.wait_ge(h_round, g * 2 + k + 1)
                        nc.vector.tensor_scalar(v, v, MAGIC - 128.0, MAGIC + 127.0, ALU.max, ALU.min).then_inc(h_quant, 1)

                def scale_out(g, par):
                    if past(g, 2):
                        dve.wait_ge(st_o[par], turns(g - 2, par))
                    for k in range(2):
                        dve.wait_ge(o_ready, g * 2 + k + 1)
                        nc.vector.tensor_tensor(final[:, par, k * 512:(k + 1) * 512].rearrange("p (t c) -> p t c", t=2),
                                                psB[par * 2 + k][:, :].rearrange("p (t c) -> p t c", t=2),
                                                orow[:, :].unsqueeze(1).to_broadcast([P, 2, D]),
                                                ALU.mult).then_inc(o_scaled, 1)

                def add(g, par):
                    dve.wait_ge(o_scaled, (g + 1) * 2)
                    nc.vector.tensor_tensor(final[:, par, :], final[:, par, :], group(xall[:, :, :], g),
                                            ALU.add).then_inc(o_added, 1)
                dve.wait_ge(sc, 5)
                skewed(dve, NG, FIRST, [(1, clip_h), (3, scale_out), (3, add)])

            @block.scalar
            def _(act):
                act.wait_ge(sc, 1)

                def subtract(g, par):
                    if past(g, 2):
                        act.wait_ge(o_ready, (g - 1) * 2)
                    act.wait_ge(h_quant, g * 2 + 1)
                    nc.scalar.activation(hq[:, par, 0:IC - 1, :], hT[:, 0:IC - 1, bass.ds(g * GW, GW)], ACT.Identity,
                                         bias=negmagic[:, :])
                    act.wait_ge(h_quant, g * 2 + 2)
                    nc.scalar.activation(hq[0:TAIL, par, IC - 1, :], hT[0:TAIL, IC - 1, bass.ds(g * GW, GW)], ACT.Identity,
                                         bias=negmagic[0:TAIL, :]).then_inc(hq_done, 1)
                skewed(act, NG, FIRST, [(1, subtract)])

            @block.tensor
            def _(pe):
                def down(g, par):
                    pe.wait_ge(hq_done, g + 1)
                    if past(g, 2):
                        pe.wait_ge(o_scaled, (g - 1) * 2)
                    for t in range(GT):
                        for c in range(IC):
                            hgt = TAIL if c == IC - 1 else P
                            last = nc.tensor.matmul(psB[par * 2 + t // 2][:, (t % 2) * D:(t % 2 + 1) * D],
                                                    hq[0:hgt, par, c, t * P:(t + 1) * P], wdT[0:hgt, c, :],
                                                    start=c == 0, stop=c == IC - 1)
                        if t % 2:
                            last.then_inc(o_ready, 1)
                skewed(pe, NG, FIRST, [(2, down)])


def build(nc, d):
    outer = ExitStack()
    with outer:
        def sb(stack, name, shape, dt=F32):
            return stack.enter_context(nc.sbuf_tensor(name, shape, dt))
        consts = sb(outer, "consts_sb", [P, C_END])
        ident16 = sb(outer, "ident16", [P, P], F16)
        ident_bf = sb(outer, "ident_bf", [P, P], BF16)
        ones16 = sb(outer, "ones16", [P, P], F16)
        env = {"ident_bf": ident_bf, "ident16": ident16, "ones16": ones16, "passed": outer.enter_context(nc.semaphore("passed"))}
        env["stage"] = sb(outer, "stage", [P, 2, 1024])
        env["kv_loaded1"] = outer.enter_context(nc.semaphore("kv_loaded1"))
        env["pos"] = sb(outer, "pos", [P, NT, 2], I32)
        env["wts"] = sb(outer, "wts", [P, NT, 2])
        with ExitStack() as moe:
            env["logits"] = sb(moe, "logits", [P, NT, EXPERTS])
            env["zero16"] = sb(moe, "zero16", [P, 2 * D], F16)
            env["wg16"] = sb(moe, "wg16", [P, DC, 2, EXPERTS], F16)
            W_all = env["W_all"] = sb(moe, "W_all", [P, PIECES, 2, 1024], F16)
            l = LAYERS[0]
            U = W_all[:, EARLY:PIECES, :, :].rearrange("p n h c -> p (n h c)")[:, 0:B * l.nu * 2 * D]
            lo, hi = REST[0], FIRST_PIECES[2]
            room = Room(W_all[:, lo:hi, :, :].rearrange("p n h c -> p (n h c)").bitcast(F32))
            with ExitStack() as a0:
                G = sb(a0, "G0", [P, B * DC * 2 * l.cols], F16)
                Brow = sb(a0, "Brow0", [P, B * l.cols], F16)
                prepare = prepare_attention(nc, a0, 0, d, consts, G[:, :], U, Brow[:, :], env, room, room)
                attention(nc, 0, d, consts, ones16, ident16, G[:, :], U, Brow[:, :], env, prepare)
            experts(nc, d, consts, ident16, env)
        env["xall"] = sb(outer, "xall", [P, NT, D])
        env["xn4"] = sb(outer, "xn4", [P, NT, D])
        env["mx"] = sb(outer, "mx", [P, NT])
        env["wgu"] = sb(outer, "wgu", [P, 2, DC, INTER], BF16)
        env["wdT"] = sb(outer, "wdT", [P, IC, D], BF16)
        env["srow"] = sb(outer, "srow", [P, 2, IC])
        env["drow"] = sb(outer, "drow", [P, D])
        env["cs"] = sb(outer, "cs", [P, 12])
        l = LAYERS[1]
        with ExitStack() as a1:
            env["bo_row"] = sb(a1, "bo_row", [P, D])
            G = sb(a1, "G1", [P, B * DC * 2 * l.cols], F16)
            U = sb(a1, "U1", [P, B * l.nu * 2 * D], F16)
            Brow = sb(a1, "Brow1", [P, B * l.cols], F16)
            wide = Room(env["xall"][:, 2:NT, :].rearrange("p t c -> p (t c)"))
            more = Room(env["xn4"][:, :, :].rearrange("p t c -> p (t c)"))
            prepare = prepare_attention(nc, a1, 1, d, consts, G[:, :], U[:, :], Brow[:, :], env, wide, more)
            attention(nc, 1, d, consts, ones16, ident16, G[:, :], U[:, :], Brow[:, :], env, prepare)
        quantised_ffn(nc, d, consts, ident16, env)


def constants(np):
    c = np.zeros((P, C_END), np.float32)
    p = np.arange(P)
    c[:, C_ID:C_ID + P] = np.eye(P)
    c[:, C_TRI:C_TRI + P] = p[:, None] < p[None, :]
    c[:, C_IOTA:C_IOTA + EXPERTS] = np.arange(EXPERTS)
    c[:, C_RESET:C_RESET + EXPERTS * NT] = np.tile(np.arange(NT) > 0, EXPERTS)
    c[:, C_THR:C_THR + ROUTED] = np.arange(ROUTED) * SLOT
    c[:, C_ONE:C_ONE + P] = 1
    c[:, C_POW] = -0.5
    return c


def head_mask(np, l):
    return ((np.arange(P) // l.dim)[:, None] == (np.arange(l.width) // KEYS)[None, :]).astype(np.float32)


def kernel(**inputs):
    import numpy as np
    import concourse.bacc as bacc
    from concourse.bass_utils import run_bass_kernel_spmd

    a = {k: np.asarray(v) for k, v in inputs.items()}

    def chunks(m):
        return np.ascontiguousarray(m.reshape(-1, P, m.shape[-1]).transpose(1, 0, 2))

    def column(v):
        return v.reshape(-1, P).T
    h0 = LAYERS[0].feat
    arrays = {
        "consts": constants(np),
        "x0": a["x"].reshape(T, D),
        "ctxT": chunks(a["ctx_1024"].reshape(B * KEYS, D).T),
        "wg": chunks(a["L0_ffn_Wg"]),
        "wk0": chunks(a["L0_xattn_key_down"].transpose(1, 0, 2).reshape(D, h0)),
        "wv0": chunks(a["L0_xattn_value_down"].transpose(1, 0, 2).reshape(D, h0)),
        "wq0": chunks(a["L0_xattn_query_down"].transpose(0, 2, 1).reshape(h0, D)),
        "wo0": chunks(a["L0_xattn_value_up"].reshape(h0, D)),
        "bias0": np.stack([column(a["L0_xattn_query_down_bias"].reshape(-1)), np.zeros((P, 4), np.float32),
                           np.zeros((P, 4), np.float32)], 1),
        "wk1": chunks(a["L1_xattn_Wk"].T),
        "wv1": chunks(a["L1_xattn_Wv"].T),
        "wq1": chunks(a["L1_xattn_Wq"]),
        "wo1": chunks(a["L1_xattn_Wo"].T),
        "bias1": np.stack([column(a["L1_xattn_b" + n]) for n in "qkv"], 1),
        "bo": np.broadcast_to(a["L1_xattn_bo"][None], (P, D)),
        "wgate": a["L1_ffn_w_gate"], "wup": a["L1_ffn_w_up"], "wd": a["L1_ffn_w_down"],
        "clip": np.broadcast_to(np.concatenate([a["L1_ffn_clip_x"], a["L1_ffn_clip_down"]])[None], (P, 2)),
    }
    w1 = np.concatenate([a["L0_ffn_Ws1"][None], a["L0_ffn_W1"]])
    w2 = np.concatenate([a["L0_ffn_Ws2"][None], a["L0_ffn_W2"]])
    w2 = w2.reshape(NE, 2, 4, P, D).transpose(0, 1, 3, 2, 4)
    arrays["w"] = np.concatenate([w1.reshape(2 * NE * P, FF), w2.reshape(2 * NE * P, FF)])
    b1 = np.concatenate([a["L0_ffn_bs1"][None], a["L0_ffn_b1"]])
    arrays["b1"] = b1.reshape(NE * FC, P).T
    b2 = np.concatenate([a["L0_ffn_bs2"][None], a["L0_ffn_b2"]])
    arrays["b2"] = np.broadcast_to(b2.reshape(1, NE * D), (P, NE * D))

    for n, l in enumerate(LAYERS):
        arrays[f"mask{n}"] = head_mask(np, l)

    nc = bacc.Bacc("TRN2", target_bir_lowering=False, num_devices=1)
    arrays = {k: np.ascontiguousarray(v) for k, v in arrays.items()}
    d = {k: nc.dram_tensor(f"in_{k}", v.shape, mybir.dt.from_np(v.dtype), kind="ExternalInput").ap()
         for k, v in arrays.items()}
    for n in ("wk", "wv", "wq", "wo", "bias", "mask"):
        d[n] = [d[n + "0"], d[n + "1"]]
    d["wgu"] = [d["wgate"], d["wup"]]
    d["x1"] = nc.dram_tensor("x1_dram", (T, D), F32, kind="Internal").ap()
    d["xs"] = nc.dram_tensor("xs_dram", (ROWS, 2 * D), F16, kind="Internal").ap()
    d["y"] = nc.dram_tensor("y_dram", (ROWS, D), F32, kind="Internal").ap()
    d["out"] = nc.dram_tensor("out_dram", (T, D), F32, kind="ExternalOutput").ap()
    build(nc, d)
    r = run_bass_kernel_spmd(nc, [{f"in_{k}": v for k, v in arrays.items()}], core_ids=[0])
    return r.results[0]["out_dram"].reshape(B, S, D)
```
